# Optimizing a Trainium2 kernel written in Bass

```python
import numpy as np
import jax
import jax.numpy as jnp

def _softmax(x, axis=-1):
    return jax.nn.softmax(x, axis=axis)

def _gelu(x):
    return jax.nn.gelu(x, approximate=True)

def _silu(x):
    return jax.nn.silu(x)

def _sigmoid(x):
    return jax.nn.sigmoid(x)

def _layernorm(x, axis=-1, eps=1e-05):
    m = jnp.mean(x, axis=axis, keepdims=True)
    v = jnp.var(x, axis=axis, keepdims=True)
    return (x - m) / jnp.sqrt(v + eps)

def _scatter_add(tgt, idx, src, axis=0):
    return tgt.at[idx].add(src)

def _segment_sum(src, seg, n):
    return jax.ops.segment_sum(src, seg, n)
kernel_name = 'mk_recurrent_d2_jaxref_r8_31b8af'

def setup_inputs(seed: int=0):
    np.random.seed(seed)
    _w = jnp.asarray

    def _L0_attn_setup():
        import jax, jax.numpy as jnp
        import numpy as np
        D_MODEL, EXPAND, D_STATE, D_CONV, HEADDIM = (128, 2, 64, 4, 64)
        D_INNER = EXPAND * D_MODEL
        NHEADS = D_INNER // HEADDIM
        CONV_DIM = D_INNER + 2 * D_STATE
        D_IN_PROJ = 2 * D_INNER + 2 * D_STATE + NHEADS
        EPS = 1e-05

        def _layernorm(x, w, b):
            mu = jnp.mean(x, axis=-1, keepdims=True)
            var = jnp.mean(jnp.square(x - mu), axis=-1, keepdims=True)
            return (x - mu) * jax.lax.rsqrt(var + EPS) * w + b

        def _mamba2(x, in_proj_w, conv_w, conv_b, dt_bias, A_log, D, norm_w, out_proj_w):
            Bt, L, _ = x.shape
            zxbcdt = x @ in_proj_w.T
            z = zxbcdt[..., :D_INNER]
            xBC = zxbcdt[..., D_INNER:D_INNER + CONV_DIM]
            dt = jax.nn.softplus(zxbcdt[..., D_INNER + CONV_DIM:] + dt_bias)
            xp = jnp.pad(xBC, ((0, 0), (D_CONV - 1, 0), (0, 0)))
            conv = conv_b
            for k in range(D_CONV):
                conv = conv + xp[:, k:k + L, :] * conv_w[:, k]
            xBC = jax.nn.silu(conv)
            xs = xBC[..., :D_INNER].reshape(Bt, L, NHEADS, HEADDIM)
            Bm = xBC[..., D_INNER:D_INNER + D_STATE]
            Cm = xBC[..., D_INNER + D_STATE:]
            A = -jnp.exp(A_log)

            def step(h, inp):
                x_t, dt_t, B_t, C_t = inp
                dA = jnp.exp(dt_t * A)
                h = h * dA[:, :, None, None] + (dt_t[:, :, None] * x_t)[..., None] * B_t[:, None, None, :]
                y = jnp.einsum('bhpn,bn->bhp', h, C_t)
                return (h, y)
            h0 = jnp.zeros((Bt, NHEADS, HEADDIM, D_STATE), x.dtype)
            xsT = jnp.moveaxis(xs, 1, 0)
            dtT = jnp.moveaxis(dt, 1, 0)
            BT = jnp.moveaxis(Bm, 1, 0)
            CT = jnp.moveaxis(Cm, 1, 0)
            _, ys = jax.lax.scan(step, h0, (xsT, dtT, BT, CT))
            y = jnp.moveaxis(ys, 0, 1) + xs * D[None, None, :, None]
            y = y.reshape(Bt, L, D_INNER)
            y = y * jax.nn.silu(z)
            y = y * jax.lax.rsqrt(jnp.mean(jnp.square(y), axis=-1, keepdims=True) + EPS) * norm_w
            return y @ out_proj_w.T
        key = jax.random.key(seed)
        ks = jax.random.split(key, 16)
        s = 0.02
        inp = {'x': jax.random.normal(ks[0], (2, 256, D_MODEL), jnp.float32), 'ln1_w': jnp.ones((D_MODEL,), jnp.float32), 'ln1_b': jnp.zeros((D_MODEL,), jnp.float32), 'in_proj_w': jax.random.normal(ks[1], (D_IN_PROJ, D_MODEL), jnp.float32) * s, 'conv_w': jax.random.normal(ks[2], (CONV_DIM, D_CONV), jnp.float32) * 0.3, 'conv_b': jnp.zeros((CONV_DIM,), jnp.float32), 'dt_bias': jnp.log(jnp.expm1(jnp.exp(jax.random.uniform(ks[3], (NHEADS,), jnp.float32, jnp.log(0.001), jnp.log(0.1))))), 'A_log': jnp.log(jax.random.uniform(ks[4], (NHEADS,), jnp.float32, 1.0, 16.0)), 'D': jnp.ones((NHEADS,), jnp.float32), 'norm_w': jnp.ones((D_INNER,), jnp.float32), 'out_proj_w': jax.random.normal(ks[5], (D_MODEL, D_INNER), jnp.float32) * s, 'ln2_w': jnp.ones((D_MODEL,), jnp.float32), 'ln2_b': jnp.zeros((D_MODEL,), jnp.float32), 'mlp_w1': jax.random.normal(ks[6], (4 * D_MODEL, D_MODEL), jnp.float32) * s, 'mlp_b1': jnp.zeros((4 * D_MODEL,), jnp.float32), 'mlp_w2': jax.random.normal(ks[7], (D_MODEL, 4 * D_MODEL), jnp.float32) * s, 'mlp_b2': jnp.zeros((D_MODEL,), jnp.float32)}
        return inp
    _L0_attn_in = _L0_attn_setup()

    def _L0_ffn_setup():
        import jax, jax.numpy as jnp
        import numpy as np
        EPS = 1e-05
        TOP_K = 2

        def _rmsnorm(x, w):
            xf = x.astype(jnp.float32)
            rms = jax.lax.rsqrt(jnp.mean(xf * xf, axis=-1, keepdims=True) + EPS)
            return (xf * rms).astype(x.dtype) * w

        def _attention(x, wq, wk, wv, wo, num_heads=16):
            B, S, H = x.shape
            D = H // num_heads
            q = (x @ wq.T).reshape(B, S, num_heads, D)
            k = (x @ wk.T).reshape(B, S, num_heads, D)
            v = (x @ wv.T).reshape(B, S, num_heads, D)
            scale = 1.0 / jnp.sqrt(jnp.float32(D)).astype(x.dtype)
            scores = jnp.einsum('bqhd,bkhd->bhqk', q, k) * scale
            probs = jax.nn.softmax(scores, axis=-1)
            out = jnp.einsum('bhqk,bkhd->bqhd', probs, v).reshape(B, S, H)
            return out @ wo.T

        def _moe(x, gate_w, w1, w2, w3):
            B, S, H = x.shape
            xf = x.reshape(-1, H)
            logits = xf @ gate_w.T
            rw, sel = jax.lax.top_k(logits, TOP_K)
            rw = jax.nn.softmax(rw.astype(jnp.float32), axis=-1).astype(x.dtype)
            E = gate_w.shape[0]
            out = jnp.zeros_like(xf)
            for e in range(E):
                we = jnp.sum(jnp.where(sel == e, rw, 0.0), axis=-1)
                h = jax.nn.silu(xf @ w1[e].T) * (xf @ w3[e].T)
                out = out + h @ w2[e].T * we[:, None]
            return out.reshape(B, S, H)
        key = jax.random.key(seed)
        ks = jax.random.split(key, 10)
        H, I, E, NH = (128, 256, 8, 16)
        B, S = (2, 256)
        s = 0.02
        return {'x': jax.random.normal(ks[0], (B, S, H), jnp.float32), 'ln1_w': jnp.ones((H,), jnp.float32), 'ln2_w': jnp.ones((H,), jnp.float32), 'wq': jax.random.normal(ks[1], (H, H), jnp.float32) * s, 'wk': jax.random.normal(ks[2], (H, H), jnp.float32) * s, 'wv': jax.random.normal(ks[3], (H, H), jnp.float32) * s, 'wo': jax.random.normal(ks[4], (H, H), jnp.float32) * s, 'gate_w': jax.random.normal(ks[5], (E, H), jnp.float32) * s, 'w1': jax.random.normal(ks[6], (E, I, H), jnp.float32) * s, 'w2': jax.random.normal(ks[7], (E, H, I), jnp.float32) * s, 'w3': jax.random.normal(ks[8], (E, I, H), jnp.float32) * s}
    _L0_ffn_in = _L0_ffn_setup()

    def _L1_attn_setup():
        import jax, jax.numpy as jnp
        import numpy as np
        FEATS = 128
        HEAD = 16
        HEAD_DIM = FEATS // HEAD
        EPS = 1e-12

        def _l2norm(t):
            n = jnp.sqrt(jnp.sum(t * t, axis=-1, keepdims=True))
            return t / jnp.maximum(n, EPS)
        key = jax.random.key(seed)
        ks = jax.random.split(key, 10)
        s = 0.02
        inp = {'x': jax.random.normal(ks[0], (4, 256, FEATS), dtype=jnp.float32), 'Wq': jax.random.normal(ks[1], (FEATS, FEATS), dtype=jnp.float32) * s, 'bq': jnp.zeros((FEATS,), dtype=jnp.float32), 'Wk': jax.random.normal(ks[2], (FEATS, FEATS), dtype=jnp.float32) * s, 'bk': jnp.zeros((FEATS,), dtype=jnp.float32), 'Wv': jax.random.normal(ks[3], (FEATS, FEATS), dtype=jnp.float32) * s, 'bv': jnp.zeros((FEATS,), dtype=jnp.float32), 'Wo': jax.random.normal(ks[4], (FEATS, FEATS), dtype=jnp.float32) * s, 'bo': jnp.zeros((FEATS,), dtype=jnp.float32), 'm': jnp.full((HEAD,), 0.5, dtype=jnp.float32)}
        return inp
    _L1_attn_in = _L1_attn_setup()

    def _L1_ffn_setup():
        import jax, jax.numpy as jnp
        import numpy as np
        E, D, F = (8, 128, 512)
        B, S = (4, 256)

        def _layernorm(x, g, b, eps=1e-05):
            mu = jnp.mean(x, axis=-1, keepdims=True)
            var = jnp.var(x, axis=-1, keepdims=True)
            return (x - mu) * jax.lax.rsqrt(var + eps) * g + b
        key = jax.random.key(seed)
        ks = jax.random.split(key, 5)
        return {'input_features': jax.random.normal(ks[0], (B, S, D), jnp.float32), 'centroids': jax.random.normal(ks[1], (E, D), jnp.float32) * 0.1, 'ln_g': jnp.ones((E, D), jnp.float32), 'ln_b': jnp.zeros((E, D), jnp.float32), 'w1': jax.random.normal(ks[2], (E, F, D), jnp.float32) * (1.0 / np.sqrt(D).astype(np.float32)), 'b1': jnp.zeros((E, F), jnp.float32), 'w2': jax.random.normal(ks[3], (E, D, F), jnp.float32) * (1.0 / np.sqrt(F).astype(np.float32)), 'b2': jnp.zeros((E, D), jnp.float32)}
    _L1_ffn_in = _L1_ffn_setup()
    _d = {'L0_attn_x': _L0_attn_in['x'], 'L0_attn_ln1_w': _L0_attn_in['ln1_w'], 'L0_attn_ln1_b': _L0_attn_in['ln1_b'], 'L0_attn_in_proj_w': _L0_attn_in['in_proj_w'], 'L0_attn_conv_w': _L0_attn_in['conv_w'], 'L0_attn_conv_b': _L0_attn_in['conv_b'], 'L0_attn_dt_bias': _L0_attn_in['dt_bias'], 'L0_attn_A_log': _L0_attn_in['A_log'], 'L0_attn_D': _L0_attn_in['D'], 'L0_attn_norm_w': _L0_attn_in['norm_w'], 'L0_attn_out_proj_w': _L0_attn_in['out_proj_w'], 'L0_attn_ln2_w': _L0_attn_in['ln2_w'], 'L0_attn_ln2_b': _L0_attn_in['ln2_b'], 'L0_attn_mlp_w1': _L0_attn_in['mlp_w1'], 'L0_attn_mlp_b1': _L0_attn_in['mlp_b1'], 'L0_attn_mlp_w2': _L0_attn_in['mlp_w2'], 'L0_attn_mlp_b2': _L0_attn_in['mlp_b2'], 'L0_ffn_ln1_w': _L0_ffn_in['ln1_w'], 'L0_ffn_ln2_w': _L0_ffn_in['ln2_w'], 'L0_ffn_wq': _L0_ffn_in['wq'], 'L0_ffn_wk': _L0_ffn_in['wk'], 'L0_ffn_wv': _L0_ffn_in['wv'], 'L0_ffn_wo': _L0_ffn_in['wo'], 'L0_ffn_gate_w': _L0_ffn_in['gate_w'], 'L0_ffn_w1': _L0_ffn_in['w1'], 'L0_ffn_w2': _L0_ffn_in['w2'], 'L0_ffn_w3': _L0_ffn_in['w3'], 'L1_attn_Wq': _L1_attn_in['Wq'], 'L1_attn_bq': _L1_attn_in['bq'], 'L1_attn_Wk': _L1_attn_in['Wk'], 'L1_attn_bk': _L1_attn_in['bk'], 'L1_attn_Wv': _L1_attn_in['Wv'], 'L1_attn_bv': _L1_attn_in['bv'], 'L1_attn_Wo': _L1_attn_in['Wo'], 'L1_attn_bo': _L1_attn_in['bo'], 'L1_attn_m': _L1_attn_in['m'], 'L1_ffn_centroids': _L1_ffn_in['centroids'], 'L1_ffn_ln_g': _L1_ffn_in['ln_g'], 'L1_ffn_ln_b': _L1_ffn_in['ln_b'], 'L1_ffn_w1': _L1_ffn_in['w1'], 'L1_ffn_b1': _L1_ffn_in['b1'], 'L1_ffn_w2': _L1_ffn_in['w2'], 'L1_ffn_b2': _L1_ffn_in['b2']}
    _x0 = _d['L0_attn_x']
    _d['L0_attn_x'] = jax.random.normal(jax.random.fold_in(jax.random.key(seed), 1), (8, 512, 128), dtype=_x0.dtype)
    del _x0
    return _d

def reference(L0_attn_x, L0_attn_ln1_w, L0_attn_ln1_b, L0_attn_in_proj_w, L0_attn_conv_w, L0_attn_conv_b, L0_attn_dt_bias, L0_attn_A_log, L0_attn_D, L0_attn_norm_w, L0_attn_out_proj_w, L0_attn_ln2_w, L0_attn_ln2_b, L0_attn_mlp_w1, L0_attn_mlp_b1, L0_attn_mlp_w2, L0_attn_mlp_b2, L0_ffn_ln1_w, L0_ffn_ln2_w, L0_ffn_wq, L0_ffn_wk, L0_ffn_wv, L0_ffn_wo, L0_ffn_gate_w, L0_ffn_w1, L0_ffn_w2, L0_ffn_w3, L1_attn_Wq, L1_attn_bq, L1_attn_Wk, L1_attn_bk, L1_attn_Wv, L1_attn_bv, L1_attn_Wo, L1_attn_bo, L1_attn_m, L1_ffn_centroids, L1_ffn_ln_g, L1_ffn_ln_b, L1_ffn_w1, L1_ffn_b1, L1_ffn_w2, L1_ffn_b2):

    def _L0_attn_ref(x, ln1_w, ln1_b, in_proj_w, conv_w, conv_b, dt_bias, A_log, D, norm_w, out_proj_w, ln2_w, ln2_b, mlp_w1, mlp_b1, mlp_w2, mlp_b2):
        import jax, jax.numpy as jnp
        import numpy as np
        D_MODEL, EXPAND, D_STATE, D_CONV, HEADDIM = (128, 2, 64, 4, 64)
        D_INNER = EXPAND * D_MODEL
        NHEADS = D_INNER // HEADDIM
        CONV_DIM = D_INNER + 2 * D_STATE
        D_IN_PROJ = 2 * D_INNER + 2 * D_STATE + NHEADS
        EPS = 1e-05

        def _layernorm(x, w, b):
            mu = jnp.mean(x, axis=-1, keepdims=True)
            var = jnp.mean(jnp.square(x - mu), axis=-1, keepdims=True)
            return (x - mu) * jax.lax.rsqrt(var + EPS) * w + b

        def _mamba2(x, in_proj_w, conv_w, conv_b, dt_bias, A_log, D, norm_w, out_proj_w):
            Bt, L, _ = x.shape
            zxbcdt = x @ in_proj_w.T
            z = zxbcdt[..., :D_INNER]
            xBC = zxbcdt[..., D_INNER:D_INNER + CONV_DIM]
            dt = jax.nn.softplus(zxbcdt[..., D_INNER + CONV_DIM:] + dt_bias)
            xp = jnp.pad(xBC, ((0, 0), (D_CONV - 1, 0), (0, 0)))
            conv = conv_b
            for k in range(D_CONV):
                conv = conv + xp[:, k:k + L, :] * conv_w[:, k]
            xBC = jax.nn.silu(conv)
            xs = xBC[..., :D_INNER].reshape(Bt, L, NHEADS, HEADDIM)
            Bm = xBC[..., D_INNER:D_INNER + D_STATE]
            Cm = xBC[..., D_INNER + D_STATE:]
            A = -jnp.exp(A_log)

            def step(h, inp):
                x_t, dt_t, B_t, C_t = inp
                dA = jnp.exp(dt_t * A)
                h = h * dA[:, :, None, None] + (dt_t[:, :, None] * x_t)[..., None] * B_t[:, None, None, :]
                y = jnp.einsum('bhpn,bn->bhp', h, C_t)
                return (h, y)
            h0 = jnp.zeros((Bt, NHEADS, HEADDIM, D_STATE), x.dtype)
            xsT = jnp.moveaxis(xs, 1, 0)
            dtT = jnp.moveaxis(dt, 1, 0)
            BT = jnp.moveaxis(Bm, 1, 0)
            CT = jnp.moveaxis(Cm, 1, 0)
            _, ys = jax.lax.scan(step, h0, (xsT, dtT, BT, CT))
            y = jnp.moveaxis(ys, 0, 1) + xs * D[None, None, :, None]
            y = y.reshape(Bt, L, D_INNER)
            y = y * jax.nn.silu(z)
            y = y * jax.lax.rsqrt(jnp.mean(jnp.square(y), axis=-1, keepdims=True) + EPS) * norm_w
            return y @ out_proj_w.T
        res = x
        h = _layernorm(x, ln1_w, ln1_b)
        h = _mamba2(h, in_proj_w, conv_w, conv_b, dt_bias, A_log, D, norm_w, out_proj_w)
        x = res + h
        res = x
        h = _layernorm(x, ln2_w, ln2_b)
        h = jax.nn.gelu(h @ mlp_w1.T + mlp_b1, approximate=False) @ mlp_w2.T + mlp_b2
        return res + h

    def _L0_ffn_ref(x, ln1_w, ln2_w, wq, wk, wv, wo, gate_w, w1, w2, w3):
        import jax, jax.numpy as jnp
        import numpy as np
        EPS = 1e-05
        TOP_K = 2

        def _rmsnorm(x, w):
            xf = x.astype(jnp.float32)
            rms = jax.lax.rsqrt(jnp.mean(xf * xf, axis=-1, keepdims=True) + EPS)
            return (xf * rms).astype(x.dtype) * w

        def _attention(x, wq, wk, wv, wo, num_heads=16):
            B, S, H = x.shape
            D = H // num_heads
            q = (x @ wq.T).reshape(B, S, num_heads, D)
            k = (x @ wk.T).reshape(B, S, num_heads, D)
            v = (x @ wv.T).reshape(B, S, num_heads, D)
            scale = 1.0 / jnp.sqrt(jnp.float32(D)).astype(x.dtype)
            scores = jnp.einsum('bqhd,bkhd->bhqk', q, k) * scale
            probs = jax.nn.softmax(scores, axis=-1)
            out = jnp.einsum('bhqk,bkhd->bqhd', probs, v).reshape(B, S, H)
            return out @ wo.T

        def _moe(x, gate_w, w1, w2, w3):
            B, S, H = x.shape
            xf = x.reshape(-1, H)
            logits = xf @ gate_w.T
            rw, sel = jax.lax.top_k(logits, TOP_K)
            rw = jax.nn.softmax(rw.astype(jnp.float32), axis=-1).astype(x.dtype)
            E = gate_w.shape[0]
            out = jnp.zeros_like(xf)
            for e in range(E):
                we = jnp.sum(jnp.where(sel == e, rw, 0.0), axis=-1)
                h = jax.nn.silu(xf @ w1[e].T) * (xf @ w3[e].T)
                out = out + h @ w2[e].T * we[:, None]
            return out.reshape(B, S, H)
        h = x + _attention(_rmsnorm(x, ln1_w), wq, wk, wv, wo)
        h = h + _moe(_rmsnorm(h, ln2_w), gate_w, w1, w2, w3)
        return h

    def _L1_attn_ref(x, Wq, bq, Wk, bk, Wv, bv, Wo, bo, m):
        import jax, jax.numpy as jnp
        import numpy as np
        FEATS = 128
        HEAD = 16
        HEAD_DIM = FEATS // HEAD
        EPS = 1e-12

        def _l2norm(t):
            n = jnp.sqrt(jnp.sum(t * t, axis=-1, keepdims=True))
            return t / jnp.maximum(n, EPS)
        b, n, f = x.shape

        def proj(W, bias):
            y = x @ W + bias
            return y.reshape(b, n, HEAD, HEAD_DIM).transpose(0, 2, 1, 3)
        q = _l2norm(proj(Wq, bq))
        k = _l2norm(proj(Wk, bk))
        v = proj(Wv, bv)
        sim = jnp.einsum('bhid,bhjd->bhij', q, k)
        sigma_m = jax.nn.sigmoid(m).reshape(1, HEAD, 1, 1)
        scaling = jnp.asarray(n, dtype=x.dtype) ** sigma_m
        attn = sim / scaling
        out = jnp.einsum('bhij,bhjd->bhid', attn, v)
        out = out.transpose(0, 2, 1, 3).reshape(b, n, f)
        return out @ Wo + bo

    def _L1_ffn_ref(input_features, centroids, ln_g, ln_b, w1, b1, w2, b2):
        import jax, jax.numpy as jnp
        import numpy as np
        E, D, F = (8, 128, 512)
        B, S = (4, 256)

        def _layernorm(x, g, b, eps=1e-05):
            mu = jnp.mean(x, axis=-1, keepdims=True)
            var = jnp.var(x, axis=-1, keepdims=True)
            return (x - mu) * jax.lax.rsqrt(var + eps) * g + b
        Bf, Sf, Df = input_features.shape
        x = input_features.reshape(-1, Df)
        aff = x @ centroids.T
        assign = jnp.argmax(aff, axis=1)
        order = jnp.argsort(assign)
        xs = x[order]
        es = assign[order]
        alpha = jax.nn.sigmoid(jnp.take_along_axis(aff[order], es[:, None], axis=1))
        nE = centroids.shape[0]
        y = jnp.zeros_like(xs)
        for e in range(nE):
            h = _layernorm(xs, ln_g[e], ln_b[e])
            h = jax.nn.relu(h @ w1[e].T + b1[e])
            ye = xs + h @ w2[e].T + b2[e]
            y = y + jnp.where((es == e)[:, None], ye, 0.0)
        out_sorted = alpha * y + (1.0 - alpha) * xs
        inv = jnp.argsort(order)
        return out_sorted[inv].reshape(Bf, Sf, Df)
    x = L0_attn_x
    xn = _layernorm(x, axis=-1)
    s = _L0_attn_ref(xn, L0_attn_ln1_w, L0_attn_ln1_b, L0_attn_in_proj_w, L0_attn_conv_w, L0_attn_conv_b, L0_attn_dt_bias, L0_attn_A_log, L0_attn_D, L0_attn_norm_w, L0_attn_out_proj_w, L0_attn_ln2_w, L0_attn_ln2_b, L0_attn_mlp_w1, L0_attn_mlp_b1, L0_attn_mlp_w2, L0_attn_mlp_b2)
    g = _silu(_L0_ffn_ref(xn, L0_ffn_ln1_w, L0_ffn_ln2_w, L0_ffn_wq, L0_ffn_wk, L0_ffn_wv, L0_ffn_wo, L0_ffn_gate_w, L0_ffn_w1, L0_ffn_w2, L0_ffn_w3))
    x = x + s * g
    xn = _layernorm(x, axis=-1)
    s = _L1_attn_ref(xn, L1_attn_Wq, L1_attn_bq, L1_attn_Wk, L1_attn_bk, L1_attn_Wv, L1_attn_bv, L1_attn_Wo, L1_attn_bo, L1_attn_m)
    g = _silu(_L1_ffn_ref(xn, L1_ffn_centroids, L1_ffn_ln_g, L1_ffn_ln_b, L1_ffn_w1, L1_ffn_b1, L1_ffn_w2, L1_ffn_b2))
    x = x + s * g
    return x

_drawn_inputs = setup_inputs


def setup_inputs(seed=0):
    import zlib

    import numpy as np

    out = dict(_drawn_inputs(seed))
    spreads = {'L0_attn_ln1_w': (1.0, 0.597),
     'L0_attn_ln1_b': (0.0, 0.638),
     'L0_attn_conv_b': (0.0, 0.1),
     'L0_attn_D': (1.0, 0.6),
     'L0_attn_norm_w': (1.0, 0.6),
     'L0_attn_ln2_w': (1.0, 0.6),
     'L0_attn_ln2_b': (0.0, 0.8),
     'L0_attn_mlp_b1': (0.0, 0.8),
     'L0_attn_mlp_b2': (0.0, 0.1),
     'L0_ffn_ln1_w': (1.0, 0.6),
     'L0_ffn_ln2_w': (1.0, 0.6),
     'L1_attn_bq': (0.0, 0.769),
     'L1_attn_bk': (0.0, 0.466),
     'L1_attn_bv': (0.0, 0.469),
     'L1_attn_bo': (0.0, 0.1),
     'L1_attn_m': (0.5, 0.6),
     'L1_ffn_ln_g': (1.0, 0.6),
     'L1_ffn_ln_b': (0.0, 0.8),
     'L1_ffn_b1': (0.0, 0.8),
     'L1_ffn_b2': (0.0, 0.8)}
    factors = {'L0_attn_dt_bias': 8.0,
     'L0_attn_A_log': 8.0,
     'L0_attn_mlp_w1': 2.998,
     'L0_attn_mlp_w2': 2.726,
     'L0_ffn_wq': 8.0,
     'L0_ffn_wk': 8.0,
     'L0_ffn_wv': 8.0,
     'L0_ffn_wo': 8.0,
     'L0_ffn_gate_w': 8.0,
     'L0_ffn_w1': 8.0,
     'L0_ffn_w2': 8.0,
     'L0_ffn_w3': 8.0,
     'L1_attn_Wq': 3.328,
     'L1_attn_Wk': 6.392,
     'L1_attn_Wv': 6.841,
     'L1_attn_Wo': 2.886,
     'L1_ffn_centroids': 2.961,
     'L1_ffn_w1': 3.501,
     'L1_ffn_w2': 2.864}
    for name, (base, spread) in spreads.items():
        noise = np.random.default_rng([zlib.crc32(name.encode()), seed]).standard_normal(out[name].shape)
        drawn = base * np.exp(spread * noise) if base else spread * noise
        out[name] = jnp.asarray(drawn.astype(out[name].dtype))
    for name, factor in factors.items():
        out[name] = (out[name] * factor).astype(out[name].dtype)
    return out
```

```python
from contextlib import ExitStack

import numpy as np

import concourse.bass as bass
from concourse import mybir

F32 = mybir.dt.float32
BF16 = mybir.dt.bfloat16
U32 = mybir.dt.uint32
ALU = mybir.AluOpType
ACT = mybir.ActivationFunctionType
AX = mybir.AxisListType

P = 128
B, T, D = 8, 512, 128
NT = T // P
HM, PM, NS, TAPS = 4, 64, 64, 4
DI = HM * PM
DIP = 2 * DI + 2 * NS + HM
MF = 4 * D
HA, DH = 16, 8
E, TOPK = 8, 2
I0, I1 = 256, 512
EPS = 1e-5
PAIRS = [(0, 0), (0, 1), (1, 0), (1, 1), (0, 2), (2, 0)]
KROWS = len(PAIRS) * DH
MROWS = KROWS + 3

PACK_A = dict(ident=P, le=P, gt=P, blk=P, iota=E, mhalf=NT, ln1w=1, ln1b=1, winT=DIP, cwx=8, cbx=2, cwbc=8,
              cbbc=2, dtb=HM, alog=HM, dskip=HM, nw=2, woutT=2 * D, ln2w=1, ln2b=1, mw1T=MF, mb1=NT, mw2T=4 * D,
              mb2=D, r1w=1, r2w=1, wqT=D, wkT=D, wvT=D, woT=D, gateT=E)
PACK_B = dict(ew1T=E * I0, ew3T=E * I0, ew2T=E * 2 * D)
PACK_C = dict(wqkv=3 * D, bqkv=3 * D, wo1=D, bo1=D, mcol=1, centT=E, lng=E, lnb=E, fb1=E * 4, fw1T=E * I1,
              fw2T=E * 4 * D)

SIGNALS = dict(
    bn=20, mv=20, xn=4, un=4, rr=1, tr_un=1, hA=1, hB=1,
    qk_ps=2, v_ps=1, xbc_ps=4, z_ps=2, dt_ps=1, q1=2, r1=2, q2=2, q3=2, vext=1, xbc=4, zs=2, dtraw=1,
    conv=4, xc=4, dtabs=1, dtu=1, adec=1, dt=1, av=4,
    xtr=4, xtok=4, cum_ps=1, ec=1, g_ps=1, gm=1, seg_ps=4, lex=4, wmat=4, xdt=4, xskip=4, xw=4,
    st_ps=3, state=4, y_ps=4, yi=4, yj=4, yk=4, yg=4, yr=1, ytr=1, yT=2, op_ps=1, x1=4,
    rr2=1, un2=4, res2=1, tr_un2=1, h2=1, up_ps=4, gel=4, down_ps=1, s0=1,
    mx_ps=64, mx=64, tr_mx=1, m1=1, mr=1, m2=1, m3=1, sc_ps=64, ex=64, pv=64, orec=2, att=2, tr_att=1, attT=1,
    wo_ps=1, hb=1,
    rr3=1, un3=4, tr_un3=1, h3=1, lg_ps=1, lg=1, top=8, topi=8, topf=1, tope=1, we=1,
    ea_ps=16, eb_ps=16, sa=16, hid=16, ed_ps=8, eacc=32, g0=1, sg0=1, x2=1,
    rr4=1, xn1=4, un4=4, tr_xn1=1, tr_un4=1, xn1T=1, un4T=1, qkv_ps=4, qkv=4, sq=1, nrm=1, inv=1,
    qkn=2, vk_ps=1, vkm=1, mm_ps=1, mm=1, qT_ps=1, qT=1, o1_ps=1, s1=1,
    af_ps=1, af=1, tpf1=1, tpe1=1, ohs=1, tr_ohs=1, ohT=1, b2_ps=1,
    fu_ps=32, fh=32, fd_ps=8, facc=33, g1=1, sg1=1, out=1,
    pool_chain=20, dve_chain=40,
    x_in=16, y_out=16, qk_store=32, qk_load=16 * 24, m_store=16, m_load=32)


def build(nc, x, pack_a, pack_b, pack_c, b2, out):
    with ExitStack() as ctx:
        def sb(name, shape, dt=F32):
            return ctx.enter_context(nc.sbuf_tensor(name, shape, dt))

        S = {name: ctx.enter_context(nc.semaphore(name)) for name in SIGNALS}
        done = ctx.enter_context(nc.semaphore("pass_done"))
        ENGINES = ("pe", "act", "dve", "pool")
        go = {k: ctx.enter_context(nc.semaphore("go_" + k)) for k in ENGINES}
        ids = sorted(x.num for x in S.values())
        assert ids == list(range(ids[0], ids[-1] + 1))

        def pass_ends(eng, name):
            eng.drain().then_inc(done, 1)
            eng.wait_ge(go[name], 1)
            eng.sem_clear(go[name])

        s_load = ctx.enter_context(nc.semaphore("tables_loaded"))
        s_set = {k: ctx.enter_context(nc.semaphore("setup_" + k)) for k in
                 ("fixed", "sig", "exps", "scal", "mask", "bias_ps", "bias", "fold")}

        tabs, cols = [], {}
        for name, pack in (("tab_a", PACK_A), ("tab_b", PACK_B), ("tab_c", PACK_C)):
            tab = sb(name, [P, sum(pack.values())])
            tabs.append(tab)
            at = 0
            for k, n in pack.items():
                cols[k] = tab[:, at:at + n]
                at += n
        C = cols
        ident = C["ident"]
        b2t = sb("b2t", [E, D])
        ones = sb("ones", [P, P])
        negA = sb("negA", [P, HM])
        msc = sb("msc", [P, P])
        mtmp = sb("mtmp", [P, 4])
        bias1 = sb("bias1", [P, E * 4])

        xin = sb("xin", [P, NT, D])
        xn = sb("xn", [P, NT, D])
        un = sb("un", [P, NT, D])
        hA = sb("hA", [P, T])
        hB = sb("hB", [P, T])
        bst = sb("bst", [P, NT, 6])
        mv = sb("mv", [P, NT, 2])
        sm = sb("sm", [P, 8, NT])
        part = sb("part", [P, 2, 3, T], BF16)
        rem = sb("rem", [P, 2, T])
        qx = sb("qx", [P, HA // 2, T], BF16)
        kx = sb("kx", [P, HA // 2, T], BF16)
        vext = sb("vext", [P, NT, HA, DH + 1])
        mx = sb("mx", [P, NT, HA])
        mpart = sb("mpart", [HA, 3, T], BF16)
        mrem = rem[0:HA, 0, :]
        pr = sb("pr", [P, 4, T])
        orec = sb("orec", [P, NT, HA])
        att = sb("att", [P, NT, D])
        attT = sb("attT", [P, T])
        hb = sb("hb", [P, NT, D])
        xbc = sb("xbc", [P, 4, T + TAPS - 1])
        fh = sb("fh", [P, 8, T])
        xc = fh[:, 0:4, :]
        wide8 = sb("wide8", [P, 8, T])
        quarter = lambda k: wide8[:, 2 * k:2 * k + 2, :].rearrange("p a (b n) -> p (a b) n", n=DI)
        zs, xskip, xw, yg = quarter(0), quarter(1), quarter(2), quarter(3)
        dts = sb("dts", [P, 8, NT * HM])
        av = fh[:, 4:8, :].rearrange("p c (h t) -> p c h t", h=HM)
        xtok = sb("xtok", [P, NT, DI + NS])
        ec = sb("ec", [P, NT, 2 * HM])
        gm = sb("gm", [P, NT, P])
        lex = sb("lex", [P, NT, HM, P])
        xdt = sb("xdt", [P, NT, DI])
        state = sb("state", [NS, NT + 1, DI])
        stmp = sb("stmp", [NS, DI])
        yT = sb("yT", [P, 2, T])
        x1 = sb("x1", [P, NT, D])
        h2 = sb("h2", [P, T])
        gel = lex[:, :, :, :].rearrange("p c h t -> p c (h t)")
        s0 = x1
        h3 = hB
        lg = sb("lg", [P, NT, E])
        top = sb("top", [P, NT, 8])
        topi = sb("topi", [P, NT, 8], U32)
        topf = sb("topf", [P, NT, 8])
        tw = sb("tw", [P, 6, NT])
        oh = sb("oh", [P, 2, NT, E])
        we = sb("we", [P, NT, E])
        hid = wide8[:, 0:4, :]
        sa = wide8[:, 4:7, :]
        g0 = attT[:, :].rearrange("p (j d) -> p j d", j=NT)
        x2 = hb
        xn1T, un4T = h2, hA
        qkv = pr[:, 0:3, :].rearrange("p a n -> p (a n)").rearrange("p (j n) -> p j n", j=NT)
        sq = xdt
        inv = sb("inv", [P, NT, 2 * HA])
        vkm, mm = gm[:, 0, :], gm[:, 1, :]
        qT = yT[:, 0, :]
        ohT = yT[0:E, 1, :]
        s1 = att
        PS = [ctx.enter_context(nc.psum_tensor(f"ps{i}", [P, 512], F32)) for i in range(8)]

        qk_dram = nc.dram_tensor("qk_scratch", [2, 3, P, T], BF16, kind="Internal").ap()
        m_dram = nc.dram_tensor("m_scratch", [3, HA, T], BF16, kind="Internal").ap()

        MX_RING = [5, 6, 7, 0, 1, 2]
        SC_RING = [0, 1, 2, 5]
        hm = lambda t: t.rearrange("p (h q) -> p h q", h=HM)
        tk = lambda t: t.rearrange("p (j n) -> p j n", j=NT)
        block = ctx.enter_context(nc.Block())

        @block.sync
        def _(sp):
            sp.dma_start(tabs[0][:, :], pack_a).then_inc(s_load, 16)
            sp.dma_start(tabs[2][:, :], pack_c).then_inc(s_load, 16)
            sp.dma_start(tabs[1][:, :], pack_b).then_inc(s_load, 16)
            sp.dma_start(b2t[:, :], b2).then_inc(s_load, 16)
            with sp.Fori(0, B) as it:
                sp.dma_start(xin[:, :, :], x[bass.ds(it, 1)].rearrange("a (j p) d -> p (a j) d", p=P)).then_inc(S["x_in"], 16)
                for s in range(2):
                    sp.wait_ge(S["q3"], s + 1)
                    sp.dma_start(qk_dram[s].rearrange("a p t -> p a t"), part[:, s, :, :]).then_inc(S["qk_store"], 16)
                for s in range(2):
                    sp.wait_ge(S["qk_store"], 32)
                    src = qk_dram[s].rearrange("a (g s d) t -> a s d g t", s=2, d=DH)
                    dst = (qx, kx)[s]
                    for j, pair in enumerate(PAIRS):
                        for h in range(2):
                            sp.dma_start(dst[64 * h + DH * j:64 * h + DH * (j + 1), :, :], src[pair[s], h]).then_inc(S["qk_load"], 16)
                sp.wait_ge(S["m3"], 1)
                sp.dma_start(m_dram.rearrange("a h t -> h a t"), mpart[:, :, :]).then_inc(S["m_store"], 16)
                sp.wait_ge(S["m_store"], 16)
                for h in range(2):
                    sp.dma_start(qx[64 * h + KROWS:64 * h + MROWS, :, :], m_dram.rearrange("a (g s) t -> s a g t", s=2)[h]).then_inc(S["m_load"], 16)
                sp.wait_ge(S["out"], 1)
                sp.dma_start(out[bass.ds(it, 1)].rearrange("a (j p) d -> p (a j) d", p=P), xn[:, :, :]).then_inc(S["y_out"], 16)
                sp.wait_ge(S["y_out"], 16)
                sp.wait_ge(done, len(ENGINES))
                sp.sem_clear(done)
                sp.sem_clear(range(ids[0], ids[-1] + 1))
                for k in ENGINES:
                    sp.sem_inc(go[k], 1)

        @block.tensor
        def _(pe):
            mmul = nc.tensor.matmul

            def turn(bank, src, width=D, rows=P, upto=NT):
                for j in range(upto):
                    last = nc.tensor.transpose(PS[bank][0:width, j * P:(j + 1) * P], src[:, j, :], ident)
                return last

            pe.wait_ge(s_load, 64)
            for e in range(E):
                for c in range(4):
                    n = e * 4 + c
                    ins = mmul(PS[0][:, n:n + 1], C["fw1T"][:, e * I1 + c * P:e * I1 + (c + 1) * P],
                               C["lnb"][:, e:e + 1], start=True, stop=True)
            ins.then_inc(s_set["bias_ps"], 1)
            pe.wait_ge(s_set["fixed"], 4)
            pe.wait_ge(s_set["bias"], 1)
            pe.wait_ge(s_set["fold"], E)

            with pe.Fori(0, B) as it:
                pe.wait_ge(S["un"], 4)
                turn(0, un).then_inc(S["tr_un"], 1)
                pe.wait_ge(S["hB"], 1)
                mmul(PS[1][:, :], C["wqT"], hB[:, :], start=True, stop=True).then_inc(S["qk_ps"], 1)
                mmul(PS[2][:, :], C["wkT"], hB[:, :], start=True, stop=True).then_inc(S["qk_ps"], 1)
                for j in range(NT):
                    ins = mmul(PS[3][:, j * D:(j + 1) * D], hB[:, j * P:(j + 1) * P], C["wvT"], start=True, stop=True)
                ins.then_inc(S["v_ps"], 1)
                pe.wait_ge(S["hA"], 1)
                for c, (a, n) in enumerate([(DI, P), (DI + P, P), (2 * DI, NS), (2 * DI + NS, NS)]):
                    mmul(PS[4 + c][0:n, :], C["winT"][:, a:a + n], hA[:, :], start=True, stop=True).then_inc(S["xbc_ps"], 1)
                pe.wait_ge(S["r1"], 1)
                for j in range(NT):
                    ins = mmul(PS[1][:, j * HM:(j + 1) * HM], hA[:, j * P:(j + 1) * P], C["winT"][:, DIP - HM:DIP],
                               start=True, stop=True)
                ins.then_inc(S["dt_ps"], 1)
                for k, bank in enumerate((0, 3)):
                    if k == 1:
                        pe.wait_ge(S["vext"], 1)
                    for j in range(2):
                        ins = mmul(PS[bank][:, j * DI:(j + 1) * DI], hA[:, (2 * k + j) * P:(2 * k + j + 1) * P],
                                   C["winT"][:, 0:DI], start=True, stop=True)
                    ins.then_inc(S["z_ps"], 1)
                pe.wait_ge(S["adec"], 1)
                pe.wait_ge(S["r1"], 2)
                for c in range(NT):
                    a = dts[:, 6, c * HM:(c + 1) * HM]
                    mmul(PS[2][:, c * 8:c * 8 + 4], C["le"], a, start=True, stop=True)
                    ins = mmul(PS[2][:, c * 8 + 4:c * 8 + 8], ones[:, :], a, start=True, stop=True)
                ins.then_inc(S["cum_ps"], 1)
                for c in range(NT):
                    pe.wait_ge(S["av"], c + 1)
                    if c == 0:
                        pe.wait_ge(S["dtraw"], 1)
                    elif c == 1:
                        pe.wait_ge(S["zs"], 2)
                    else:
                        pe.wait_ge(S["lex"], c - 1)
                    mmul(PS[(1, 3)[c % 2]][:, :], C["gt"], av[:, c, :, :], start=True, stop=True).then_inc(S["seg_ps"], 1)
                pe.wait_ge(S["xc"], 4)
                pe.wait_ge(S["zs"], 1)
                for c in range(NT):
                    ins = mmul(PS[0][:, c * P:(c + 1) * P], xc[0:NS, 2, c * P:(c + 1) * P],
                               xc[0:NS, 3, c * P:(c + 1) * P], start=True, stop=True)
                ins.then_inc(S["g_ps"], 1)
                for c in range(NT):
                    pe.wait_ge(S["xbc"], c + 1)
                    for k in range(2):
                        nc.tensor.transpose(PS[4 + c][:, k * P:(k + 1) * P], xc[:, k, c * P:(c + 1) * P], ident)
                    nc.tensor.transpose(PS[4 + c][:, DI:DI + NS], xc[0:NS, 2, c * P:(c + 1) * P], C["ident"][0:NS, 0:NS]).then_inc(S["xtr"], 1)
                for c in range(NT - 1):
                    pe.wait_ge(S["xtok"], c + 1)
                    pe.wait_ge(S["xw"], c + 1)
                    mmul(PS[4 + c][0:NS, 0:DI], xtok[:, c, DI:DI + NS], xw[:, c, :], start=True, stop=True).then_inc(S["st_ps"], 1)
                pe.wait_ge(S["gm"], 1)
                pe.wait_ge(S["ec"], 1)
                for c in range(NT):
                    pe.wait_ge(S["wmat"], c + 1)
                    pe.wait_ge(S["xdt"], c + 1)
                    if c in (1, 3):
                        pe.wait_ge(S["lex"], 3 + c // 2)
                    for h in range(HM):
                        mmul(PS[c][:, h * PM:(h + 1) * PM], av[:, c, h, :], xdt[:, c, h * PM:(h + 1) * PM],
                             start=True, stop=True)
                    pe.wait_ge(S["state"], c + 1)
                    mmul(PS[c][:, DI:2 * DI], xc[0:NS, 3, c * P:(c + 1) * P], state[:, c, :], start=True, stop=True).then_inc(S["y_ps"], 1)
                pe.wait_ge(S["state"], 4)
                pe.wait_ge(S["xtok"], 4)
                for j in range(NT):
                    pe.wait_ge(S["yg"], j + 1)
                    for k in range(2):
                        ins = nc.tensor.transpose(PS[4 + k][:, j * P:(j + 1) * P], yg[:, j, k * P:(k + 1) * P], ident)
                ins.then_inc(S["ytr"], 1)
                pe.wait_ge(S["yT"], 2)
                for j in range(NT):
                    for k in range(2):
                        ins = mmul(PS[6][:, j * D:(j + 1) * D], yT[:, k, j * P:(j + 1) * P],
                                   C["woutT"][:, k * D:(k + 1) * D], start=(k == 0), stop=(k == 1))
                ins.then_inc(S["op_ps"], 1)
                pe.wait_ge(S["un2"], 4)
                turn(7, un).then_inc(S["tr_un2"], 1)
                pe.wait_ge(S["h2"], 1)
                pe.wait_ge(S["yj"], 4)
                for c in range(4):
                    mmul(PS[c][:, :], C["mw1T"][:, c * P:(c + 1) * P], h2[:, :], start=True, stop=True).then_inc(S["up_ps"], 1)
                pe.wait_ge(S["gel"], 4)
                for j in range(NT):
                    for c in range(4):
                        ins = mmul(PS[4][:, j * D:(j + 1) * D], gel[:, c, j * P:(j + 1) * P],
                                   C["mw2T"][:, c * D:(c + 1) * D], start=(c == 0), stop=(c == 3))
                ins.then_inc(S["down_ps"], 1)
                pe.wait_ge(S["qk_load"], 384)
                pe.wait_ge(S["x1"], 4)
                for u in range(64):
                    h, j = divmod(u, NT)
                    a = 64 * (h % 2)
                    if u >= len(MX_RING):
                        pe.wait_ge(S["mx"], u - len(MX_RING) + 1)
                    mmul(PS[MX_RING[u % len(MX_RING)]][:, :], qx[a:a + KROWS, h // 2, j * P:(j + 1) * P], kx[a:a + KROWS, h // 2, :], start=True, stop=True).then_inc(S["mx_ps"], 1)
                pe.wait_ge(S["mx"], 64)
                turn(3, mx, HA).then_inc(S["tr_mx"], 1)

                def score(u):
                    h, k = divmod(u, NT)
                    a = 64 * (h % 2)
                    if u >= len(SC_RING):
                        pe.wait_ge(S["ex"], u - len(SC_RING) + 1)
                    mmul(PS[SC_RING[u % len(SC_RING)]][:, :], kx[a:a + MROWS, h // 2, k * P:(k + 1) * P], qx[a:a + MROWS, h // 2, :], start=True, stop=True).then_inc(S["sc_ps"], 1)

                def values(u):
                    h, k = divmod(u, NT)
                    pe.wait_ge(S["ex"], u + 1)
                    for j in range(NT):
                        o = (j % 2) * HA * (DH + 1) + h * (DH + 1)
                        ins = mmul(PS[6 + j // 2][:, o:o + DH + 1], pr[:, u % 4, j * P:(j + 1) * P],
                                   vext[:, k, h, :], start=(k == 0 and j % 2 == 0), stop=(k == 3),
                                   skip_group_check=True)
                    ins.then_inc(S["pv"], 1)

                pe.wait_ge(S["m_load"], 32)
                for u in range(2):
                    score(u)
                for u in range(64):
                    if u + 2 < 64:
                        score(u + 2)
                    values(u)
                pe.wait_ge(S["att"], 2)
                pe.wait_ge(S["m1"], 1)
                pe.wait_ge(S["mr"], 1)
                turn(3, att).then_inc(S["tr_att"], 1)
                pe.wait_ge(S["attT"], 1)
                pe.wait_ge(S["s0"], 1)
                for j in range(NT):
                    ins = mmul(PS[4][:, j * D:(j + 1) * D], attT[:, j * P:(j + 1) * P], C["woT"], start=True, stop=True)
                ins.then_inc(S["wo_ps"], 1)
                pe.wait_ge(S["un3"], 4)
                turn(0, un).then_inc(S["tr_un3"], 1)
                pe.wait_ge(S["h3"], 1)
                for j in range(NT):
                    ins = mmul(PS[1][:, j * E:(j + 1) * E], h3[:, j * P:(j + 1) * P], C["gateT"], start=True, stop=True)
                ins.then_inc(S["lg_ps"], 1)
                pe.wait_ge(S["lg"], 1)

                def expert_up(u):
                    pair = u % 3
                    if u >= 3:
                        pe.wait_ge(S["hid"], u - 2)
                    mmul(PS[2 * pair][:, :], C["ew1T"][:, u * P:(u + 1) * P], h3[:, :], start=True, stop=True).then_inc(S["ea_ps"], 1)
                    mmul(PS[2 * pair + 1][:, :], C["ew3T"][:, u * P:(u + 1) * P], h3[:, :], start=True, stop=True).then_inc(S["eb_ps"], 1)

                def expert_down(e):
                    pe.wait_ge(S["hid"], 2 * e + 2)
                    if e >= 2:
                        pe.wait_ge(S["eacc"], 4 * (e - 1))
                    for j in range(NT):
                        for c in range(2):
                            u = 2 * e + c
                            ins = mmul(PS[6 + e % 2][:, j * D:(j + 1) * D], hid[:, u % 4, j * P:(j + 1) * P],
                                       C["ew2T"][:, u * D:(u + 1) * D], start=(c == 0), stop=(c == 1))
                    ins.then_inc(S["ed_ps"], 1)

                pe.wait_ge(S["hb"], 1)
                for e in range(E):
                    expert_up(2 * e)
                    if e:
                        expert_down(e - 1)
                    expert_up(2 * e + 1)
                expert_down(E - 1)
                pe.wait_ge(S["xn1"], 4)
                pe.wait_ge(S["hid"], 16)
                turn(0, xn).then_inc(S["tr_xn1"], 1)
                pe.wait_ge(S["un4"], 4)
                turn(1, un).then_inc(S["tr_un4"], 1)
                pe.wait_ge(S["xn1T"], 1)
                for j in range(NT):
                    mmul(PS[2 + j][:, 0:3 * D], xn1T[:, j * P:(j + 1) * P], C["wqkv"], start=True, stop=True).then_inc(S["qkv_ps"], 1)
                for j in range(NT):
                    ins = mmul(PS[0][:, j * E:(j + 1) * E], xn1T[:, j * P:(j + 1) * P], C["centT"],
                               start=True, stop=True)
                ins.then_inc(S["af_ps"], 1)
                pe.wait_ge(S["qkn"], 2)
                pe.wait_ge(S["eacc"], 32)
                for j in range(NT):
                    ins = mmul(PS[6][:, 0:P], qkv[:, j, 2 * D:3 * D], qkv[:, j, D:2 * D], start=(j == 0),
                               stop=(j == NT - 1))
                ins.then_inc(S["vk_ps"], 1)
                turn(2, qkv[:, :, 0:D]).then_inc(S["qT_ps"], 1)
                pe.wait_ge(S["vkm"], 1)
                mmul(PS[7][:, 0:P], vkm, C["wo1"], start=True, stop=True).then_inc(S["mm_ps"], 1)
                pe.wait_ge(S["ohs"], 1)
                pe.wait_ge(S["un4T"], 1)
                for j in range(NT):
                    ins = nc.tensor.transpose(PS[1][0:E, j * P:(j + 1) * P], we[:, j, :], ident)
                ins.then_inc(S["tr_ohs"], 1)
                pe.wait_ge(S["mm"], 1)
                pe.wait_ge(S["qT"], 1)
                for j in range(NT):
                    ins = mmul(PS[3][:, j * D:(j + 1) * D], qT[:, j * P:(j + 1) * P], mm, start=True, stop=True)
                ins.then_inc(S["o1_ps"], 1)
                pe.wait_ge(S["ohT"], 1)
                for j in range(NT):
                    ins = mmul(PS[4][:, j * D:(j + 1) * D], ohT[:, j * P:(j + 1) * P], b2t[:, :], start=True, stop=True)
                ins.then_inc(S["b2_ps"], 1)

                def ffn_up(u):
                    if u >= 6:
                        pe.wait_ge(S["fh"], u - 5)
                    mmul(PS[u % 6][:, :], C["fw1T"][:, u * P:(u + 1) * P], un4T[:, :], start=True, stop=True).then_inc(S["fu_ps"], 1)

                def ffn_down(e):
                    pe.wait_ge(S["fh"], 4 * e + 4)
                    if e >= 2:
                        pe.wait_ge(S["facc"], 4 * (e - 1) + 1)
                    for j in range(NT):
                        for c in range(4):
                            u = 4 * e + c
                            ins = mmul(PS[6 + e % 2][:, j * D:(j + 1) * D], fh[:, u % 8, j * P:(j + 1) * P],
                                       C["fw2T"][:, u * D:(u + 1) * D], start=(c == 0), stop=(c == 3))
                    ins.then_inc(S["fd_ps"], 1)

                pe.wait_ge(S["s1"], 1)
                pe.wait_ge(S["facc"], 1)
                for e in range(E):
                    for c in range(2):
                        ffn_up(4 * e + c)
                    if e:
                        ffn_down(e - 1)
                    for c in range(2, 4):
                        ffn_up(4 * e + c)
                ffn_down(E - 1)
                pass_ends(pe, "pe")

        @block.scalar
        def _(act):
            A = nc.scalar.activation
            act.wait_ge(s_load, 64)
            A(mtmp[:, 0:1], C["mcol"], ACT.Exp, scale=-1.0).then_inc(s_set["exps"], 1)
            A(negA[:, :], C["alog"], ACT.Exp).then_inc(s_set["exps"], 1)
            act.wait_ge(s_set["sig"], 2)
            A(mtmp[:, 3:4], mtmp[:, 2:3], ACT.Exp, scale=-float(np.log(T))).then_inc(s_set["scal"], 1)
            with act.Fori(0, B) as it:
                act.wait_ge(S["hA"], 1)
                A(hB[:, :], PS[0][:, :], ACT.Copy, scale=C["r1w"]).then_inc(S["hB"], 1)
                for s in range(2):
                    act.wait_ge(S["qk_ps"], s + 1)
                    A(part[:, s, 0, :], PS[1 + s][:, :], ACT.Copy).then_inc(S["q1"], 1)
                act.wait_ge(S["v_ps"], 1)
                A(vext[:, :, :, 0:DH], PS[3][:, :].rearrange("p (j h d) -> p j h d", j=NT, h=HA), ACT.Copy).then_inc(S["vext"], 1)
                for c in range(4):
                    n = P if c < 2 else NS
                    act.wait_ge(S["xbc_ps"], c + 1)
                    A(xbc[0:n, c, TAPS - 1:], PS[4 + c][0:n, :], ACT.Copy).then_inc(S["xbc"], 1)
                act.wait_ge(S["dtabs"], 1)
                A(dts[:, 2, :], dts[:, 1, :], ACT.Exp, scale=-1.0).then_inc(S["dtu"], 1)
                for k in range(2):
                    act.wait_ge(S["z_ps"], k + 1)
                    A(zs[:, 2 * k:2 * k + 2, :], PS[(0, 3)[k]][:, :].rearrange("p (j n) -> p j n", j=2), ACT.Silu).then_inc(S["zs"], 1)
                for c in range(4):
                    n = P if c < 2 else NS
                    act.wait_ge(S["conv"], c + 1)
                    A(xc[0:n, c, :], xc[0:n, c, :], ACT.Silu).then_inc(S["xc"], 1)
                act.wait_ge(S["cum_ps"], 1)
                A(ec[:, :, :], PS[2][:, 0:NT * 8].rearrange("p (c n) -> p c n", c=NT), ACT.Exp).then_inc(S["ec"], 1)
                for c in range(NT):
                    act.wait_ge(S["seg_ps"], c + 1)
                    A(lex[:, c, :, :], hm(PS[(1, 3)[c % 2]][:, :]), ACT.Exp).then_inc(S["lex"], 1)
                for c in range(NT):
                    act.wait_ge(S["xtr"], c + 1)
                    A(xtok[:, c, :], PS[4 + c][:, 0:DI + NS], ACT.Copy).then_inc(S["xtok"], 1)
                act.wait_ge(S["ytr"], 1)
                for k in range(2):
                    A(yT[:, k, :], PS[4 + k][:, :], ACT.Copy, scale=C["nw"][:, k:k + 1]).then_inc(S["yT"], 1)
                for c in range(4):
                    act.wait_ge(S["up_ps"], c + 1)
                    A(gel[:, c, :], PS[c][:, :], ACT.Gelu, bias=C["mb1"][:, c:c + 1]).then_inc(S["gel"], 1)
                act.wait_ge(S["tr_mx"], 1)
                A(mpart[:, 0, :], PS[3][0:HA, :], ACT.Copy, scale=-1.0).then_inc(S["m1"], 1)
                for u in range(64):
                    act.wait_ge(S["sc_ps"], u + 1)
                    if u >= 4:
                        act.wait_ge(S["pv"], u - 3)
                    A(pr[:, u % 4, :], PS[SC_RING[u % len(SC_RING)]][:, :], ACT.Exp, scale=float(DH) ** -0.5).then_inc(S["ex"], 1)
                act.wait_ge(S["tr_att"], 1)
                A(attT[:, :], PS[3][:, :], ACT.Copy).then_inc(S["attT"], 1)
                act.wait_ge(S["tr_un3"], 1)
                A(h3[:, :], PS[0][:, :], ACT.Copy, scale=C["r2w"]).then_inc(S["h3"], 1)
                act.wait_ge(S["topf"], 1)
                A(tw[:, 1, :], tw[:, 0, :], ACT.Exp).then_inc(S["tope"], 1)
                for u in range(16):
                    act.wait_ge(S["ea_ps"], u + 1)
                    if u >= 3:
                        act.wait_ge(S["hid"], u - 2)
                    A(sa[:, u % 3, :], PS[2 * (u % 3)][:, :], ACT.Silu).then_inc(S["sa"], 1)
                act.wait_ge(S["eacc"], 32)
                A(g0[:, :, :], hb[:, :, :], ACT.Silu).then_inc(S["g0"], 1)
                act.wait_ge(S["tr_xn1"], 1)
                A(xn1T[:, :], PS[0][:, :], ACT.Copy).then_inc(S["xn1T"], 1)
                act.wait_ge(S["tpf1"], 1)
                A(tw[:, 1, :], tw[:, 0, :], ACT.Exp, scale=-1.0).then_inc(S["tpe1"], 1)
                act.wait_ge(S["qT_ps"], 1)
                A(qT, PS[2][:, :], ACT.Copy).then_inc(S["qT"], 1)
                act.wait_ge(S["mm_ps"], 1)
                A(mm, PS[7][:, 0:P], ACT.Copy).then_inc(S["mm"], 1)
                act.wait_ge(S["tr_ohs"], 1)
                A(ohT, PS[1][0:E, :], ACT.Copy).then_inc(S["ohT"], 1)
                for u in range(32):
                    act.wait_ge(S["fu_ps"], u + 1)
                    if u >= 8:
                        act.wait_ge(S["fd_ps"], u // 4 - 1)
                    A(fh[:, u % 8, :], PS[u % 6][:, :], ACT.Relu, bias=bias1[:, u:u + 1]).then_inc(S["fh"], 1)
                act.wait_ge(S["facc"], 33)
                A(g0[:, :, :], x1[:, :, :], ACT.Silu).then_inc(S["g1"], 1)
                pass_ends(act, "act")

        @block.vector
        def _(dve):
            V = nc.vector
            V.memset(ones[:, :], 1.0).then_inc(s_set["fixed"], 1)
            V.memset(xbc[:, :, 0:TAPS - 1], 0.0)
            V.memset(vext[:, :, :, DH:DH + 1], 1.0)
            V.memset(state[:, 0, :], 0.0).then_inc(s_set["fixed"], 1)
            V.memset(kx[32:64, :, :], 1.0).then_inc(s_set["fixed"], 1)
            V.memset(kx[96:128, :, :], 1.0).then_inc(s_set["fixed"], 1)
            dve.wait_ge(s_load, 64)
            dve.wait_ge(s_set["exps"], 2)
            V.tensor_scalar(negA[:, :], negA[:, :], -1.0, None, ALU.mult).then_inc(s_set["mask"], 1)
            V.tensor_scalar(mtmp[:, 1:2], mtmp[:, 0:1], 1.0, None, ALU.add).then_inc(s_set["sig"], 1)
            dve.wait_ge(s_set["sig"], 1)
            V.reciprocal(mtmp[:, 2:3], mtmp[:, 1:2]).then_inc(s_set["sig"], 1)
            dve.wait_ge(s_set["scal"], 1)
            V.tensor_scalar(msc[:, :], C["blk"], mtmp[:, 3:4], None, ALU.mult).then_inc(s_set["mask"], 1)
            dve.wait_ge(s_set["bias_ps"], 1)
            V.tensor_tensor(bias1[:, :], PS[0][:, 0:E * 4], C["fb1"], ALU.add).then_inc(s_set["bias"], 1)
            for e in range(E):
                w = C["fw1T"][:, e * I1:(e + 1) * I1]
                V.tensor_scalar(w, w, C["lng"][:, e:e + 1], None, ALU.mult).then_inc(s_set["fold"], 1)
            dve.wait_ge(s_set["mask"], 2)
            dve.wait_ge(s_set["fixed"], 4)

            with dve.Fori(0, B) as it:
                links = [0]

                def link(ins):
                    ins.then_inc(S["dve_chain"], 1)
                    links[0] += 1
                    dve.wait_ge(S["dve_chain"], links[0])

                def stats(src, n):
                    for j in range(NT):
                        V.bn_stats(bst[:, j, :], src(j)).then_inc(S["bn"], 1)
                    for j in range(NT):
                        dve.wait_ge(S["bn"], n * NT + j + 1)
                        V.bn_aggr(mv[:, j, :], bst[:, j, :]).then_inc(S["mv"], 1)

                dve.wait_ge(S["x_in"], 16)
                stats(lambda j: xin[:, j, :], 0)
                dve.wait_ge(S["rr"], 1)
                for j in range(NT):
                    V.tensor_scalar(un[:, j, :], xin[:, j, :], mv[:, j, 0:1], sm[:, 3, j:j + 1], ALU.subtract, ALU.mult).then_inc(S["un"], 1)
                for j in range(NT):
                    V.tensor_scalar(xn[:, j, :], xin[:, j, :], mv[:, j, 0:1], sm[:, 1, j:j + 1], ALU.subtract, ALU.mult).then_inc(S["xn"], 1)
                dve.wait_ge(S["tr_un"], 1)
                V.tensor_scalar(hA[:, :], PS[0][:, :], C["ln1w"], C["ln1b"], ALU.mult, ALU.add).then_inc(S["hA"], 1)
                for s in range(2):
                    dve.wait_ge(S["q1"], s + 1)
                    V.tensor_tensor(rem[:, s, :], PS[1 + s][:, :], part[:, s, 0, :], ALU.subtract).then_inc(S["r1"], 1)
                dve.wait_ge(S["dt_ps"], 1)
                bc = lambda t, n=NT: t.rearrange("p (a h) -> p a h", a=1).broadcast_to([P, n, t.shape[1]])
                t4 = lambda k: dts[:, k, :].rearrange("p (j h) -> p j h", j=NT)
                V.tensor_tensor(t4(0), PS[1][:, 0:NT * HM].rearrange("p (j h) -> p j h", j=NT), bc(C["dtb"]), ALU.add).then_inc(S["dtraw"], 1)
                dve.wait_ge(S["dtraw"], 1)
                V.scalar_tensor_tensor(dts[:, 1, :], dts[:, 0, :], -1.0, dts[:, 0, :], ALU.mult, ALU.max).then_inc(S["dtabs"], 1)
                for c in range(4):
                    n = P if c < 2 else NS
                    w = C["cwx"][:, c * 4:c * 4 + 4] if c < 2 else C["cwbc"][0:NS, (c - 2) * 4:(c - 2) * 4 + 4]
                    b = C["cbx"][:, c:c + 1] if c < 2 else C["cbbc"][0:NS, c - 2:c - 1]
                    dve.wait_ge(S["xbc"], c + 1)
                    link(V.tensor_scalar(xc[0:n, c, :], xbc[0:n, c, 0:T], w[:, 0:1], b, ALU.mult, ALU.add))
                    for k in range(1, TAPS):
                        ins = V.scalar_tensor_tensor(xc[0:n, c, :], xbc[0:n, c, k:k + T], w[:, k:k + 1], xc[0:n, c, :],
                                                     ALU.mult, ALU.add)
                        if k < TAPS - 1:
                            link(ins)
                        else:
                            ins.then_inc(S["conv"], 1)
                dve.wait_ge(S["dtu"], 1)
                link(V.tensor_scalar(dts[:, 3, :], dts[:, 2, :], 2.0, None, ALU.add))
                link(V.reciprocal(dts[:, 4, :], dts[:, 3, :]))
                link(V.tensor_tensor(dts[:, 3, :], dts[:, 2, :], dts[:, 4, :], ALU.mult))
                link(V.tensor_tensor(dts[:, 4, :], dts[:, 3, :], dts[:, 3, :], ALU.mult))
                link(V.tensor_scalar(dts[:, 5, :], dts[:, 4, :], 1.0 / 15, None, ALU.mult))
                for k in (13, 11, 9, 7, 5, 3):
                    link(V.scalar_tensor_tensor(dts[:, 5, :], dts[:, 5, :], 1.0 / k, dts[:, 4, :], ALU.add, ALU.mult))
                link(V.tensor_scalar(dts[:, 5, :], dts[:, 5, :], 1.0, 2.0, ALU.add, ALU.mult))
                link(V.tensor_tensor(dts[:, 5, :], dts[:, 5, :], dts[:, 3, :], ALU.mult))
                V.scalar_tensor_tensor(dts[:, 7, :], dts[:, 0, :], 0.0, dts[:, 5, :], ALU.max, ALU.add).then_inc(S["dt"], 1)
                dve.wait_ge(S["dt"], 1)
                V.tensor_tensor(t4(6), t4(7), bc(negA[:, :]), ALU.mult).then_inc(S["adec"], 1)
                dve.wait_ge(S["adec"], 1)
                for c in range(NT):
                    a = dts[:, 6, c * HM:(c + 1) * HM].rearrange("p (h a) -> p h a", a=1).broadcast_to([P, HM, P])
                    V.tensor_tensor(av[:, c, :, :], bc(C["le"], HM), a, ALU.mult).then_inc(S["av"], 1)
                dve.wait_ge(S["g_ps"], 1)
                V.tensor_tensor(gm[:, :, :], tk(PS[0][:, :]), bc(C["le"], NT), ALU.mult).then_inc(S["gm"], 1)
                dve.wait_ge(S["gm"], 1)
                for c in range(NT):
                    dve.wait_ge(S["lex"], c + 1)
                    V.tensor_tensor(av[:, c, :, :], lex[:, c, :, :], bc(gm[:, c, :], HM), ALU.mult).then_inc(S["wmat"], 1)
                V.memset(state[:, 0, :], 0.0).then_inc(S["state"], 1)
                dve.wait_ge(S["ec"], 1)
                for c in range(NT - 1):
                    dve.wait_ge(S["state"], c + 1)
                    tot = ec[0:NS, c, HM:2 * HM].rearrange("p (h a) -> p h a", a=1).broadcast_to([NS, HM, PM])
                    link(V.tensor_tensor(hm(stmp[:, :]), hm(state[:, c, :]), tot, ALU.mult))
                    dve.wait_ge(S["st_ps"], c + 1)
                    V.tensor_tensor(state[:, c + 1, :], stmp[:, :], PS[4 + c][0:NS, 0:DI], ALU.add).then_inc(S["state"], 1)
                for c in range(NT):
                    dve.wait_ge(S["y_ps"], c + 1)
                    cum = ec[:, c, 0:HM].rearrange("p (h a) -> p h a", a=1).broadcast_to([P, HM, PM])
                    V.tensor_tensor(hm(yg[:, c, :]), hm(PS[c][:, DI:2 * DI]), cum, ALU.mult).then_inc(S["yi"], 1)
                    dve.wait_ge(S["yi"], c + 1)
                    V.tensor_tensor(yg[:, c, :], yg[:, c, :], PS[c][:, 0:DI], ALU.add).then_inc(S["yj"], 1)
                dve.wait_ge(S["yg"], 4)
                stats(lambda j: yg[:, j, :], 1)
                dve.wait_ge(S["op_ps"], 1)
                dve.wait_ge(S["yr"], 1)
                for j in range(NT):
                    V.scalar_tensor_tensor(x1[:, j, :], PS[6][:, j * D:(j + 1) * D], sm[:, 1, j:j + 1], xn[:, j, :], ALU.mult, ALU.add).then_inc(S["x1"], 1)
                dve.wait_ge(S["x1"], 4)
                stats(lambda j: x1[:, j, :], 2)
                dve.wait_ge(S["rr2"], 1)
                for j in range(NT):
                    V.tensor_scalar(un[:, j, :], x1[:, j, :], mv[:, j, 0:1], sm[:, 1, j:j + 1], ALU.subtract, ALU.mult).then_inc(S["un2"], 1)
                dve.wait_ge(S["tr_un2"], 1)
                V.tensor_scalar(h2[:, :], PS[7][:, :], C["ln2w"], C["ln2b"], ALU.mult, ALU.add).then_inc(S["h2"], 1)
                dve.wait_ge(S["down_ps"], 1)
                dve.wait_ge(S["res2"], 1)
                V.tensor_tensor(s0[:, :, :], tk(PS[4][:, :]), x1[:, :, :], ALU.add).then_inc(S["s0"], 1)
                for u in range(64):
                    h, j = divmod(u, NT)
                    dve.wait_ge(S["mx_ps"], u + 1)
                    V.tensor_reduce(mx[:, j, h:h + 1], PS[MX_RING[u % len(MX_RING)]][:, :], AX.X, ALU.max).then_inc(S["mx"], 1)
                dve.wait_ge(S["m1"], 1)
                V.scalar_tensor_tensor(mrem, PS[3][0:HA, :], -1.0, mpart[:, 0, :], ALU.mult, ALU.subtract).then_inc(S["mr"], 1)
                dve.wait_ge(S["pv"], 64)
                for k in range(2):
                    o = PS[6 + k][:, 0:2 * HA * (DH + 1)].rearrange("p (j h d) -> p j h d", j=2, h=HA)
                    V.reciprocal(orec[:, 2 * k:2 * k + 2, :], o[:, :, :, DH]).then_inc(S["orec"], 1)
                    dve.wait_ge(S["orec"], k + 1)
                    r = orec[:, 2 * k:2 * k + 2, :].rearrange("p j (h a) -> p j h a", a=1).broadcast_to([P, 2, HA, DH])
                    V.tensor_tensor(att[:, 2 * k:2 * k + 2, :].rearrange("p j (h d) -> p j h d", h=HA), o[:, :, :, 0:DH], r, ALU.mult).then_inc(S["att"], 1)
                dve.wait_ge(S["wo_ps"], 1)
                V.tensor_tensor(hb[:, :, :], tk(PS[4][:, :]), xn[:, :, :], ALU.add).then_inc(S["hb"], 1)
                dve.wait_ge(S["hb"], 1)
                stats(lambda j: hb[:, j, :], 3)
                dve.wait_ge(S["rr3"], 1)
                for j in range(NT):
                    V.tensor_scalar(un[:, j, :], hb[:, j, :], sm[:, 1, j:j + 1], None, ALU.mult).then_inc(S["un3"], 1)
                dve.wait_ge(S["lg_ps"], 1)
                V.tensor_copy(lg[:, :, :], tk(PS[1][:, 0:NT * E])).then_inc(S["lg"], 1)
                dve.wait_ge(S["lg"], 1)
                for j in range(NT):
                    V.max(top[:, j, :], lg[:, j, :]).then_inc(S["top"], 1)
                for j in range(NT):
                    dve.wait_ge(S["top"], j + 1)
                    V.max_index(topi[:, j, :], top[:, j, :], lg[:, j, :]).then_inc(S["topi"], 1)
                dve.wait_ge(S["topi"], 4)
                link(V.tensor_copy(topf[:, :, :], topi[:, :, :]))
                V.tensor_tensor(tw[:, 0, :], top[:, :, 1], top[:, :, 0], ALU.subtract).then_inc(S["topf"], 1)
                wide = lambda t: t.rearrange("p (j a) -> p j a", a=1).broadcast_to([P, NT, E])
                io = bc(C["iota"], NT)
                link(V.tensor_tensor(oh[:, 0, :, :], io, wide(topf[:, :, 0]), ALU.is_equal))
                link(V.tensor_tensor(oh[:, 1, :, :], io, wide(topf[:, :, 1]), ALU.is_equal))
                dve.wait_ge(S["tope"], 1)
                link(V.tensor_scalar(tw[:, 2, :], tw[:, 1, :], 1.0, None, ALU.add))
                link(V.reciprocal(tw[:, 3, :], tw[:, 2, :]))
                link(V.tensor_tensor(tw[:, 4, :], tw[:, 3, :], tw[:, 1, :], ALU.mult))
                link(V.tensor_tensor(oh[:, 0, :, :], oh[:, 0, :, :], wide(tw[:, 3, :]), ALU.mult))
                link(V.tensor_tensor(oh[:, 1, :, :], oh[:, 1, :, :], wide(tw[:, 4, :]), ALU.mult))
                V.tensor_tensor(we[:, :, :], oh[:, 0, :, :], oh[:, 1, :, :], ALU.add).then_inc(S["we"], 1)
                dve.wait_ge(S["we"], 1)

                def expert_hidden(u):
                    dve.wait_ge(S["sa"], u + 1)
                    dve.wait_ge(S["eb_ps"], u + 1)
                    if u >= 4:
                        dve.wait_ge(S["ed_ps"], u // 2 - 1)
                    V.tensor_tensor(hid[:, u % 4, :], sa[:, u % 3, :], PS[2 * (u % 3) + 1][:, :], ALU.mult).then_inc(S["hid"], 1)

                def expert_sum(e):
                    dve.wait_ge(S["ed_ps"], e + 1)
                    for j in range(NT):
                        if e:
                            dve.wait_ge(S["eacc"], 4 * (e - 1) + j + 1)
                        V.scalar_tensor_tensor(hb[:, j, :], PS[6 + e % 2][:, j * D:(j + 1) * D], we[:, j, e:e + 1], hb[:, j, :], ALU.mult, ALU.add).then_inc(S["eacc"], 1)

                for e in range(E):
                    expert_hidden(2 * e)
                    if e:
                        expert_sum(e - 1)
                    expert_hidden(2 * e + 1)
                expert_sum(E - 1)
                dve.wait_ge(S["g0"], 1)
                V.tensor_tensor(x2[:, :, :], s0[:, :, :], g0[:, :, :], ALU.mult).then_inc(S["sg0"], 1)
                dve.wait_ge(S["sg0"], 1)
                V.tensor_tensor(x2[:, :, :], x2[:, :, :], xin[:, :, :], ALU.add).then_inc(S["x2"], 1)
                dve.wait_ge(S["x2"], 1)
                stats(lambda j: x2[:, j, :], 4)
                dve.wait_ge(S["rr4"], 1)
                for j in range(NT):
                    V.tensor_scalar(xn[:, j, :], x2[:, j, :], mv[:, j, 0:1], sm[:, 1, j:j + 1], ALU.subtract, ALU.mult).then_inc(S["xn1"], 1)
                for j in range(NT):
                    V.tensor_scalar(un[:, j, :], x2[:, j, :], mv[:, j, 0:1], sm[:, 3, j:j + 1], ALU.subtract, ALU.mult).then_inc(S["un4"], 1)
                dve.wait_ge(S["tr_un4"], 1)
                V.tensor_copy(un4T[:, :], PS[1][:, :]).then_inc(S["un4T"], 1)
                for j in range(NT):
                    dve.wait_ge(S["qkv_ps"], j + 1)
                    V.tensor_tensor(qkv[:, j, :], PS[2 + j][:, 0:3 * D], C["bqkv"], ALU.add).then_inc(S["qkv"], 1)
                dve.wait_ge(S["sq"], 1)
                V.tensor_reduce(inv[:, :, :], sq[:, :, :].rearrange("p j (h d) -> p j h d", d=DH), AX.X, ALU.add).then_inc(S["nrm"], 1)
                dve.wait_ge(S["af_ps"], 1)
                V.tensor_copy(lg[:, :, :], tk(PS[0][:, 0:NT * E])).then_inc(S["af"], 1)
                dve.wait_ge(S["af"], 1)
                for j in range(NT):
                    V.max(top[:, j, :], lg[:, j, :]).then_inc(S["top"], 1)
                for j in range(NT):
                    dve.wait_ge(S["top"], 5 + j)
                    V.max_index(topi[:, j, :], top[:, j, :], lg[:, j, :]).then_inc(S["topi"], 1)
                dve.wait_ge(S["topi"], 8)
                link(V.tensor_copy(topf[:, :, :], topi[:, :, :]))
                V.tensor_copy(tw[:, 0, :], top[:, :, 0]).then_inc(S["tpf1"], 1)
                link(V.tensor_tensor(oh[:, 0, :, :], io, wide(topf[:, :, 0]), ALU.is_equal))
                dve.wait_ge(S["tpe1"], 1)
                link(V.tensor_scalar(tw[:, 2, :], tw[:, 1, :], 1.0, None, ALU.add))
                link(V.reciprocal(tw[:, 3, :], tw[:, 2, :]))
                V.tensor_tensor(we[:, :, :], oh[:, 0, :, :], wide(tw[:, 3, :]), ALU.mult).then_inc(S["ohs"], 1)
                dve.wait_ge(S["vk_ps"], 1)
                V.tensor_tensor(vkm, PS[6][:, 0:P], msc[:, :], ALU.mult).then_inc(S["vkm"], 1)
                dve.wait_ge(S["o1_ps"], 1)
                V.tensor_tensor(s1[:, :, :], tk(PS[3][:, :]), bc(C["bo1"], NT), ALU.add).then_inc(S["s1"], 1)
                dve.wait_ge(S["b2_ps"], 1)
                V.tensor_tensor(x1[:, :, :], tk(PS[4][:, :]), xn[:, :, :], ALU.add).then_inc(S["facc"], 1)
                for e in range(E):
                    dve.wait_ge(S["fd_ps"], e + 1)
                    for j in range(NT):
                        dve.wait_ge(S["facc"], 1 if e == 0 else 4 * (e - 1) + j + 2)
                        V.scalar_tensor_tensor(x1[:, j, :], PS[6 + e % 2][:, j * D:(j + 1) * D], we[:, j, e:e + 1], x1[:, j, :], ALU.mult, ALU.add).then_inc(S["facc"], 1)
                dve.wait_ge(S["g1"], 1)
                V.tensor_tensor(s1[:, :, :], s1[:, :, :], g0[:, :, :], ALU.mult).then_inc(S["sg1"], 1)
                dve.wait_ge(S["sg1"], 1)
                V.tensor_tensor(xn[:, :, :], s1[:, :, :], x2[:, :, :], ALU.add).then_inc(S["out"], 1)
                pass_ends(dve, "dve")

        @block.gpsimd
        def _(pool):
            G = nc.gpsimd
            pool.wait_ge(s_load, 64)
            with pool.Fori(0, B) as it:
                links = [0]

                def link(ins):
                    ins.then_inc(S["pool_chain"], 1)
                    links[0] += 1
                    pool.wait_ge(S["pool_chain"], links[0])

                def rsqrt(k, src, signal=None):
                    link(G.tensor_scalar(sm[:, k, :], src, EPS, None, ALU.add))
                    ins = G.tensor_tensor(sm[:, k, :], sm[:, k, :], C["mhalf"], ALU.pow)
                    ins.then_inc(signal, 1) if signal else link(ins)

                def twice_normed():
                    rsqrt(1, mv[:, :, 1])
                    link(G.tensor_tensor(sm[:, 2, :], sm[:, 1, :], mv[:, :, 1], ALU.mult))
                    link(G.tensor_tensor(sm[:, 2, :], sm[:, 2, :], sm[:, 1, :], ALU.mult))
                    rsqrt(2, sm[:, 2, :])

                def mean_square():
                    link(G.tensor_tensor(sm[:, 0, :], mv[:, :, 0], mv[:, :, 0], ALU.mult))
                    link(G.tensor_tensor(sm[:, 0, :], sm[:, 0, :], mv[:, :, 1], ALU.add))

                bc = lambda t, n=PM: t.rearrange("p (h a) -> p h a", a=1).broadcast_to([P, HM, n])
                pool.wait_ge(S["mv"], 4)
                twice_normed()
                G.tensor_tensor(sm[:, 3, :], sm[:, 1, :], sm[:, 2, :], ALU.mult).then_inc(S["rr"], 1)
                for s in range(2):
                    pool.wait_ge(S["r1"], s + 1)
                    G.tensor_copy(part[:, s, 1, :], rem[:, s, :]).then_inc(S["q2"], 1)
                    pool.wait_ge(S["q2"], s + 1)
                    G.tensor_tensor(part[:, s, 2, :], rem[:, s, :], part[:, s, 1, :], ALU.subtract).then_inc(S["q3"], 1)
                for c in range(NT):
                    pool.wait_ge(S["xtok"], c + 1)
                    G.tensor_tensor(hm(xdt[:, c, :]), hm(xtok[:, c, 0:DI]), bc(dts[:, 7, c * HM:(c + 1) * HM]), ALU.mult).then_inc(S["xdt"], 1)
                    G.tensor_tensor(hm(xskip[:, c, :]), hm(xtok[:, c, 0:DI]), bc(C["dskip"]), ALU.mult).then_inc(S["xskip"], 1)
                    pool.wait_ge(S["xdt"], c + 1)
                    pool.wait_ge(S["lex"], c + 1)
                    G.tensor_tensor(hm(xw[:, c, :]), hm(xdt[:, c, :]), bc(lex[:, c, :, P - 1]), ALU.mult).then_inc(S["xw"], 1)
                for c in range(NT):
                    pool.wait_ge(S["xskip"], c + 1)
                    pool.wait_ge(S["yj"], c + 1)
                    G.tensor_tensor(yg[:, c, :], yg[:, c, :], xskip[:, c, :], ALU.add).then_inc(S["yk"], 1)
                    pool.wait_ge(S["yk"], c + 1)
                    pool.wait_ge(S["zs"], 2)
                    G.tensor_tensor(yg[:, c, :], yg[:, c, :], zs[:, c, :], ALU.mult).then_inc(S["yg"], 1)
                pool.wait_ge(S["mv"], 8)
                mean_square()
                rsqrt(1, sm[:, 0, :], S["yr"])
                pool.wait_ge(S["mv"], 12)
                pool.wait_ge(S["x1"], 4)
                rsqrt(1, mv[:, :, 1], S["rr2"])
                pool.wait_ge(S["un2"], 4)
                G.tensor_tensor(x1[:, :, :], x1[:, :, :], C["mb2"].rearrange("p (a n) -> p a n", a=1).broadcast_to([P, NT, D]), ALU.add).then_inc(S["res2"], 1)
                pool.wait_ge(S["mr"], 1)
                G.tensor_copy(mpart[:, 1, :], mrem).then_inc(S["m2"], 1)
                pool.wait_ge(S["m2"], 1)
                G.tensor_tensor(mpart[:, 2, :], mrem, mpart[:, 1, :], ALU.subtract).then_inc(S["m3"], 1)
                pool.wait_ge(S["mv"], 16)
                mean_square()
                rsqrt(1, sm[:, 0, :], S["rr3"])
                pool.wait_ge(S["mv"], 20)
                twice_normed()
                G.tensor_tensor(sm[:, 3, :], sm[:, 1, :], sm[:, 2, :], ALU.mult).then_inc(S["rr4"], 1)
                pool.wait_ge(S["qkv"], 4)
                G.tensor_tensor(sq[:, :, :], qkv[:, :, 0:2 * D], qkv[:, :, 0:2 * D], ALU.mult).then_inc(S["sq"], 1)
                pool.wait_ge(S["nrm"], 1)
                flat = inv[:, :, :].rearrange("p j h -> p (j h)")
                link(G.tensor_scalar(flat, flat, 1e-24, None, ALU.max))
                half = C["mhalf"][:, 0:1].broadcast_to([P, NT * 2 * HA])
                G.tensor_tensor(flat, flat, half, ALU.pow).then_inc(S["inv"], 1)
                pool.wait_ge(S["inv"], 1)
                for k in range(2):
                    t = qkv[:, :, k * D:(k + 1) * D].rearrange("p j (h d) -> p j h d", d=DH)
                    r = inv[:, :, k * HA:(k + 1) * HA].rearrange("p j (h a) -> p j h a", a=1)
                    G.tensor_tensor(t, t, r.broadcast_to([P, NT, HA, DH]), ALU.mult).then_inc(S["qkn"], 1)
                pass_ends(pool, "pool")



def _tables(i):
    T_ = np.transpose
    row = lambda a: np.broadcast_to(a.reshape(1, -1), (P, a.size))
    col = lambda a: a.reshape(-1, P).T
    r = np.arange(P)
    f = np.float32
    head = r // DH
    cw, cb = i["L0_attn_conv_w"], i["L0_attn_conv_b"]
    bcw = T_(cw[DI:].reshape(2, NS, TAPS), (1, 0, 2)).reshape(NS, 8)
    bcb = cb[DI:].reshape(2, NS).T
    up = lambda w: T_(w, (2, 0, 1)).reshape(P, -1)
    down = lambda w: T_(w.reshape(E, D, -1, P), (3, 0, 2, 1)).reshape(P, -1)
    a = dict(
        ident=np.eye(P, dtype=f), le=(r[:, None] <= r[None, :]).astype(f), gt=(r[:, None] > r[None, :]).astype(f),
        blk=(head[:, None] == head[None, :]).astype(f), iota=row(np.arange(E, dtype=f)),
        mhalf=np.full((P, NT), -0.5, f), ln1w=col(i["L0_attn_ln1_w"]), ln1b=col(i["L0_attn_ln1_b"]),
        winT=i["L0_attn_in_proj_w"].T, cwx=T_(cw[:DI].reshape(2, P, TAPS), (1, 0, 2)).reshape(P, 8),
        cbx=col(cb[:DI]), cwbc=np.concatenate([bcw, bcw]), cbbc=np.concatenate([bcb, bcb]),
        dtb=row(i["L0_attn_dt_bias"]), alog=row(i["L0_attn_A_log"]), dskip=row(i["L0_attn_D"]),
        nw=col(i["L0_attn_norm_w"]), woutT=T_(i["L0_attn_out_proj_w"].reshape(D, 2, P), (2, 1, 0)).reshape(P, -1),
        ln2w=col(i["L0_attn_ln2_w"]), ln2b=col(i["L0_attn_ln2_b"]), mw1T=i["L0_attn_mlp_w1"].T,
        mb1=col(i["L0_attn_mlp_b1"]), mw2T=T_(i["L0_attn_mlp_w2"].reshape(D, 4, P), (2, 1, 0)).reshape(P, -1),
        mb2=row(i["L0_attn_mlp_b2"]), r1w=col(i["L0_ffn_ln1_w"]), r2w=col(i["L0_ffn_ln2_w"]),
        wqT=i["L0_ffn_wq"].T, wkT=i["L0_ffn_wk"].T, wvT=i["L0_ffn_wv"].T, woT=i["L0_ffn_wo"].T,
        gateT=i["L0_ffn_gate_w"].T)
    b = dict(ew1T=up(i["L0_ffn_w1"]), ew3T=up(i["L0_ffn_w3"]), ew2T=down(i["L0_ffn_w2"]))
    c = dict(
        wqkv=np.concatenate([i["L1_attn_Wq"], i["L1_attn_Wk"], i["L1_attn_Wv"]], axis=1),
        bqkv=row(np.concatenate([i["L1_attn_bq"], i["L1_attn_bk"], i["L1_attn_bv"]])), wo1=i["L1_attn_Wo"],
        bo1=row(i["L1_attn_bo"]), mcol=np.repeat(i["L1_attn_m"], DH).reshape(P, 1), centT=i["L1_ffn_centroids"].T,
        lng=i["L1_ffn_ln_g"].T, lnb=i["L1_ffn_ln_b"].T, fb1=T_(i["L1_ffn_b1"].reshape(E * 4, P), (1, 0)),
        fw1T=up(i["L1_ffn_w1"]), fw2T=down(i["L1_ffn_w2"]))
    return [np.ascontiguousarray(np.concatenate([t[k] for k in pack], axis=1))
            for t, pack in ((a, PACK_A), (b, PACK_B), (c, PACK_C))]


def kernel(**inputs):
    import concourse.bacc as bacc
    from concourse.bass_utils import run_bass_kernel_spmd

    i = {k: np.asarray(v) for k, v in inputs.items()}
    pack_a, pack_b, pack_c = _tables(i)
    arrays = {"x": np.ascontiguousarray(i["L0_attn_x"]), "pack_a": pack_a, "pack_b": pack_b, "pack_c": pack_c,
              "b2": np.ascontiguousarray(i["L1_ffn_b2"])}
    nc = bacc.Bacc("TRN2", target_bir_lowering=False, num_devices=1)
    aps = [nc.dram_tensor(k, a.shape, F32, kind="ExternalInput").ap() for k, a in arrays.items()]
    y = nc.dram_tensor("y", (B, T, D), F32, kind="ExternalOutput").ap()
    build(nc, *aps, y)
    r = run_bass_kernel_spmd(nc, [arrays], core_ids=[0])
    return r.results[0]["y"]
```

```python
from contextlib import ExitStack

import numpy as np

import concourse.bass as bass
from concourse import mybir

F32 = mybir.dt.float32
BF16 = mybir.dt.bfloat16
U32 = mybir.dt.uint32
ALU = mybir.AluOpType
ACT = mybir.ActivationFunctionType
AX = mybir.AxisListType

P = 128
B, T, D = 8, 512, 128
NT = T // P
HM, PM, NS, TAPS = 4, 64, 64, 4
DI = HM * PM
DIP = 2 * DI + 2 * NS + HM
MF = 4 * D
HA, DH = 16, 8
E, TOPK = 8, 2
I0, I1 = 256, 512
EPS = 1e-5
PAIRS = [(0, 0), (0, 1), (1, 0), (1, 1), (0, 2), (2, 0)]
KROWS = len(PAIRS) * DH
MROWS = KROWS + 3
HROWS = 64
PREP = 15
GH = 4
NG = HA // GH

PACK_A = dict(ident=P, le=P, gt=P, blk=P, iota=E, mhalf=NT, ln1w=1, ln1b=1, winT=DIP, cwx=8, cbx=2, cwbc=8,
              cbbc=2, dtb=HM, alog=HM, dskip=HM, nw=2, woutT=2 * D, ln2w=1, ln2b=1, mw1T=MF, mb1=NT, mw2T=4 * D,
              mb2=D, r1w=1, r2w=1, wqT=D, wkT=D, wvT=D, woT=D, gateT=E)
PACK_B = dict(ew1T=E * I0, ew3T=E * I0, ew2T=E * 2 * D)
PACK_C = dict(wqkv=3 * D, bqkv=3 * D, wo1=D, bo1=D, mcol=1, centT=E, lng=E, lnb=E, fb1=E * 4, fw1T=E * I1,
              fw2T=E * 4 * D)

SIGNALS = dict(
    bn=20, mv=20, xn=4, un=4, rr=1, tr_un=1, hA=1, hB=1,
    qk_ps=2, v_ps=1, xbc_ps=4, z_ps=2, dt_ps=1, q1=2, r1=2, q2=2, q3=2, vext=1, xbc=4, zs=2, dtraw=1,
    conv=4, xc=4, dtabs=1, dtu=1, adec=1, dt=1, av=4,
    xtr=4, xtok=4, cum_ps=1, ec=1, g_ps=1, gm=1, seg_ps=4, lex=4, wmat=4, xdt=4, xskip=4, xw=4,
    st_ps=3, state=4, y_ps=4, yi=4, yj=4, yk=4, yg=4, yr=1, ytr=1, yT=2, op_ps=1, x1=4,
    rr2=1, un2=4, res2=1, tr_un2=1, h2=1, up_ps=4, gel=4, down_ps=1, s0=1,
    qz=2, mx_ps=64, mx=64, tr_mx=4, m1=4, mr=4, m2=4, m3=4, sc_ps=64, ex=64, pv=16, oc=4, tr_o=4, orec=4, att=4,
    tr_att=1, attT=1,
    wo_ps=1, hb=1,
    rr3=1, un3=4, tr_un3=1, h3=1, lg_ps=1, lg=1, top=8, topi=8, topf=1, tope=1, we=1,
    ea_ps=16, eb_ps=16, sa=16, hid=16, ed_ps=8, eacc=32, g0=1, sg0=1, x2=1,
    rr4=1, xn1=4, un4=4, tr_xn1=1, tr_un4=1, xn1T=1, un4T=1, qkv_ps=4, qkv=4, sq=1, nrm=1, inv=1,
    qkn=2, vk_ps=1, vkm=1, mm_ps=1, mm=1, qT_ps=1, qT=1, o1_ps=1, s1=1,
    af_ps=1, af=1, tpf1=1, tpe1=1, ohs=1, tr_ohs=1, ohT=1, b2_ps=1,
    fu_ps=32, fh=32, fd_ps=8, facc=33, g1=1, sg1=1, out=1,
    pool_chain=20, dve_chain=40,
    x_in=16, y_out=16, qk_store=32, qk_load=16 * 24, m_store=16 * 4, m_load=32 * 4)


def build(nc, x, pack_a, pack_b, pack_c, b2, out):
    with ExitStack() as ctx:
        def sb(name, shape, dt=F32):
            return ctx.enter_context(nc.sbuf_tensor(name, shape, dt))

        S = {name: ctx.enter_context(nc.semaphore(name)) for name in SIGNALS}
        done = ctx.enter_context(nc.semaphore("pass_done"))
        ENGINES = ("pe", "act", "dve", "pool")
        go = {k: ctx.enter_context(nc.semaphore("go_" + k)) for k in ENGINES}
        ids = sorted(x.num for x in S.values())
        assert ids == list(range(ids[0], ids[-1] + 1))

        def pass_ends(eng, name):
            eng.drain().then_inc(done, 1)
            eng.wait_ge(go[name], 1)
            eng.sem_clear(go[name])

        s_load = ctx.enter_context(nc.semaphore("tables_loaded"))
        s_set = {k: ctx.enter_context(nc.semaphore("setup_" + k)) for k in
                 ("prep", "sig", "exps", "scal", "bias_ps")}

        tabs, cols = [], {}
        for name, pack in (("tab_a", PACK_A), ("tab_b", PACK_B), ("tab_c", PACK_C)):
            tab = sb(name, [P, sum(pack.values())])
            tabs.append(tab)
            at = 0
            for k, n in pack.items():
                cols[k] = tab[:, at:at + n]
                at += n
        C = cols
        ident = C["ident"]
        b2t = sb("b2t", [E, D])
        ones = sb("ones", [P, P])
        negA = sb("negA", [P, HM])
        msc = sb("msc", [P, P])
        mtmp = sb("mtmp", [P, 4])
        bias1 = sb("bias1", [P, E * 4])

        xin = sb("xin", [P, NT, D])
        xn = sb("xn", [P, NT, D])
        un = sb("un", [P, NT, D])
        hA = sb("hA", [P, T])
        hB = sb("hB", [P, T])
        bst = sb("bst", [P, NT, 6])
        mv = sb("mv", [P, NT, 2])
        sm = sb("sm", [P, 8, NT])
        part = sb("part", [P, 2, 3, T], BF16)
        rem = sb("rem", [P, 2, T])
        qx = sb("qx", [P, HA // 2, T], BF16)
        kx = sb("kx", [P, HA // 2, T], BF16)
        vext = sb("vext", [P, NT, HA, 32])
        mx = sb("mx", [P, NT, HA])
        mpart = sb("mpart", [GH, 3, T], BF16)
        mrem = rem[0:GH, 0, :]
        pr = sb("pr", [P, 8, T])
        oc = sb("oc", [P, T])
        orec = sb("orec", [P, NT, GH])
        att = sb("att", [P, NT, D])
        attT = sb("attT", [P, T])
        hb = sb("hb", [P, NT, D])
        xbc = sb("xbc", [P, 4, T + TAPS - 1])
        fh = pr
        xc = fh[:, 0:4, :]
        wide8 = sb("wide8", [P, 8, T])
        quarter = lambda k: wide8[:, 2 * k:2 * k + 2, :].rearrange("p a (b n) -> p (a b) n", n=DI)
        zs, xskip, xw, yg = quarter(0), quarter(1), quarter(2), quarter(3)
        dts = sb("dts", [P, 8, NT * HM])
        av = fh[:, 4:8, :].rearrange("p c (h t) -> p c h t", h=HM)
        xtok = sb("xtok", [P, NT, DI + NS])
        ec = sb("ec", [P, NT, 2 * HM])
        gm = sb("gm", [P, NT, P])
        lex = sb("lex", [P, NT, HM, P])
        xdt = sb("xdt", [P, NT, DI])
        state = sb("state", [NS, NT + 1, DI])
        stmp = sb("stmp", [NS, DI])
        yT = sb("yT", [P, 2, T])
        x1 = sb("x1", [P, NT, D])
        h2 = sb("h2", [P, T])
        gel = lex[:, :, :, :].rearrange("p c h t -> p c (h t)")
        s0 = x1
        h3 = hB
        lg = sb("lg", [P, NT, E])
        top = sb("top", [P, NT, 8])
        topi = sb("topi", [P, NT, 8], U32)
        topf = sb("topf", [P, NT, 8])
        tw = sb("tw", [P, 6, NT])
        oh = sb("oh", [P, 2, NT, E])
        we = sb("we", [P, NT, E])
        hid = wide8[:, 0:4, :]
        sa = wide8[:, 4:7, :]
        g0 = attT[:, :].rearrange("p (j d) -> p j d", j=NT)
        x2 = hb
        xn1T, un4T = h2, hA
        qkv = gel[:, 0:3, :].rearrange("p a n -> p (a n)").rearrange("p (j n) -> p j n", j=NT)
        sq = xdt
        inv = sb("inv", [P, NT, 2 * HA])
        vkm, mm = gm[:, 0, :], gm[:, 1, :]
        qT = yT[:, 0, :]
        ohT = yT[0:E, 1, :]
        s1 = att
        PS = [ctx.enter_context(nc.psum_tensor(f"ps{i}", [P, 512], F32)) for i in range(8)]

        qk_dram = nc.dram_tensor("qk_scratch", [2, 3, P, T], BF16, kind="Internal").ap()
        m_dram = nc.dram_tensor("m_scratch", [3, HA, T], BF16, kind="Internal").ap()

        MX_RING = [5, 6]
        SC_RING = [0, 1, 2, 7]
        hm = lambda t: t.rearrange("p (h q) -> p h q", h=HM)
        tk = lambda t: t.rearrange("p (j n) -> p j n", j=NT)
        block = ctx.enter_context(nc.Block())

        @block.sync
        def _(sp):
            sp.dma_start(tabs[0][:, :], pack_a).then_inc(s_load, 16)
            sp.dma_start(tabs[2][:, :], pack_c).then_inc(s_load, 16)
            sp.dma_start(tabs[1][:, :], pack_b).then_inc(s_load, 16)
            sp.dma_start(b2t[:, :], b2).then_inc(s_load, 16)
            with sp.Fori(0, B) as it:
                sp.dma_start(xin[:, :, :], x[bass.ds(it, 1)].rearrange("a (j p) d -> p (a j) d", p=P)).then_inc(S["x_in"], 16)
                for s in range(2):
                    sp.wait_ge(S["q3"], s + 1)
                    sp.dma_start(qk_dram[s].rearrange("a p t -> p a t"), part[:, s, :, :]).then_inc(S["qk_store"], 16)
                sp.wait_ge(S["qz"], 2)
                for s in range(2):
                    sp.wait_ge(S["qk_store"], 32)
                    src = qk_dram[s].rearrange("a (g s d) t -> a s d g t", s=2, d=DH)
                    dst = (qx, kx)[s]
                    for j, pair in enumerate(PAIRS):
                        for h in range(2):
                            sp.dma_start(dst[64 * h + DH * j:64 * h + DH * (j + 1), :, :], src[pair[s], h]).then_inc(S["qk_load"], 16)
                for g in range(NG):
                    sp.wait_ge(S["m3"], g + 1)
                    sp.dma_start(m_dram[:, GH * g:GH * g + GH].rearrange("a h t -> h a t"),
                                 mpart[:, :, :]).then_inc(S["m_store"], 16)
                    sp.wait_ge(S["m_store"], 16 * (g + 1))
                    if g:
                        sp.wait_ge(S["m_load"], 32 * g)
                    for h in range(2):
                        sp.dma_start(qx[64 * h + KROWS:64 * h + MROWS, 2 * g:2 * g + 2, :],
                                     m_dram[:, GH * g:GH * g + GH].rearrange("a (g s) t -> s a g t", s=2)[h]
                                     ).then_inc(S["m_load"], 16)
                sp.wait_ge(S["out"], 1)
                sp.dma_start(out[bass.ds(it, 1)].rearrange("a (j p) d -> p (a j) d", p=P), xn[:, :, :]).then_inc(S["y_out"], 16)
                sp.wait_ge(S["y_out"], 16)
                sp.wait_ge(done, len(ENGINES))
                sp.sem_clear(done)
                sp.sem_clear(range(ids[0], ids[-1] + 1))
                for k in ENGINES:
                    sp.sem_inc(go[k], 1)

        @block.tensor
        def _(pe):
            mmul = nc.tensor.matmul

            def turn(bank, src, width=D, rows=P, upto=NT):
                for j in range(upto):
                    last = nc.tensor.transpose(PS[bank][0:width, j * P:(j + 1) * P], src[:, j, :], ident)
                return last

            pe.wait_ge(s_load, 64)
            for e in range(E):
                for c in range(4):
                    n = e * 4 + c
                    ins = mmul(PS[0][:, n:n + 1], C["fw1T"][:, e * I1 + c * P:e * I1 + (c + 1) * P],
                               C["lnb"][:, e:e + 1], start=True, stop=True)
            ins.then_inc(s_set["bias_ps"], 1)
            pe.wait_ge(s_set["prep"], PREP)

            with pe.Fori(0, B) as it:
                pe.wait_ge(S["un"], 4)
                turn(0, un).then_inc(S["tr_un"], 1)
                pe.wait_ge(S["hB"], 1)
                mmul(PS[1][:, :], C["wqT"], hB[:, :], start=True, stop=True).then_inc(S["qk_ps"], 1)
                mmul(PS[2][:, :], C["wkT"], hB[:, :], start=True, stop=True).then_inc(S["qk_ps"], 1)
                for j in range(NT):
                    ins = mmul(PS[3][:, j * D:(j + 1) * D], hB[:, j * P:(j + 1) * P], C["wvT"], start=True, stop=True)
                ins.then_inc(S["v_ps"], 1)
                pe.wait_ge(S["hA"], 1)
                for c, (a, n) in enumerate([(DI, P), (DI + P, P), (2 * DI, NS), (2 * DI + NS, NS)]):
                    mmul(PS[4 + c][0:n, :], C["winT"][:, a:a + n], hA[:, :], start=True, stop=True).then_inc(S["xbc_ps"], 1)
                pe.wait_ge(S["r1"], 1)
                for j in range(NT):
                    ins = mmul(PS[1][:, j * HM:(j + 1) * HM], hA[:, j * P:(j + 1) * P], C["winT"][:, DIP - HM:DIP],
                               start=True, stop=True)
                ins.then_inc(S["dt_ps"], 1)
                for k, bank in enumerate((0, 3)):
                    if k == 1:
                        pe.wait_ge(S["vext"], 1)
                    for j in range(2):
                        ins = mmul(PS[bank][:, j * DI:(j + 1) * DI], hA[:, (2 * k + j) * P:(2 * k + j + 1) * P],
                                   C["winT"][:, 0:DI], start=True, stop=True)
                    ins.then_inc(S["z_ps"], 1)
                pe.wait_ge(S["adec"], 1)
                pe.wait_ge(S["r1"], 2)
                for c in range(NT):
                    a = dts[:, 6, c * HM:(c + 1) * HM]
                    mmul(PS[2][:, c * 8:c * 8 + 4], C["le"], a, start=True, stop=True)
                    ins = mmul(PS[2][:, c * 8 + 4:c * 8 + 8], ones[:, :], a, start=True, stop=True)
                ins.then_inc(S["cum_ps"], 1)
                for c in range(NT):
                    pe.wait_ge(S["av"], c + 1)
                    if c == 0:
                        pe.wait_ge(S["dtraw"], 1)
                    elif c == 1:
                        pe.wait_ge(S["zs"], 2)
                    else:
                        pe.wait_ge(S["lex"], c - 1)
                    mmul(PS[(1, 3)[c % 2]][:, :], C["gt"], av[:, c, :, :], start=True, stop=True).then_inc(S["seg_ps"], 1)
                pe.wait_ge(S["xc"], 4)
                pe.wait_ge(S["zs"], 1)
                for c in range(NT):
                    ins = mmul(PS[0][:, c * P:(c + 1) * P], xc[0:NS, 2, c * P:(c + 1) * P],
                               xc[0:NS, 3, c * P:(c + 1) * P], start=True, stop=True)
                ins.then_inc(S["g_ps"], 1)
                for c in range(NT):
                    pe.wait_ge(S["xbc"], c + 1)
                    for k in range(2):
                        nc.tensor.transpose(PS[4 + c][:, k * P:(k + 1) * P], xc[:, k, c * P:(c + 1) * P], ident)
                    nc.tensor.transpose(PS[4 + c][:, DI:DI + NS], xc[0:NS, 2, c * P:(c + 1) * P], C["ident"][0:NS, 0:NS]).then_inc(S["xtr"], 1)
                for c in range(NT - 1):
                    pe.wait_ge(S["xtok"], c + 1)
                    pe.wait_ge(S["xw"], c + 1)
                    mmul(PS[4 + c][0:NS, 0:DI], xtok[:, c, DI:DI + NS], xw[:, c, :], start=True, stop=True).then_inc(S["st_ps"], 1)
                pe.wait_ge(S["gm"], 1)
                pe.wait_ge(S["ec"], 1)
                for c in range(NT):
                    pe.wait_ge(S["wmat"], c + 1)
                    pe.wait_ge(S["xdt"], c + 1)
                    if c in (1, 3):
                        pe.wait_ge(S["lex"], 3 + c // 2)
                    for h in range(HM):
                        mmul(PS[c][:, h * PM:(h + 1) * PM], av[:, c, h, :], xdt[:, c, h * PM:(h + 1) * PM],
                             start=True, stop=True)
                    pe.wait_ge(S["state"], c + 1)
                    mmul(PS[c][:, DI:2 * DI], xc[0:NS, 3, c * P:(c + 1) * P], state[:, c, :], start=True, stop=True).then_inc(S["y_ps"], 1)
                pe.wait_ge(S["state"], 4)
                pe.wait_ge(S["xtok"], 4)
                for j in range(NT):
                    pe.wait_ge(S["yg"], j + 1)
                    for k in range(2):
                        ins = nc.tensor.transpose(PS[4 + k][:, j * P:(j + 1) * P], yg[:, j, k * P:(k + 1) * P], ident)
                ins.then_inc(S["ytr"], 1)
                pe.wait_ge(S["yT"], 2)
                for j in range(NT):
                    for k in range(2):
                        ins = mmul(PS[6][:, j * D:(j + 1) * D], yT[:, k, j * P:(j + 1) * P],
                                   C["woutT"][:, k * D:(k + 1) * D], start=(k == 0), stop=(k == 1))
                ins.then_inc(S["op_ps"], 1)
                pe.wait_ge(S["un2"], 4)
                turn(7, un).then_inc(S["tr_un2"], 1)
                pe.wait_ge(S["h2"], 1)
                pe.wait_ge(S["yj"], 4)
                for c in range(4):
                    mmul(PS[c][:, :], C["mw1T"][:, c * P:(c + 1) * P], h2[:, :], start=True, stop=True).then_inc(S["up_ps"], 1)
                pe.wait_ge(S["gel"], 4)
                for j in range(NT):
                    for c in range(4):
                        ins = mmul(PS[4][:, j * D:(j + 1) * D], gel[:, c, j * P:(j + 1) * P],
                                   C["mw2T"][:, c * D:(c + 1) * D], start=(c == 0), stop=(c == 3))
                ins.then_inc(S["down_ps"], 1)
                def max_scores(n, count):
                    for u in range(n, n + count):
                        h, j = divmod(u, NT)
                        a = HROWS * (h % 2)
                        if u >= 2:
                            pe.wait_ge(S["mx"], u - 1)
                        mmul(PS[MX_RING[u % 2]][:, :], qx[a:a + HROWS, h // 2, j * P:(j + 1) * P],
                             kx[a:a + HROWS, h // 2, :], start=True, stop=True).then_inc(S["mx_ps"], 1)

                def turn_max(g):
                    pe.wait_ge(S["mx"], 16 * (g + 1))
                    if g:
                        pe.wait_ge(S["mr"], g)
                    if g >= 3:
                        pe.wait_ge(S["att"], g - 2)
                    for j in range(NT):
                        ins = nc.tensor.transpose(PS[4][0:GH, j * P:(j + 1) * P], mx[:, j, GH * g:GH * g + GH], ident)
                    ins.then_inc(S["tr_mx"], 1)

                def score(u, i):
                    g, k = divmod(u, NT)
                    h, n = GH * g + i, GH * u + i
                    a = HROWS * (h % 2)
                    if k == 0 and i == 0:
                        pe.wait_ge(S["m_load"], 32 * (g + 1))
                    if n >= 4:
                        pe.wait_ge(S["ex"], n - 3)
                    mmul(PS[SC_RING[n % 4]][:, :], kx[a:a + HROWS, h // 2, k * P:(k + 1) * P],
                         qx[a:a + HROWS, h // 2, :], start=True, stop=True).then_inc(S["sc_ps"], 1)

                def values(u):
                    g, k = divmod(u, NT)
                    pe.wait_ge(S["ex"], GH * (u + 1))
                    if k == 0 and g:
                        pe.wait_ge(S["oc"], g)
                    for i in range(GH):
                        ins = mmul(PS[3][32 * i:32 * i + 32, :], vext[:, k, GH * g + i, :], pr[:, GH * (u % 2) + i, :],
                                   start=(k == 0), stop=(k == NT - 1))
                    ins.then_inc(S["pv"], 1)

                def turn_out(g):
                    pe.wait_ge(S["oc"], g + 1)
                    if g:
                        pe.wait_ge(S["att"], g)
                    if g < 2:
                        pe.wait_ge(S["mr"], g + 3)
                    for j in range(NT):
                        ins = nc.tensor.transpose(PS[4][:, j * P:(j + 1) * P], oc[:, j * P:(j + 1) * P], ident)
                    ins.then_inc(S["tr_o"], 1)

                pe.wait_ge(S["qk_load"], 384)
                pe.wait_ge(S["s0"], 1)
                for g in range(2):
                    max_scores(16 * g, 16)
                    turn_max(g)
                for i in range(GH):
                    score(0, i)
                for u in range(4 * NG):
                    if u in (4, 8):
                        turn_max(u // 4 + 1)
                    for i in range(GH):
                        if u < 4 * NG - 1:
                            score(u + 1, i)
                        if u < 8:
                            max_scores(32 + 4 * u + i, 1)
                    values(u)
                    if u >= 5 and u % 4 == 1:
                        turn_out(u // 4 - 1)
                turn_out(NG - 1)
                pe.wait_ge(S["att"], 4)
                turn(3, att).then_inc(S["tr_att"], 1)
                pe.wait_ge(S["attT"], 1)
                pe.wait_ge(S["s0"], 1)
                for j in range(NT):
                    ins = mmul(PS[4][:, j * D:(j + 1) * D], attT[:, j * P:(j + 1) * P], C["woT"], start=True, stop=True)
                ins.then_inc(S["wo_ps"], 1)
                pe.wait_ge(S["un3"], 4)
                turn(0, un).then_inc(S["tr_un3"], 1)
                pe.wait_ge(S["h3"], 1)
                for j in range(NT):
                    ins = mmul(PS[1][:, j * E:(j + 1) * E], h3[:, j * P:(j + 1) * P], C["gateT"], start=True, stop=True)
                ins.then_inc(S["lg_ps"], 1)
                pe.wait_ge(S["lg"], 1)

                def expert_up(u):
                    pair = u % 3
                    if u >= 3:
                        pe.wait_ge(S["hid"], u - 2)
                    mmul(PS[2 * pair][:, :], C["ew1T"][:, u * P:(u + 1) * P], h3[:, :], start=True, stop=True).then_inc(S["ea_ps"], 1)
                    mmul(PS[2 * pair + 1][:, :], C["ew3T"][:, u * P:(u + 1) * P], h3[:, :], start=True, stop=True).then_inc(S["eb_ps"], 1)

                def expert_down(e):
                    pe.wait_ge(S["hid"], 2 * e + 2)
                    if e >= 2:
                        pe.wait_ge(S["eacc"], 4 * (e - 1))
                    for j in range(NT):
                        for c in range(2):
                            u = 2 * e + c
                            ins = mmul(PS[6 + e % 2][:, j * D:(j + 1) * D], hid[:, u % 4, j * P:(j + 1) * P],
                                       C["ew2T"][:, u * D:(u + 1) * D], start=(c == 0), stop=(c == 1))
                    ins.then_inc(S["ed_ps"], 1)

                pe.wait_ge(S["hb"], 1)
                for e in range(E):
                    expert_up(2 * e)
                    if e:
                        expert_down(e - 1)
                    expert_up(2 * e + 1)
                expert_down(E - 1)
                pe.wait_ge(S["xn1"], 4)
                pe.wait_ge(S["hid"], 16)
                turn(0, xn).then_inc(S["tr_xn1"], 1)
                pe.wait_ge(S["un4"], 4)
                turn(1, un).then_inc(S["tr_un4"], 1)
                pe.wait_ge(S["xn1T"], 1)
                for j in range(NT):
                    mmul(PS[2 + j][:, 0:3 * D], xn1T[:, j * P:(j + 1) * P], C["wqkv"], start=True, stop=True).then_inc(S["qkv_ps"], 1)
                for j in range(NT):
                    ins = mmul(PS[0][:, j * E:(j + 1) * E], xn1T[:, j * P:(j + 1) * P], C["centT"],
                               start=True, stop=True)
                ins.then_inc(S["af_ps"], 1)
                pe.wait_ge(S["qkn"], 2)
                pe.wait_ge(S["eacc"], 32)
                for j in range(NT):
                    ins = mmul(PS[6][:, 0:P], qkv[:, j, 2 * D:3 * D], qkv[:, j, D:2 * D], start=(j == 0),
                               stop=(j == NT - 1))
                ins.then_inc(S["vk_ps"], 1)
                turn(2, qkv[:, :, 0:D]).then_inc(S["qT_ps"], 1)
                pe.wait_ge(S["vkm"], 1)
                mmul(PS[7][:, 0:P], vkm, C["wo1"], start=True, stop=True).then_inc(S["mm_ps"], 1)
                pe.wait_ge(S["ohs"], 1)
                pe.wait_ge(S["un4T"], 1)
                for j in range(NT):
                    ins = nc.tensor.transpose(PS[1][0:E, j * P:(j + 1) * P], we[:, j, :], ident)
                ins.then_inc(S["tr_ohs"], 1)
                pe.wait_ge(S["mm"], 1)
                pe.wait_ge(S["qT"], 1)
                for j in range(NT):
                    ins = mmul(PS[3][:, j * D:(j + 1) * D], qT[:, j * P:(j + 1) * P], mm, start=True, stop=True)
                ins.then_inc(S["o1_ps"], 1)
                pe.wait_ge(S["ohT"], 1)
                for j in range(NT):
                    ins = mmul(PS[4][:, j * D:(j + 1) * D], ohT[:, j * P:(j + 1) * P], b2t[:, :], start=True, stop=True)
                ins.then_inc(S["b2_ps"], 1)

                def ffn_up(u):
                    if u >= 6:
                        pe.wait_ge(S["fh"], u - 5)
                    mmul(PS[u % 6][:, :], C["fw1T"][:, u * P:(u + 1) * P], un4T[:, :], start=True, stop=True).then_inc(S["fu_ps"], 1)

                def ffn_down(e):
                    pe.wait_ge(S["fh"], 4 * e + 4)
                    if e >= 2:
                        pe.wait_ge(S["facc"], 4 * (e - 1) + 1)
                    for j in range(NT):
                        for c in range(4):
                            u = 4 * e + c
                            ins = mmul(PS[6 + e % 2][:, j * D:(j + 1) * D], fh[:, u % 8, j * P:(j + 1) * P],
                                       C["fw2T"][:, u * D:(u + 1) * D], start=(c == 0), stop=(c == 3))
                    ins.then_inc(S["fd_ps"], 1)

                pe.wait_ge(S["s1"], 1)
                pe.wait_ge(S["facc"], 1)
                for e in range(E):
                    for c in range(2):
                        ffn_up(4 * e + c)
                    if e:
                        ffn_down(e - 1)
                    for c in range(2, 4):
                        ffn_up(4 * e + c)
                ffn_down(E - 1)
                pass_ends(pe, "pe")

        @block.scalar
        def _(act):
            A = nc.scalar.activation
            act.wait_ge(s_load, 64)
            A(mtmp[:, 0:1], C["mcol"], ACT.Exp, scale=-1.0).then_inc(s_set["exps"], 1)
            A(negA[:, :], C["alog"], ACT.Exp).then_inc(s_set["exps"], 1)
            act.wait_ge(s_set["sig"], 2)
            A(mtmp[:, 3:4], mtmp[:, 2:3], ACT.Exp, scale=-float(np.log(T))).then_inc(s_set["scal"], 1)
            with act.Fori(0, B) as it:
                act.wait_ge(S["hA"], 1)
                A(hB[:, :], PS[0][:, :], ACT.Copy, scale=C["r1w"]).then_inc(S["hB"], 1)
                for s in range(2):
                    act.wait_ge(S["qk_ps"], s + 1)
                    A(part[:, s, 0, :], PS[1 + s][:, :], ACT.Copy).then_inc(S["q1"], 1)
                act.wait_ge(S["v_ps"], 1)
                A(vext[:, :, :, 0:DH], PS[3][:, :].rearrange("p (j h d) -> p j h d", j=NT, h=HA), ACT.Copy).then_inc(S["vext"], 1)
                for c in range(4):
                    n = P if c < 2 else NS
                    act.wait_ge(S["xbc_ps"], c + 1)
                    A(xbc[0:n, c, TAPS - 1:], PS[4 + c][0:n, :], ACT.Copy).then_inc(S["xbc"], 1)
                act.wait_ge(S["dtabs"], 1)
                A(dts[:, 2, :], dts[:, 1, :], ACT.Exp, scale=-1.0).then_inc(S["dtu"], 1)
                for k in range(2):
                    act.wait_ge(S["z_ps"], k + 1)
                    A(zs[:, 2 * k:2 * k + 2, :], PS[(0, 3)[k]][:, :].rearrange("p (j n) -> p j n", j=2), ACT.Silu).then_inc(S["zs"], 1)
                for c in range(4):
                    n = P if c < 2 else NS
                    act.wait_ge(S["conv"], c + 1)
                    A(xc[0:n, c, :], xc[0:n, c, :], ACT.Silu).then_inc(S["xc"], 1)
                act.wait_ge(S["cum_ps"], 1)
                A(ec[:, :, :], PS[2][:, 0:NT * 8].rearrange("p (c n) -> p c n", c=NT), ACT.Exp).then_inc(S["ec"], 1)
                for c in range(NT):
                    act.wait_ge(S["seg_ps"], c + 1)
                    A(lex[:, c, :, :], hm(PS[(1, 3)[c % 2]][:, :]), ACT.Exp).then_inc(S["lex"], 1)
                for c in range(NT):
                    act.wait_ge(S["xtr"], c + 1)
                    A(xtok[:, c, :], PS[4 + c][:, 0:DI + NS], ACT.Copy).then_inc(S["xtok"], 1)
                act.wait_ge(S["ytr"], 1)
                for k in range(2):
                    A(yT[:, k, :], PS[4 + k][:, :], ACT.Copy, scale=C["nw"][:, k:k + 1]).then_inc(S["yT"], 1)
                for c in range(4):
                    act.wait_ge(S["up_ps"], c + 1)
                    A(gel[:, c, :], PS[c][:, :], ACT.Gelu, bias=C["mb1"][:, c:c + 1]).then_inc(S["gel"], 1)
                def first_part(g):
                    act.wait_ge(S["tr_mx"], g + 1)
                    if g:
                        act.wait_ge(S["m_store"], 16 * g)
                    A(mpart[:, 0, :], PS[4][0:GH, :], ACT.Copy, scale=-1.0).then_inc(S["m1"], 1)

                for g in range(2):
                    first_part(g)
                for u in range(4 * NG):
                    if u in (5, 9):
                        first_part((u - 1) // 4 + 1)
                    for i in range(GH):
                        n = GH * u + i
                        act.wait_ge(S["sc_ps"], n + 1)
                        if u >= 2 and i == 0:
                            act.wait_ge(S["pv"], u - 1)
                        A(pr[:, GH * (u % 2) + i, :], PS[SC_RING[n % 4]][:, :], ACT.Exp,
                          scale=float(DH) ** -0.5).then_inc(S["ex"], 1)
                    if u >= 4 and u % 4 == 0:
                        act.wait_ge(S["pv"], u)
                        if u > 4:
                            act.wait_ge(S["tr_o"], u // 4 - 1)
                        A(oc[:, :], PS[3][:, :], ACT.Copy).then_inc(S["oc"], 1)
                act.wait_ge(S["pv"], 4 * NG)
                act.wait_ge(S["tr_o"], NG - 1)
                A(oc[:, :], PS[3][:, :], ACT.Copy).then_inc(S["oc"], 1)
                act.wait_ge(S["tr_att"], 1)
                A(attT[:, :], PS[3][:, :], ACT.Copy).then_inc(S["attT"], 1)
                act.wait_ge(S["tr_un3"], 1)
                A(h3[:, :], PS[0][:, :], ACT.Copy, scale=C["r2w"]).then_inc(S["h3"], 1)
                act.wait_ge(S["topf"], 1)
                A(tw[:, 1, :], tw[:, 0, :], ACT.Exp).then_inc(S["tope"], 1)
                for u in range(16):
                    act.wait_ge(S["ea_ps"], u + 1)
                    if u >= 3:
                        act.wait_ge(S["hid"], u - 2)
                    A(sa[:, u % 3, :], PS[2 * (u % 3)][:, :], ACT.Silu).then_inc(S["sa"], 1)
                act.wait_ge(S["eacc"], 32)
                A(g0[:, :, :], hb[:, :, :], ACT.Silu).then_inc(S["g0"], 1)
                act.wait_ge(S["tr_xn1"], 1)
                A(xn1T[:, :], PS[0][:, :], ACT.Copy).then_inc(S["xn1T"], 1)
                act.wait_ge(S["tpf1"], 1)
                A(tw[:, 1, :], tw[:, 0, :], ACT.Exp, scale=-1.0).then_inc(S["tpe1"], 1)
                act.wait_ge(S["qT_ps"], 1)
                A(qT, PS[2][:, :], ACT.Copy).then_inc(S["qT"], 1)
                act.wait_ge(S["mm_ps"], 1)
                A(mm, PS[7][:, 0:P], ACT.Copy).then_inc(S["mm"], 1)
                act.wait_ge(S["tr_ohs"], 1)
                A(ohT, PS[1][0:E, :], ACT.Copy).then_inc(S["ohT"], 1)
                for u in range(32):
                    act.wait_ge(S["fu_ps"], u + 1)
                    if u >= 8:
                        act.wait_ge(S["fd_ps"], u // 4 - 1)
                    A(fh[:, u % 8, :], PS[u % 6][:, :], ACT.Relu, bias=bias1[:, u:u + 1]).then_inc(S["fh"], 1)
                act.wait_ge(S["facc"], 33)
                A(g0[:, :, :], x1[:, :, :], ACT.Silu).then_inc(S["g1"], 1)
                pass_ends(act, "act")

        @block.vector
        def _(dve):
            V = nc.vector
            V.memset(ones[:, :], 1.0).then_inc(s_set["prep"], 1)
            V.memset(xbc[:, :, 0:TAPS - 1], 0.0)
            V.memset(vext[:, :, :, DH:DH + 1], 1.0)
            V.memset(vext[:, :, :, DH + 1:], 0.0)
            V.memset(state[:, 0, :], 0.0).then_inc(s_set["prep"], 1)
            V.memset(kx[32:64, :, :], 1.0).then_inc(s_set["prep"], 1)
            V.memset(kx[96:128, :, :], 1.0).then_inc(s_set["prep"], 1)
            dve.wait_ge(s_load, 64)
            dve.wait_ge(s_set["exps"], 2)
            V.tensor_scalar(negA[:, :], negA[:, :], -1.0, None, ALU.mult).then_inc(s_set["prep"], 1)
            V.tensor_scalar(mtmp[:, 1:2], mtmp[:, 0:1], 1.0, None, ALU.add).then_inc(s_set["sig"], 1)
            dve.wait_ge(s_set["sig"], 1)
            V.reciprocal(mtmp[:, 2:3], mtmp[:, 1:2]).then_inc(s_set["sig"], 1)
            dve.wait_ge(s_set["scal"], 1)
            V.tensor_scalar(msc[:, :], C["blk"], mtmp[:, 3:4], None, ALU.mult).then_inc(s_set["prep"], 1)
            dve.wait_ge(s_set["bias_ps"], 1)
            V.tensor_tensor(bias1[:, :], PS[0][:, 0:E * 4], C["fb1"], ALU.add).then_inc(s_set["prep"], 1)
            for e in range(E):
                w = C["fw1T"][:, e * I1:(e + 1) * I1]
                V.tensor_scalar(w, w, C["lng"][:, e:e + 1], None, ALU.mult).then_inc(s_set["prep"], 1)
            dve.wait_ge(s_set["prep"], PREP)

            with dve.Fori(0, B) as it:
                links = [0]

                def link(ins):
                    ins.then_inc(S["dve_chain"], 1)
                    links[0] += 1
                    dve.wait_ge(S["dve_chain"], links[0])

                def stats(src, n):
                    for j in range(NT):
                        V.bn_stats(bst[:, j, :], src(j)).then_inc(S["bn"], 1)
                    for j in range(NT):
                        dve.wait_ge(S["bn"], n * NT + j + 1)
                        V.bn_aggr(mv[:, j, :], bst[:, j, :]).then_inc(S["mv"], 1)

                dve.wait_ge(S["x_in"], 16)
                stats(lambda j: xin[:, j, :], 0)
                dve.wait_ge(S["rr"], 1)
                for j in range(NT):
                    V.tensor_scalar(un[:, j, :], xin[:, j, :], mv[:, j, 0:1], sm[:, 3, j:j + 1], ALU.subtract, ALU.mult).then_inc(S["un"], 1)
                for j in range(NT):
                    V.tensor_scalar(xn[:, j, :], xin[:, j, :], mv[:, j, 0:1], sm[:, 1, j:j + 1], ALU.subtract, ALU.mult).then_inc(S["xn"], 1)
                dve.wait_ge(S["tr_un"], 1)
                V.tensor_scalar(hA[:, :], PS[0][:, :], C["ln1w"], C["ln1b"], ALU.mult, ALU.add).then_inc(S["hA"], 1)
                for s in range(2):
                    dve.wait_ge(S["q1"], s + 1)
                    V.tensor_tensor(rem[:, s, :], PS[1 + s][:, :], part[:, s, 0, :], ALU.subtract).then_inc(S["r1"], 1)
                dve.wait_ge(S["dt_ps"], 1)
                bc = lambda t, n=NT: t.rearrange("p (a h) -> p a h", a=1).broadcast_to([P, n, t.shape[1]])
                t4 = lambda k: dts[:, k, :].rearrange("p (j h) -> p j h", j=NT)
                V.tensor_tensor(t4(0), PS[1][:, 0:NT * HM].rearrange("p (j h) -> p j h", j=NT), bc(C["dtb"]), ALU.add).then_inc(S["dtraw"], 1)
                dve.wait_ge(S["dtraw"], 1)
                V.scalar_tensor_tensor(dts[:, 1, :], dts[:, 0, :], -1.0, dts[:, 0, :], ALU.mult, ALU.max).then_inc(S["dtabs"], 1)
                for c in range(4):
                    n = P if c < 2 else NS
                    w = C["cwx"][:, c * 4:c * 4 + 4] if c < 2 else C["cwbc"][0:NS, (c - 2) * 4:(c - 2) * 4 + 4]
                    b = C["cbx"][:, c:c + 1] if c < 2 else C["cbbc"][0:NS, c - 2:c - 1]
                    dve.wait_ge(S["xbc"], c + 1)
                    link(V.tensor_scalar(xc[0:n, c, :], xbc[0:n, c, 0:T], w[:, 0:1], b, ALU.mult, ALU.add))
                    for k in range(1, TAPS):
                        ins = V.scalar_tensor_tensor(xc[0:n, c, :], xbc[0:n, c, k:k + T], w[:, k:k + 1], xc[0:n, c, :],
                                                     ALU.mult, ALU.add)
                        if k < TAPS - 1:
                            link(ins)
                        else:
                            ins.then_inc(S["conv"], 1)
                dve.wait_ge(S["dtu"], 1)
                link(V.tensor_scalar(dts[:, 3, :], dts[:, 2, :], 2.0, None, ALU.add))
                link(V.reciprocal(dts[:, 4, :], dts[:, 3, :]))
                link(V.tensor_tensor(dts[:, 3, :], dts[:, 2, :], dts[:, 4, :], ALU.mult))
                link(V.tensor_tensor(dts[:, 4, :], dts[:, 3, :], dts[:, 3, :], ALU.mult))
                link(V.tensor_scalar(dts[:, 5, :], dts[:, 4, :], 1.0 / 15, None, ALU.mult))
                for k in (13, 11, 9, 7, 5, 3):
                    link(V.scalar_tensor_tensor(dts[:, 5, :], dts[:, 5, :], 1.0 / k, dts[:, 4, :], ALU.add, ALU.mult))
                link(V.tensor_scalar(dts[:, 5, :], dts[:, 5, :], 1.0, 2.0, ALU.add, ALU.mult))
                link(V.tensor_tensor(dts[:, 5, :], dts[:, 5, :], dts[:, 3, :], ALU.mult))
                V.scalar_tensor_tensor(dts[:, 7, :], dts[:, 0, :], 0.0, dts[:, 5, :], ALU.max, ALU.add).then_inc(S["dt"], 1)
                dve.wait_ge(S["dt"], 1)
                V.tensor_tensor(t4(6), t4(7), bc(negA[:, :]), ALU.mult).then_inc(S["adec"], 1)
                dve.wait_ge(S["adec"], 1)
                for c in range(NT):
                    a = dts[:, 6, c * HM:(c + 1) * HM].rearrange("p (h a) -> p h a", a=1).broadcast_to([P, HM, P])
                    V.tensor_tensor(av[:, c, :, :], bc(C["le"], HM), a, ALU.mult).then_inc(S["av"], 1)
                dve.wait_ge(S["g_ps"], 1)
                V.tensor_tensor(gm[:, :, :], tk(PS[0][:, :]), bc(C["le"], NT), ALU.mult).then_inc(S["gm"], 1)
                dve.wait_ge(S["gm"], 1)
                for c in range(NT):
                    dve.wait_ge(S["lex"], c + 1)
                    V.tensor_tensor(av[:, c, :, :], lex[:, c, :, :], bc(gm[:, c, :], HM), ALU.mult).then_inc(S["wmat"], 1)
                V.memset(state[:, 0, :], 0.0).then_inc(S["state"], 1)
                dve.wait_ge(S["ec"], 1)
                for c in range(NT - 1):
                    dve.wait_ge(S["state"], c + 1)
                    tot = ec[0:NS, c, HM:2 * HM].rearrange("p (h a) -> p h a", a=1).broadcast_to([NS, HM, PM])
                    link(V.tensor_tensor(hm(stmp[:, :]), hm(state[:, c, :]), tot, ALU.mult))
                    dve.wait_ge(S["st_ps"], c + 1)
                    V.tensor_tensor(state[:, c + 1, :], stmp[:, :], PS[4 + c][0:NS, 0:DI], ALU.add).then_inc(S["state"], 1)
                for c in range(NT):
                    dve.wait_ge(S["y_ps"], c + 1)
                    cum = ec[:, c, 0:HM].rearrange("p (h a) -> p h a", a=1).broadcast_to([P, HM, PM])
                    V.tensor_tensor(hm(yg[:, c, :]), hm(PS[c][:, DI:2 * DI]), cum, ALU.mult).then_inc(S["yi"], 1)
                    dve.wait_ge(S["yi"], c + 1)
                    V.tensor_tensor(yg[:, c, :], yg[:, c, :], PS[c][:, 0:DI], ALU.add).then_inc(S["yj"], 1)
                dve.wait_ge(S["yg"], 4)
                stats(lambda j: yg[:, j, :], 1)
                dve.wait_ge(S["op_ps"], 1)
                dve.wait_ge(S["yr"], 1)
                for j in range(NT):
                    V.scalar_tensor_tensor(x1[:, j, :], PS[6][:, j * D:(j + 1) * D], sm[:, 1, j:j + 1], xn[:, j, :], ALU.mult, ALU.add).then_inc(S["x1"], 1)
                dve.wait_ge(S["x1"], 4)
                stats(lambda j: x1[:, j, :], 2)
                dve.wait_ge(S["rr2"], 1)
                for j in range(NT):
                    V.tensor_scalar(un[:, j, :], x1[:, j, :], mv[:, j, 0:1], sm[:, 1, j:j + 1], ALU.subtract, ALU.mult).then_inc(S["un2"], 1)
                dve.wait_ge(S["tr_un2"], 1)
                V.tensor_scalar(h2[:, :], PS[7][:, :], C["ln2w"], C["ln2b"], ALU.mult, ALU.add).then_inc(S["h2"], 1)
                dve.wait_ge(S["down_ps"], 1)
                dve.wait_ge(S["res2"], 1)
                V.tensor_tensor(s0[:, :, :], tk(PS[4][:, :]), x1[:, :, :], ALU.add).then_inc(S["s0"], 1)
                def maxima(n, count):
                    for u in range(n, n + count):
                        h, j = divmod(u, NT)
                        dve.wait_ge(S["mx_ps"], u + 1)
                        V.tensor_reduce(mx[:, j, h:h + 1], PS[MX_RING[u % 2]][:, :], AX.X, ALU.max).then_inc(S["mx"], 1)

                def remainder(g):
                    dve.wait_ge(S["m1"], g + 1)
                    if g:
                        dve.wait_ge(S["m3"], g)
                    V.scalar_tensor_tensor(mrem, PS[4][0:GH, :], -1.0, mpart[:, 0, :], ALU.mult,
                                           ALU.subtract).then_inc(S["mr"], 1)

                def normalise(g):
                    dve.wait_ge(S["tr_o"], g + 1)
                    o = PS[4][:, :].rearrange("p (j h d) -> p j h d", j=NT, h=GH)
                    V.reciprocal(orec[:, :, :], o[:, :, :, DH]).then_inc(S["orec"], 1)
                    dve.wait_ge(S["orec"], g + 1)
                    w = orec[:, :, :].rearrange("p j (h a) -> p j h a", a=1).broadcast_to([P, NT, GH, DH])
                    V.tensor_tensor(att[:, :, GH * DH * g:GH * DH * (g + 1)].rearrange("p j (h d) -> p j h d", h=GH),
                                    o[:, :, :, 0:DH], w, ALU.mult).then_inc(S["att"], 1)

                for g in range(2):
                    maxima(16 * g, 16)
                    remainder(g)
                for u in range(4 * NG):
                    if u < 8:
                        maxima(32 + 4 * u, 4)
                    if u in (4, 8):
                        remainder(u // 4 + 1)
                    if u >= 6 and u % 4 == 2:
                        normalise(u // 4 - 1)
                normalise(NG - 1)
                dve.wait_ge(S["wo_ps"], 1)
                V.tensor_tensor(hb[:, :, :], tk(PS[4][:, :]), xn[:, :, :], ALU.add).then_inc(S["hb"], 1)
                dve.wait_ge(S["hb"], 1)
                stats(lambda j: hb[:, j, :], 3)
                dve.wait_ge(S["rr3"], 1)
                for j in range(NT):
                    V.tensor_scalar(un[:, j, :], hb[:, j, :], sm[:, 1, j:j + 1], None, ALU.mult).then_inc(S["un3"], 1)
                dve.wait_ge(S["lg_ps"], 1)
                V.tensor_copy(lg[:, :, :], tk(PS[1][:, 0:NT * E])).then_inc(S["lg"], 1)
                dve.wait_ge(S["lg"], 1)
                for j in range(NT):
                    V.max(top[:, j, :], lg[:, j, :]).then_inc(S["top"], 1)
                for j in range(NT):
                    dve.wait_ge(S["top"], j + 1)
                    V.max_index(topi[:, j, :], top[:, j, :], lg[:, j, :]).then_inc(S["topi"], 1)
                dve.wait_ge(S["topi"], 4)
                link(V.tensor_copy(topf[:, :, :], topi[:, :, :]))
                V.tensor_tensor(tw[:, 0, :], top[:, :, 1], top[:, :, 0], ALU.subtract).then_inc(S["topf"], 1)
                wide = lambda t: t.rearrange("p (j a) -> p j a", a=1).broadcast_to([P, NT, E])
                io = bc(C["iota"], NT)
                link(V.tensor_tensor(oh[:, 0, :, :], io, wide(topf[:, :, 0]), ALU.is_equal))
                link(V.tensor_tensor(oh[:, 1, :, :], io, wide(topf[:, :, 1]), ALU.is_equal))
                dve.wait_ge(S["tope"], 1)
                link(V.tensor_scalar(tw[:, 2, :], tw[:, 1, :], 1.0, None, ALU.add))
                link(V.reciprocal(tw[:, 3, :], tw[:, 2, :]))
                link(V.tensor_tensor(tw[:, 4, :], tw[:, 3, :], tw[:, 1, :], ALU.mult))
                link(V.tensor_tensor(oh[:, 0, :, :], oh[:, 0, :, :], wide(tw[:, 3, :]), ALU.mult))
                link(V.tensor_tensor(oh[:, 1, :, :], oh[:, 1, :, :], wide(tw[:, 4, :]), ALU.mult))
                V.tensor_tensor(we[:, :, :], oh[:, 0, :, :], oh[:, 1, :, :], ALU.add).then_inc(S["we"], 1)
                dve.wait_ge(S["we"], 1)

                def expert_hidden(u):
                    dve.wait_ge(S["sa"], u + 1)
                    dve.wait_ge(S["eb_ps"], u + 1)
                    if u >= 4:
                        dve.wait_ge(S["ed_ps"], u // 2 - 1)
                    V.tensor_tensor(hid[:, u % 4, :], sa[:, u % 3, :], PS[2 * (u % 3) + 1][:, :], ALU.mult).then_inc(S["hid"], 1)

                def expert_sum(e):
                    dve.wait_ge(S["ed_ps"], e + 1)
                    for j in range(NT):
                        if e:
                            dve.wait_ge(S["eacc"], 4 * (e - 1) + j + 1)
                        V.scalar_tensor_tensor(hb[:, j, :], PS[6 + e % 2][:, j * D:(j + 1) * D], we[:, j, e:e + 1], hb[:, j, :], ALU.mult, ALU.add).then_inc(S["eacc"], 1)

                for e in range(E):
                    expert_hidden(2 * e)
                    if e:
                        expert_sum(e - 1)
                    expert_hidden(2 * e + 1)
                expert_sum(E - 1)
                dve.wait_ge(S["g0"], 1)
                V.tensor_tensor(x2[:, :, :], s0[:, :, :], g0[:, :, :], ALU.mult).then_inc(S["sg0"], 1)
                dve.wait_ge(S["sg0"], 1)
                V.tensor_tensor(x2[:, :, :], x2[:, :, :], xin[:, :, :], ALU.add).then_inc(S["x2"], 1)
                dve.wait_ge(S["x2"], 1)
                stats(lambda j: x2[:, j, :], 4)
                dve.wait_ge(S["rr4"], 1)
                for j in range(NT):
                    V.tensor_scalar(xn[:, j, :], x2[:, j, :], mv[:, j, 0:1], sm[:, 1, j:j + 1], ALU.subtract, ALU.mult).then_inc(S["xn1"], 1)
                for j in range(NT):
                    V.tensor_scalar(un[:, j, :], x2[:, j, :], mv[:, j, 0:1], sm[:, 3, j:j + 1], ALU.subtract, ALU.mult).then_inc(S["un4"], 1)
                dve.wait_ge(S["tr_un4"], 1)
                V.tensor_copy(un4T[:, :], PS[1][:, :]).then_inc(S["un4T"], 1)
                for j in range(NT):
                    dve.wait_ge(S["qkv_ps"], j + 1)
                    V.tensor_tensor(qkv[:, j, :], PS[2 + j][:, 0:3 * D], C["bqkv"], ALU.add).then_inc(S["qkv"], 1)
                dve.wait_ge(S["sq"], 1)
                V.tensor_reduce(inv[:, :, :], sq[:, :, :].rearrange("p j (h d) -> p j h d", d=DH), AX.X, ALU.add).then_inc(S["nrm"], 1)
                dve.wait_ge(S["af_ps"], 1)
                V.tensor_copy(lg[:, :, :], tk(PS[0][:, 0:NT * E])).then_inc(S["af"], 1)
                dve.wait_ge(S["af"], 1)
                for j in range(NT):
                    V.max(top[:, j, :], lg[:, j, :]).then_inc(S["top"], 1)
                for j in range(NT):
                    dve.wait_ge(S["top"], 5 + j)
                    V.max_index(topi[:, j, :], top[:, j, :], lg[:, j, :]).then_inc(S["topi"], 1)
                dve.wait_ge(S["topi"], 8)
                link(V.tensor_copy(topf[:, :, :], topi[:, :, :]))
                V.tensor_copy(tw[:, 0, :], top[:, :, 0]).then_inc(S["tpf1"], 1)
                link(V.tensor_tensor(oh[:, 0, :, :], io, wide(topf[:, :, 0]), ALU.is_equal))
                dve.wait_ge(S["tpe1"], 1)
                link(V.tensor_scalar(tw[:, 2, :], tw[:, 1, :], 1.0, None, ALU.add))
                link(V.reciprocal(tw[:, 3, :], tw[:, 2, :]))
                V.tensor_tensor(we[:, :, :], oh[:, 0, :, :], wide(tw[:, 3, :]), ALU.mult).then_inc(S["ohs"], 1)
                dve.wait_ge(S["vk_ps"], 1)
                V.tensor_tensor(vkm, PS[6][:, 0:P], msc[:, :], ALU.mult).then_inc(S["vkm"], 1)
                dve.wait_ge(S["o1_ps"], 1)
                V.tensor_tensor(s1[:, :, :], tk(PS[3][:, :]), bc(C["bo1"], NT), ALU.add).then_inc(S["s1"], 1)
                dve.wait_ge(S["b2_ps"], 1)
                V.tensor_tensor(x1[:, :, :], tk(PS[4][:, :]), xn[:, :, :], ALU.add).then_inc(S["facc"], 1)
                for e in range(E):
                    dve.wait_ge(S["fd_ps"], e + 1)
                    for j in range(NT):
                        dve.wait_ge(S["facc"], 1 if e == 0 else 4 * (e - 1) + j + 2)
                        V.scalar_tensor_tensor(x1[:, j, :], PS[6 + e % 2][:, j * D:(j + 1) * D], we[:, j, e:e + 1], x1[:, j, :], ALU.mult, ALU.add).then_inc(S["facc"], 1)
                dve.wait_ge(S["g1"], 1)
                V.tensor_tensor(s1[:, :, :], s1[:, :, :], g0[:, :, :], ALU.mult).then_inc(S["sg1"], 1)
                dve.wait_ge(S["sg1"], 1)
                V.tensor_tensor(xn[:, :, :], s1[:, :, :], x2[:, :, :], ALU.add).then_inc(S["out"], 1)
                pass_ends(dve, "dve")

        @block.gpsimd
        def _(pool):
            G = nc.gpsimd
            pool.wait_ge(s_load, 64)
            with pool.Fori(0, B) as it:
                links = [0]

                def link(ins):
                    ins.then_inc(S["pool_chain"], 1)
                    links[0] += 1
                    pool.wait_ge(S["pool_chain"], links[0])

                def rsqrt(k, src, signal=None):
                    link(G.tensor_scalar(sm[:, k, :], src, EPS, None, ALU.add))
                    ins = G.tensor_tensor(sm[:, k, :], sm[:, k, :], C["mhalf"], ALU.pow)
                    ins.then_inc(signal, 1) if signal else link(ins)

                def twice_normed():
                    rsqrt(1, mv[:, :, 1])
                    link(G.tensor_tensor(sm[:, 2, :], sm[:, 1, :], mv[:, :, 1], ALU.mult))
                    link(G.tensor_tensor(sm[:, 2, :], sm[:, 2, :], sm[:, 1, :], ALU.mult))
                    rsqrt(2, sm[:, 2, :])

                def mean_square():
                    link(G.tensor_tensor(sm[:, 0, :], mv[:, :, 0], mv[:, :, 0], ALU.mult))
                    link(G.tensor_tensor(sm[:, 0, :], sm[:, 0, :], mv[:, :, 1], ALU.add))

                bc = lambda t, n=PM: t.rearrange("p (h a) -> p h a", a=1).broadcast_to([P, HM, n])
                pool.wait_ge(S["mv"], 4)
                twice_normed()
                G.tensor_tensor(sm[:, 3, :], sm[:, 1, :], sm[:, 2, :], ALU.mult).then_inc(S["rr"], 1)
                pool.wait_ge(S["rr"], 1)
                for n, a in enumerate((32, 96)):
                    G.memset(qx[a:a + 32, :, :].bitcast(U32), 0).then_inc(S["qz"], 1)
                    pool.wait_ge(S["qz"], n + 1)
                for s in range(2):
                    pool.wait_ge(S["r1"], s + 1)
                    G.tensor_copy(part[:, s, 1, :], rem[:, s, :]).then_inc(S["q2"], 1)
                    pool.wait_ge(S["q2"], s + 1)
                    G.tensor_tensor(part[:, s, 2, :], rem[:, s, :], part[:, s, 1, :], ALU.subtract).then_inc(S["q3"], 1)
                for c in range(NT):
                    pool.wait_ge(S["xtok"], c + 1)
                    G.tensor_tensor(hm(xdt[:, c, :]), hm(xtok[:, c, 0:DI]), bc(dts[:, 7, c * HM:(c + 1) * HM]), ALU.mult).then_inc(S["xdt"], 1)
                    G.tensor_tensor(hm(xskip[:, c, :]), hm(xtok[:, c, 0:DI]), bc(C["dskip"]), ALU.mult).then_inc(S["xskip"], 1)
                    pool.wait_ge(S["xdt"], c + 1)
                    pool.wait_ge(S["lex"], c + 1)
                    G.tensor_tensor(hm(xw[:, c, :]), hm(xdt[:, c, :]), bc(lex[:, c, :, P - 1]), ALU.mult).then_inc(S["xw"], 1)
                for c in range(NT):
                    pool.wait_ge(S["xskip"], c + 1)
                    pool.wait_ge(S["yj"], c + 1)
                    G.tensor_tensor(yg[:, c, :], yg[:, c, :], xskip[:, c, :], ALU.add).then_inc(S["yk"], 1)
                    pool.wait_ge(S["yk"], c + 1)
                    pool.wait_ge(S["zs"], 2)
                    G.tensor_tensor(yg[:, c, :], yg[:, c, :], zs[:, c, :], ALU.mult).then_inc(S["yg"], 1)
                pool.wait_ge(S["mv"], 8)
                mean_square()
                rsqrt(1, sm[:, 0, :], S["yr"])
                pool.wait_ge(S["mv"], 12)
                pool.wait_ge(S["x1"], 4)
                rsqrt(1, mv[:, :, 1], S["rr2"])
                pool.wait_ge(S["un2"], 4)
                G.tensor_tensor(x1[:, :, :], x1[:, :, :], C["mb2"].rearrange("p (a n) -> p a n", a=1).broadcast_to([P, NT, D]), ALU.add).then_inc(S["res2"], 1)
                for g in range(NG):
                    pool.wait_ge(S["mr"], g + 1)
                    G.tensor_copy(mpart[:, 1, :], mrem).then_inc(S["m2"], 1)
                    pool.wait_ge(S["m2"], g + 1)
                    G.tensor_tensor(mpart[:, 2, :], mrem, mpart[:, 1, :], ALU.subtract).then_inc(S["m3"], 1)
                pool.wait_ge(S["mv"], 16)
                mean_square()
                rsqrt(1, sm[:, 0, :], S["rr3"])
                pool.wait_ge(S["mv"], 20)
                twice_normed()
                G.tensor_tensor(sm[:, 3, :], sm[:, 1, :], sm[:, 2, :], ALU.mult).then_inc(S["rr4"], 1)
                pool.wait_ge(S["qkv"], 4)
                G.tensor_tensor(sq[:, :, :], qkv[:, :, 0:2 * D], qkv[:, :, 0:2 * D], ALU.mult).then_inc(S["sq"], 1)
                pool.wait_ge(S["nrm"], 1)
                flat = inv[:, :, :].rearrange("p j h -> p (j h)")
                link(G.tensor_scalar(flat, flat, 1e-24, None, ALU.max))
                half = C["mhalf"][:, 0:1].broadcast_to([P, NT * 2 * HA])
                G.tensor_tensor(flat, flat, half, ALU.pow).then_inc(S["inv"], 1)
                pool.wait_ge(S["inv"], 1)
                for k in range(2):
                    t = qkv[:, :, k * D:(k + 1) * D].rearrange("p j (h d) -> p j h d", d=DH)
                    r = inv[:, :, k * HA:(k + 1) * HA].rearrange("p j (h a) -> p j h a", a=1)
                    G.tensor_tensor(t, t, r.broadcast_to([P, NT, HA, DH]), ALU.mult).then_inc(S["qkn"], 1)
                pass_ends(pool, "pool")



def _tables(i):
    T_ = np.transpose
    row = lambda a: np.broadcast_to(a.reshape(1, -1), (P, a.size))
    col = lambda a: a.reshape(-1, P).T
    r = np.arange(P)
    f = np.float32
    head = r // DH
    cw, cb = i["L0_attn_conv_w"], i["L0_attn_conv_b"]
    bcw = T_(cw[DI:].reshape(2, NS, TAPS), (1, 0, 2)).reshape(NS, 8)
    bcb = cb[DI:].reshape(2, NS).T
    up = lambda w: T_(w, (2, 0, 1)).reshape(P, -1)
    down = lambda w: T_(w.reshape(E, D, -1, P), (3, 0, 2, 1)).reshape(P, -1)
    a = dict(
        ident=np.eye(P, dtype=f), le=(r[:, None] <= r[None, :]).astype(f), gt=(r[:, None] > r[None, :]).astype(f),
        blk=(head[:, None] == head[None, :]).astype(f), iota=row(np.arange(E, dtype=f)),
        mhalf=np.full((P, NT), -0.5, f), ln1w=col(i["L0_attn_ln1_w"]), ln1b=col(i["L0_attn_ln1_b"]),
        winT=i["L0_attn_in_proj_w"].T, cwx=T_(cw[:DI].reshape(2, P, TAPS), (1, 0, 2)).reshape(P, 8),
        cbx=col(cb[:DI]), cwbc=np.concatenate([bcw, bcw]), cbbc=np.concatenate([bcb, bcb]),
        dtb=row(i["L0_attn_dt_bias"]), alog=row(i["L0_attn_A_log"]), dskip=row(i["L0_attn_D"]),
        nw=col(i["L0_attn_norm_w"]), woutT=T_(i["L0_attn_out_proj_w"].reshape(D, 2, P), (2, 1, 0)).reshape(P, -1),
        ln2w=col(i["L0_attn_ln2_w"]), ln2b=col(i["L0_attn_ln2_b"]), mw1T=i["L0_attn_mlp_w1"].T,
        mb1=col(i["L0_attn_mlp_b1"]), mw2T=T_(i["L0_attn_mlp_w2"].reshape(D, 4, P), (2, 1, 0)).reshape(P, -1),
        mb2=row(i["L0_attn_mlp_b2"]), r1w=col(i["L0_ffn_ln1_w"]), r2w=col(i["L0_ffn_ln2_w"]),
        wqT=i["L0_ffn_wq"].T, wkT=i["L0_ffn_wk"].T, wvT=i["L0_ffn_wv"].T, woT=i["L0_ffn_wo"].T,
        gateT=i["L0_ffn_gate_w"].T)
    b = dict(ew1T=up(i["L0_ffn_w1"]), ew3T=up(i["L0_ffn_w3"]), ew2T=down(i["L0_ffn_w2"]))
    c = dict(
        wqkv=np.concatenate([i["L1_attn_Wq"], i["L1_attn_Wk"], i["L1_attn_Wv"]], axis=1),
        bqkv=row(np.concatenate([i["L1_attn_bq"], i["L1_attn_bk"], i["L1_attn_bv"]])), wo1=i["L1_attn_Wo"],
        bo1=row(i["L1_attn_bo"]), mcol=np.repeat(i["L1_attn_m"], DH).reshape(P, 1), centT=i["L1_ffn_centroids"].T,
        lng=i["L1_ffn_ln_g"].T, lnb=i["L1_ffn_ln_b"].T, fb1=T_(i["L1_ffn_b1"].reshape(E * 4, P), (1, 0)),
        fw1T=up(i["L1_ffn_w1"]), fw2T=down(i["L1_ffn_w2"]))
    return [np.ascontiguousarray(np.concatenate([t[k] for k in pack], axis=1))
            for t, pack in ((a, PACK_A), (b, PACK_B), (c, PACK_C))]


def kernel(**inputs):
    import concourse.bacc as bacc
    from concourse.bass_utils import run_bass_kernel_spmd

    i = {k: np.asarray(v) for k, v in inputs.items()}
    pack_a, pack_b, pack_c = _tables(i)
    arrays = {"x": np.ascontiguousarray(i["L0_attn_x"]), "pack_a": pack_a, "pack_b": pack_b, "pack_c": pack_c,
              "b2": np.ascontiguousarray(i["L1_ffn_b2"])}
    nc = bacc.Bacc("TRN2", target_bir_lowering=False, num_devices=1)
    aps = [nc.dram_tensor(k, a.shape, F32, kind="ExternalInput").ap() for k, a in arrays.items()]
    y = nc.dram_tensor("y", (B, T, D), F32, kind="ExternalOutput").ap()
    build(nc, *aps, y)
    r = run_bass_kernel_spmd(nc, [arrays], core_ids=[0])
    return r.results[0]["y"]
```

```python
from contextlib import ExitStack

import numpy as np

import concourse.bass as bass
from concourse import mybir

F32 = mybir.dt.float32
BF16 = mybir.dt.bfloat16
U32 = mybir.dt.uint32
ALU = mybir.AluOpType
ACT = mybir.ActivationFunctionType
AX = mybir.AxisListType

P = 128
B, T, D = 8, 512, 128
NT = T // P
HM, PM, NS, TAPS = 4, 64, 64, 4
DI = HM * PM
DIP = 2 * DI + 2 * NS + HM
MF = 4 * D
HA, DH = 16, 8
E, TOPK = 8, 2
I0, I1 = 256, 512
EPS = 1e-5
PAIRS = [(0, 0), (1, 1), (2, 0), (1, 0), (0, 1), (0, 2)]
RUNS = (((0, 0, 3), (3, 1, 1), (4, 0, 1), (5, 0, 1)), ((0, 0, 2), (2, 0, 1), (3, 0, 3)))
KROWS = len(PAIRS) * DH
MROWS = KROWS + 3
HROWS = 64
GH = 4
NG = HA // GH

PACK_A = dict(ident=P, le=P, gt=P, blk=P, iota=E, mhalf=NT, ln1w=1, ln1b=1, winT=DIP, cw=3 * TAPS, cb=3,
              dtb=HM, alog=HM, dskip=HM, nw=2, woutT=2 * D, ln2w=1, ln2b=1, mw1T=MF, mb1=NT, mw2T=4 * D,
              mb2=D, r1w=1, r2w=1, wqT=D, wkT=D, wvT=D, woT=D, gateT=E)
PACK_B = dict(ew1T=E * I0, ew3T=E * I0, ew2T=E * 2 * D)
PACK_C = dict(wqkv=3 * D, bqkv=3 * D, wo1=D, bo1=D, mcol=1, centT=E, lng=E, lnb=E, fb1=E * 4, fw1T=E * I1,
              fw2T=E * 4 * D)

SIGNALS = (
    "x_in bn mv xn un rr tr_un hA hB "
    "dt_ps qk_ps v_ps xbc_ps z_ps q1 r1 q2 q3 q_store k_store qz qk_load vext xbc zs dtraw conv xc dtabs dtu dt adec av "
    "cum_ps ec seg_ps lex g_ps gm wmat xtr xtok xdt xw st_ps state y_ps yj yg yr ytr yT op_ps x1 "
    "rr2 un2 res2 tr_un2 h2 up_ps gel down_ps s0 "
    "mx_ps mx tr_mx m1 mr m3 m_store m_load sc_ps ex pv oc tr_o att tr_att attT wo_ps hb "
    "rr3 un3 tr_un3 h3 lg_ps lg top topi topf tope we "
    "ea_ps eb_ps sa hid ed_ps eacc g0 xr_in x2 "
    "bnB mvB rr4 xn1 un4 tr_xn1 tr_un4 xn1T un4T qkv_ps qkv sq nrm rt inv qkn vk_ps vkm mm_ps mm qT_ps qT o1_ps s1 "
    "af_ps af tpf1 tpe1 ohs tr_ohs ohT b2_ps fu_ps fh fd_ps facc g1 out "
    "dve_chain pool_chain").split()


WEAVE = ("babbbbbbbbbbbbbbbbabbbabaaaaababaabaabbbbmabmabmabbmbbabmmbmbmbaamaaaabmbbmamaabmabmbmbbmamabmbm"
         "abbmmbmabmbmbmbmabmbmbmbmbmbmbmbmbbbambbmabbmamamabmbabmbbmabmbbmabmbmbmaabmaabmababbmbaaamaabaa"
         "amaabmaambmaaabamaaabaabmabmabmaaabmaaabmabaaabmaamaabmabmabaabbmaabmbmaaabaaaaabaaabbaaabaaabaa"
         "ababaaaaaaaabaabaaaaaabaababbbabaa")


def order():
    a = [("a", "stats"), ("a", "norm"), ("a", "dt, q, k, v")] + [("in", c) for c in range(3)]
    a += [("a", "softplus"), ("a", "z")] + [("conv", c) for c in range(3)]
    a += [("a", "decays")] + [("seg", c) for c in range(NT)] + [("a", "B.C")] + [("xtok", c) for c in range(NT)]
    a += [("a", "first state")] + [("grow", c) for c in range(NT - 1)]
    a += [("a", "scan")] + [("y", c) for c in range(NT)]
    a += [("a", step) for step in ("turn y", "mamba out", "norm 2", "bias 2")]
    a += [("mlp up", c) for c in range(4)] + [("a", "mlp down")]
    a += [("score", i) for i in range(GH)]
    for u in range(4 * NG):
        for i in range(GH if u < 4 * NG - 1 else 0):
            a.append(("score", GH * (u + 1) + i))
            if u >= 6 and u % 4 == 2 and i == 1:
                a.append(("turn out", u // 4 - 1))
        a.append(("values", u))
        if u % 4 == 3:
            a.append(("outputs", u // 4))
    a.append(("turn out", NG - 1))
    a += [("a", step) for step in ("turn att", "attention out", "norm 3", "logits", "top two")]
    b, m = [], []
    for u in range(2 * E):
        b += [("gate", u), ("up", u)]
        if u % 2 == 0 and u:
            b += [("down", u - 2), ("down", u - 1)]
    b += [("down", 2 * E - 2), ("down", 2 * E - 1)]
    b += [("b", step) for step in ("silu", "residual", "norms", "turn norms", "q, k, v", "lengths", "inverse lengths",
                                   "v.k", "attention out")]
    for u in range(4 * E):
        b.append(("ffn up", u))
        if u >= 4 and u % 4 < 2:
            b += [("ffn down", u - 4 + u % 4), ("ffn down", u - 3 + u % 4)]
    b += [("ffn down", 4 * E - 4 + j) for j in range(NT)] + [("b", "output")]
    for g in range(NG):
        m += [("max", n) for n in range(16 * g, 16 * g + 16)] + [("turn max", g)]
    strands = {"a": a, "b": b, "m": m}
    assert all(len(strand) == WEAVE.count(k) for k, strand in strands.items())
    return [strands[k].pop(0) for k in WEAVE]


ORDER = order()
STAGE_B = ("gate", "up", "down", "b", "ffn up", "ffn down")


def build(nc, x, pack_a, pack_b, pack_c, b2, out):
    with ExitStack() as ctx:
        def sb(name, shape, dt=F32):
            return ctx.enter_context(nc.sbuf_tensor(name, shape, dt))

        S = {name: ctx.enter_context(nc.semaphore(name)) for name in SIGNALS}
        done = ctx.enter_context(nc.semaphore("pass_done"))
        ENGINES = ("pe", "act", "dve", "pool")
        go = {k: ctx.enter_context(nc.semaphore("go_" + k)) for k in ENGINES}
        ids = sorted(x.num for x in S.values())
        assert ids == list(range(ids[0], ids[-1] + 1))

        def pass_ends(eng, name):
            eng.drain().then_inc(done, 1)
            eng.wait_ge(go[name], 1)
            eng.sem_clear(go[name])

        y_out = ctx.enter_context(nc.semaphore("y_out"))
        s_a = ctx.enter_context(nc.semaphore("table_a_loaded"))
        s_load = ctx.enter_context(nc.semaphore("tables_loaded"))
        s_set = {k: ctx.enter_context(nc.semaphore("setup_" + k)) for k in
                 ("prep", "sig", "exps", "scal", "bias_ps")}

        tabs, cols = [], {}
        for name, pack in (("tab_a", PACK_A), ("tab_b", PACK_B), ("tab_c", PACK_C)):
            tab = sb(name, [P, sum(pack.values())])
            tabs.append(tab)
            at = 0
            for k, n in pack.items():
                cols[k] = tab[:, at:at + n]
                at += n
        C = cols
        ident = C["ident"]
        b2t = sb("b2t", [E, D])
        ones = sb("ones", [P, P])
        negA = sb("negA", [P, HM])
        msc = sb("msc", [P, P])
        mtmp = sb("mtmp", [P, 4])
        bias1 = sb("bias1", [P, E * 4])

        xin = sb("xin", [P, NT, D])
        xn = sb("xn", [P, NT, D])
        un = sb("un", [P, NT, D])
        hA = sb("hA", [P, T])
        hB = sb("hB", [P, T])
        bst = sb("bst", [P, NT, 6])
        mv = sb("mv", [P, NT, 2])
        sm = sb("sm", [P, 4, NT])
        qx = sb("qx", [P, HA // 2, T], BF16)
        kx = sb("kx", [P, HA // 2, T], BF16)
        vext = sb("vext", [P, NT, HA, DH + 1])
        mx = sb("mx", [P, HA, NT])
        mpart = sb("mpart", [GH * NT, 3, P], BF16)
        mrem = sb("mrem", [GH * NT, P])
        pr = sb("pr", [P, 8, T])
        xc = pr[:, 0:4, :]
        av = pr[:, 4:8, :].rearrange("p c (h t) -> p c h t", h=HM)
        oc = sb("oc", [P, T])
        orec = sb("orec", [P, NT, GH])
        xbc = sb("xbc", [P, 3, T + TAPS - 1])
        zs = sb("zs", [P, NT, DI])
        dts = sb("dts", [P, 8, NT * HM])
        xtok = sb("xtok", [P, NT, DI + NS])
        ec = sb("ec", [P, NT, 2 * HM])
        gm = sb("gm", [P, NT, P])
        lex = sb("lex", [P, NT, HM, P])
        gel = lex[:, :, :, :].rearrange("p c h t -> p c (h t)")
        part = gel.bitcast(BF16)[:, 0:3, :].rearrange("p a (s t) -> p s a t", s=2)
        xdt = sb("xdt", [P, NT, DI])
        xw = sb("xw", [P, NT, DI])
        yg = sb("yg", [P, NT, DI])
        rem = yg[:, :, :].rearrange("p (s j) n -> p s (j n)", s=2)
        state = sb("state", [NS, NT, DI])
        stmp = sb("stmp", [NS, DI])
        yT = xdt[:, :, :].rearrange("p (k j) n -> p k (j n)", k=2)
        x1 = sb("x1", [P, NT, D])
        h2, attT, att = hA, hB, un
        h3 = sb("h3", [P, T])
        hb = sb("hb", [P, NT, D])
        s0 = sb("s0", [P, NT, D])
        we = sb("we", [P, NT, E])
        lg = sb("lg", [P, NT, E])
        top = sb("top", [P, NT, 8])
        topi = sb("topi", [P, NT, 8], U32)
        topf = sb("topf", [P, NT, 8])
        tw = sb("tw", [P, 6, NT])
        oh = sb("oh", [P, 2, NT, E])
        xres = sb("xres", [P, NT, D])
        fh = sb("fh", [P, 6, T])
        hid, sa = fh[:, 0:4, :], fh[:, 4:6, :]
        qkv = fh[:, 0:3, :].rearrange("p a n -> p (a n)").rearrange("p (j n) -> p j n", j=NT)
        sq = fh[:, 3:5, :].rearrange("p a n -> p (a n)").rearrange("p (j n) -> p j n", j=NT)
        g0 = sb("g0", [P, NT, D])
        x2 = sb("x2", [P, NT, D])
        xn1 = sb("xn1", [P, NT, D])
        un4 = sb("un4", [P, NT, D])
        ob = un4
        bstB = sb("bstB", [P, NT, 6])
        mvB = sb("mvB", [P, NT, 2])
        smB = sb("smB", [P, 4, NT])
        xn1T = h3
        un4T = sb("un4T", [P, T])
        inv = sb("inv", [P, 4, NT * 2 * HA])
        vkm = sb("vkm", [P, P])
        mm = sb("mm", [P, P])
        qT = fh[:, 3, :]
        ohT = h3[0:E, :]
        s1 = sb("s1", [P, NT, D])
        wf = sb("wf", [P, NT, E])
        fa = g0
        PS = [ctx.enter_context(nc.psum_tensor(f"ps{i}", [P, 512], F32)) for i in range(8)]

        qk_dram = nc.dram_tensor("qk_scratch", [2, 2, 3, HROWS, T], BF16, kind="Internal").ap()
        m_dram = nc.dram_tensor("m_scratch", [3, HA, T], BF16, kind="Internal").ap()

        TURNS = [step for step in ORDER if step[0] in ("max", "turn max", "turn out")]
        BEFORE = dict(zip(TURNS[1:], TURNS))
        RING = 3
        SEG_BANK, XT_BANK, ST_BANK, Y_BANK, UP_BANK = (1, 2), (0, 1), (2, 3, 0), (1, 2, 3, 0), (0, 3, 2, 1)
        hm = lambda t: t.rearrange("p (h q) -> p h q", h=HM)
        tk = lambda t: t.rearrange("p (j n) -> p j n", j=NT)
        block = ctx.enter_context(nc.Block())

        def passes(eng, run):
            run(0, True, False)
            with eng.Fori(1, B) as it:
                run(it, True, True)
            run(B, False, True)

        def steps(a, b):
            taken = [(part, n) for part, n in ORDER if (b if part in STAGE_B else a)]
            if not b:
                taken.insert(taken.index(("score", 24)), ("tables", 0))
            return taken

        @block.sync
        def _(sp):
            sp.dma_start(tabs[0][:, :], pack_a).then_inc(s_a, 16)

            def tokens(dram, n):
                return dram[bass.ds(n, 1)].rearrange("a (j p) d -> p (a j) d", p=P)

            def run(it, a, b):
                if a:
                    sp.dma_start(xin[:, :, :], tokens(x, it)).then_inc(S["x_in"], 16)
                if not b:
                    sp.dma_start(tabs[2][:, :], pack_c).then_inc(s_load, 16)
                    sp.dma_start(tabs[1][:, :], pack_b).then_inc(s_load, 16)
                    sp.dma_start(b2t[:, :], b2).then_inc(s_load, 16)
                if b:
                    sp.dma_start(xres[:, :, :], tokens(x, it - 1)).then_inc(S["xr_in"], 16)
                if a:
                    for n in range(2):
                        sp.wait_ge(S["q3"], n + 1)
                        for h in range(2):
                            sp.dma_start(qk_dram[n, h].rearrange("a r t -> r a t"),
                                         part[HROWS * h:HROWS * (h + 1), n, :, :]
                                         ).then_inc(S[("q_store", "k_store")[n]], 16)
                    sp.wait_ge(S["qz"], 2)
                    for n in range(2):
                        sp.wait_ge(S[("q_store", "k_store")[n]], 32)
                        for h in range(2):
                            src = qk_dram[n, h].rearrange("a (d g) t -> (a d) g t", d=DH)
                            for first, of, count in RUNS[n]:
                                at = HROWS * h + DH * first
                                sp.dma_start((qx, kx)[n][at:at + DH * count, :, :],
                                             src[DH * of:DH * (of + count)]).then_inc(S["qk_load"], 16)
                    for g in range(NG):
                        sp.wait_ge(S["m3"], g + 1)
                        sp.dma_start(m_dram[:, GH * g:GH * g + GH].rearrange("a h (j t) -> (h j) a t", t=P),
                                     mpart[:, :, :]).then_inc(S["m_store"], 16)
                        sp.wait_ge(S["m_store"], 16 * (g + 1))
                        if g:
                            sp.wait_ge(S["m_load"], 32 * g)
                        for h in range(2):
                            sp.dma_start(qx[HROWS * h + KROWS:HROWS * h + MROWS, 2 * g:2 * g + 2, :],
                                         m_dram[:, GH * g:GH * g + GH].rearrange("a (g s) t -> s a g t", s=2)[h]
                                         ).then_inc(S["m_load"], 16)
                if b:
                    sp.wait_ge(S["out"], 1)
                    sp.sem_clear(y_out)
                    sp.dma_start(tokens(out, it - 1), ob[:, :, :]).then_inc(y_out, 16)
                else:
                    sp.sem_inc(y_out, 16)
                sp.wait_ge(done, len(ENGINES))
                sp.sem_clear(done)
                sp.sem_clear(range(ids[0], ids[-1] + 1))
                for k in ENGINES:
                    sp.sem_inc(go[k], 1)

            passes(sp, run)
            sp.wait_ge(y_out, 16)

        @block.tensor
        def _(pe):
            mmul = nc.tensor.matmul

            def turn(bank, src, width=D):
                for j in range(NT):
                    last = nc.tensor.transpose(PS[bank][0:width, j * P:(j + 1) * P], src[:, j, :], ident)
                return last

            pe.wait_ge(s_a, 16)
            pe.wait_ge(s_set["prep"], 5)

            def tables():
                pe.wait_ge(s_load, 48)
                for e in range(E):
                    for c in range(4):
                        n = e * 4 + c
                        ins = mmul(PS[5][:, n:n + 1], C["fw1T"][:, e * I1 + c * P:e * I1 + (c + 1) * P],
                                   C["lnb"][:, e:e + 1], start=True, stop=True)
                ins.then_inc(s_set["bias_ps"], 1)

            def gate(u):
                if u:
                    pe.wait_ge(S["sa"], u)
                mmul(PS[5][:, :], C["ew1T"][:, u * P:(u + 1) * P], h3[:, :], start=True, stop=True
                     ).then_inc(S["ea_ps"], 1)

            def up(u):
                if u:
                    pe.wait_ge(S["hid"], u)
                mmul(PS[6][:, :], C["ew3T"][:, u * P:(u + 1) * P], h3[:, :], start=True, stop=True
                     ).then_inc(S["eb_ps"], 1)

            def down(n):
                e = n // 2
                if n % 2 == 0:
                    pe.wait_ge(S["hid"], 2 * e + 2)
                    if e:
                        pe.wait_ge(S["eacc"], 4 * e)
                for j in range(n % 2 * 2, n % 2 * 2 + 2):
                    for c in range(2):
                        k = 2 * e + c
                        ins = mmul(PS[7][:, j * D:(j + 1) * D], hid[:, k % 4, j * P:(j + 1) * P],
                                   C["ew2T"][:, k * D:(k + 1) * D], start=(c == 0), stop=(c == 1))
                if n % 2:
                    ins.then_inc(S["ed_ps"], 1)

            def ffn_up(u):
                if u == 0:
                    pe.wait_ge(S["s1"], 1)
                    pe.wait_ge(S["facc"], 1)
                if u >= 2:
                    pe.wait_ge(S["fh"], u - 1)
                mmul(PS[5 + u % 2][:, :], C["fw1T"][:, u * P:(u + 1) * P], un4T[:, :], start=True, stop=True
                     ).then_inc(S["fu_ps"], 1)

            def ffn_down(n):
                e, j = divmod(n, NT)
                if j == 0:
                    pe.wait_ge(S["fh"], 4 * e + 4)
                    if e:
                        pe.wait_ge(S["facc"], 4 * e + 1)
                for c in range(4):
                    k = 4 * e + c
                    ins = mmul(PS[7][:, j * D:(j + 1) * D], fh[:, k % 6, j * P:(j + 1) * P],
                               C["fw2T"][:, k * D:(k + 1) * D], start=(c == 0), stop=(c == 3))
                if j == NT - 1:
                    ins.then_inc(S["fd_ps"], 1)

            def stage_b(step):
                if step == "turn norms":
                    pe.wait_ge(S["xn1"], 4)
                    turn(5, xn1).then_inc(S["tr_xn1"], 1)
                    pe.wait_ge(S["un4"], 4)
                    turn(6, un4).then_inc(S["tr_un4"], 1)
                elif step == "q, k, v":
                    pe.wait_ge(S["xn1T"], 1)
                    pe.wait_ge(S["eacc"], 32)
                    for j in range(NT):
                        if j == 2:
                            pe.wait_ge(S["un4T"], 1)
                        elif j == 3:
                            pe.wait_ge(S["qkv"], 1)
                        mmul(PS[(7, 5, 6, 7)[j]][:, 0:3 * D], xn1T[:, j * P:(j + 1) * P], C["wqkv"],
                             start=True, stop=True).then_inc(S["qkv_ps"], 1)
                    pe.wait_ge(S["qkv"], 2)
                    for j in range(NT):
                        ins = mmul(PS[5][:, j * E:(j + 1) * E], xn1T[:, j * P:(j + 1) * P], C["centT"],
                                   start=True, stop=True)
                    ins.then_inc(S["af_ps"], 1)
                elif step == "v.k":
                    pe.wait_ge(S["qkn"], 2)
                    for j in range(NT):
                        ins = mmul(PS[6][:, 0:P], qkv[:, j, 2 * D:3 * D], qkv[:, j, D:2 * D], start=(j == 0),
                                   stop=(j == NT - 1))
                    ins.then_inc(S["vk_ps"], 1)
                    turn(7, qkv[:, :, 0:D]).then_inc(S["qT_ps"], 1)
                    pe.wait_ge(S["ohs"], 1)
                    for j in range(NT):
                        ins = nc.tensor.transpose(PS[5][0:E, j * P:(j + 1) * P], wf[:, j, :], ident)
                    ins.then_inc(S["tr_ohs"], 1)
                    pe.wait_ge(S["vkm"], 1)
                    mmul(PS[6][:, P:2 * P], vkm[:, :], C["wo1"], start=True, stop=True).then_inc(S["mm_ps"], 1)
                elif step == "attention out":
                    pe.wait_ge(S["mm"], 1)
                    pe.wait_ge(S["qT"], 1)
                    for j in range(NT):
                        ins = mmul(PS[7][:, j * D:(j + 1) * D], qT[:, j * P:(j + 1) * P], mm[:, :], start=True,
                                   stop=True)
                    ins.then_inc(S["o1_ps"], 1)
                    pe.wait_ge(S["ohT"], 1)
                    for j in range(NT):
                        ins = mmul(PS[5][:, j * D:(j + 1) * D], ohT[:, j * P:(j + 1) * P], b2t[:, :], start=True,
                                   stop=True)
                    ins.then_inc(S["b2_ps"], 1)

            def bank_read(step):
                if step in BEFORE:
                    part, n = BEFORE[step]
                    if part == "max":
                        pe.wait_ge(S["mx"], n + 1)
                    elif part == "turn max":
                        pe.wait_ge(S["mr"], n + 1)
                    else:
                        pe.wait_ge(S["att"], n + 1)

            def max_score(n):
                h, j = divmod(n, NT)
                row = HROWS * (h % 2)
                if n == 0:
                    pe.wait_ge(S["qk_load"], 16 * 14)
                    pe.wait_ge(S["ec"], 1)
                bank_read(("max", n))
                mmul(PS[4][:, :], qx[row:row + HROWS, h // 2, j * P:(j + 1) * P],
                     kx[row:row + HROWS, h // 2, :], start=True, stop=True).then_inc(S["mx_ps"], 1)

            def turn_max(g):
                pe.wait_ge(S["mx"], 16 * (g + 1))
                bank_read(("turn max", g))
                nc.tensor.transpose(PS[4][0:GH * NT, 0:P], mx[:, GH * g:GH * g + GH, :].rearrange("p h j -> p (h j)"),
                                    ident).then_inc(S["tr_mx"], 1)

            def score(n):
                u, i = divmod(n, GH)
                g, k = divmod(u, NT)
                h = GH * g + i
                row = HROWS * (h % 2)
                if k == 0 and i == 0:
                    pe.wait_ge(S["m_load"], 32 * (g + 1))
                if n == 0:
                    pe.wait_ge(S["s0"], 1)
                elif n >= RING:
                    pe.wait_ge(S["ex"], n - RING + 1)
                mmul(PS[n % RING][:, :], kx[row:row + HROWS, h // 2, k * P:(k + 1) * P],
                     qx[row:row + HROWS, h // 2, :], start=True, stop=True).then_inc(S["sc_ps"], 1)

            def values(u):
                g, k = divmod(u, NT)
                pe.wait_ge(S["ex"], GH * (u + 1))
                if k == 0 and g:
                    pe.wait_ge(S["oc"], g)
                for i in range(GH):
                    ins = mmul(PS[3][32 * i:32 * i + DH + 1, :], vext[:, k, GH * g + i, :], pr[:, GH * (u % 2) + i, :],
                               start=(k == 0), stop=(k == NT - 1))
                ins.then_inc(S["pv"], 1)

            def turn_out(g):
                pe.wait_ge(S["oc"], g + 1)
                bank_read(("turn out", g))
                for j in range(NT):
                    ins = nc.tensor.transpose(PS[4][:, j * P:(j + 1) * P], oc[:, j * P:(j + 1) * P], ident)
                ins.then_inc(S["tr_o"], 1)

            def project(c):
                bank, signal = ((0, "hB"), (1, "r1"), (4, "dtraw"))[c]
                pe.wait_ge(S[signal], 1)
                mmul(PS[bank][:, :], C["winT"][:, DI + c * P:DI + (c + 1) * P], hA[:, :], start=True, stop=True
                     ).then_inc(S["xbc_ps"], 1)

            def segment(c):
                pe.wait_ge(S["av"], c + 1)
                if c == 0:
                    pe.wait_ge(S["xbc"], 2)
                elif c == 1:
                    pe.wait_ge(S["r1"], 2)
                else:
                    pe.wait_ge(S["lex"], c - 1)
                mmul(PS[SEG_BANK[c % 2]][:, :], C["gt"], av[:, c, :, :], start=True, stop=True
                     ).then_inc(S["seg_ps"], 1)

            def turn_xb(c):
                if c == 0:
                    pe.wait_ge(S["zs"], 2)
                elif c == 1:
                    pe.wait_ge(S["lex"], 3)
                else:
                    pe.wait_ge(S["xtok"], c - 1)
                bank = PS[XT_BANK[c % 2]]
                for k in range(2):
                    nc.tensor.transpose(bank[:, k * P:(k + 1) * P], xc[:, k, c * P:(c + 1) * P], ident)
                nc.tensor.transpose(bank[:, DI:DI + NS], xc[0:NS, 2, c * P:(c + 1) * P],
                                    C["ident"][0:NS, 0:NS]).then_inc(S["xtr"], 1)

            def grow(c):
                pe.wait_ge(S["xtok"], c + 1)
                pe.wait_ge(S["xw"], c + 1)
                if c == 0:
                    pe.wait_ge(S["lex"], 4)
                elif c == 1:
                    pe.wait_ge(S["gm"], 1)
                mmul(PS[ST_BANK[c]][0:NS, 0:DI], xtok[:, c, DI:DI + NS], xw[:, c, :], start=True, stop=True
                     ).then_inc(S["st_ps"], 1)

            def outcome(c):
                pe.wait_ge(S["wmat"], c + 1)
                pe.wait_ge(S["xdt"], c + 1)
                if c == 0:
                    pe.wait_ge(S["xtok"], 4)
                pe.wait_ge(S["state"], c + 1)
                bank = PS[Y_BANK[c]]
                for h in range(HM):
                    mmul(bank[:, h * PM:(h + 1) * PM], av[:, c, h, :], xdt[:, c, h * PM:(h + 1) * PM],
                         start=True, stop=True)
                mmul(bank[:, DI:2 * DI], xc[0:NS, 3, c * P:(c + 1) * P], state[:, c, :],
                     start=True, stop=True).then_inc(S["y_ps"], 1)

            def mlp_up(c):
                if c == 0:
                    pe.wait_ge(S["h2"], 1)
                mmul(PS[UP_BANK[c]][:, :], C["mw1T"][:, c * P:(c + 1) * P], h2[:, :], start=True, stop=True
                     ).then_inc(S["up_ps"], 1)

            def stage_a(step, b):
                if step == "norm":
                    pe.wait_ge(S["un"], 4)
                    turn(0, un).then_inc(S["tr_un"], 1)
                elif step == "dt, q, k, v":
                    pe.wait_ge(S["hA"], 1)
                    for j in range(NT):
                        ins = mmul(PS[4][:, j * HM:(j + 1) * HM], hA[:, j * P:(j + 1) * P], C["winT"][:, DIP - HM:DIP],
                                   start=True, stop=True)
                    ins.then_inc(S["dt_ps"], 1)
                    pe.wait_ge(S["hB"], 1)
                    mmul(PS[1][:, :], C["wqT"], hB[:, :], start=True, stop=True).then_inc(S["qk_ps"], 1)
                    mmul(PS[2][:, :], C["wkT"], hB[:, :], start=True, stop=True).then_inc(S["qk_ps"], 1)
                    for j in range(NT):
                        ins = mmul(PS[3][:, j * D:(j + 1) * D], hB[:, j * P:(j + 1) * P], C["wvT"], start=True,
                                   stop=True)
                    ins.then_inc(S["v_ps"], 1)
                elif step == "z":
                    for k, bank in enumerate((3, 0)):
                        pe.wait_ge(S[("vext", "xbc")[k]], 1)
                        for j in range(2):
                            ins = mmul(PS[bank][:, j * DI:(j + 1) * DI], hA[:, (2 * k + j) * P:(2 * k + j + 1) * P],
                                       C["winT"][:, 0:DI], start=True, stop=True)
                        ins.then_inc(S["z_ps"], 1)
                elif step == "decays":
                    pe.wait_ge(S["adec"], 1)
                    pe.wait_ge(S["xbc"], 3)
                    for c in range(NT):
                        dec = dts[:, 6, c * HM:(c + 1) * HM]
                        mmul(PS[4][:, c * 8:c * 8 + 4], C["le"], dec, start=True, stop=True)
                        ins = mmul(PS[4][:, c * 8 + 4:c * 8 + 8], ones[:, :], dec, start=True, stop=True)
                    ins.then_inc(S["cum_ps"], 1)
                elif step == "B.C":
                    pe.wait_ge(S["xc"], 4)
                    pe.wait_ge(S["zs"], 1)
                    for c in range(NT):
                        ins = mmul(PS[3][:, c * P:(c + 1) * P], xc[0:NS, 2, c * P:(c + 1) * P],
                                   xc[0:NS, 3, c * P:(c + 1) * P], start=True, stop=True)
                    ins.then_inc(S["g_ps"], 1)
                elif step == "turn y":
                    for j in range(NT):
                        pe.wait_ge(S["yg"], max(j + 1, 2))
                        for k in range(2):
                            ins = nc.tensor.transpose(PS[1 + k][:, j * P:(j + 1) * P], yg[:, j, k * P:(k + 1) * P],
                                                      ident)
                    ins.then_inc(S["ytr"], 1)
                elif step == "mamba out":
                    pe.wait_ge(S["yT"], 2)
                    for j in range(NT):
                        for k in range(2):
                            ins = mmul(PS[3][:, j * D:(j + 1) * D], yT[:, k, j * P:(j + 1) * P],
                                       C["woutT"][:, k * D:(k + 1) * D], start=(k == 0), stop=(k == 1))
                    ins.then_inc(S["op_ps"], 1)
                elif step == "norm 2":
                    pe.wait_ge(S["un2"], 4)
                    turn(1, un).then_inc(S["tr_un2"], 1)
                elif step == "mlp down":
                    pe.wait_ge(S["gel"], 4)
                    for j in range(NT):
                        for c in range(4):
                            ins = mmul(PS[0][:, j * D:(j + 1) * D], gel[:, c, j * P:(j + 1) * P],
                                       C["mw2T"][:, c * D:(c + 1) * D], start=(c == 0), stop=(c == 3))
                    ins.then_inc(S["down_ps"], 1)
                elif step == "turn att":
                    pe.wait_ge(S["att"], 4)
                    turn(3, att).then_inc(S["tr_att"], 1)
                elif step == "attention out":
                    pe.wait_ge(S["attT"], 1)
                    for j in range(NT):
                        ins = mmul(PS[4][:, j * D:(j + 1) * D], attT[:, j * P:(j + 1) * P], C["woT"], start=True,
                                   stop=True)
                    ins.then_inc(S["wo_ps"], 1)
                elif step == "norm 3":
                    pe.wait_ge(S["un3"], 4)
                    turn(0, un).then_inc(S["tr_un3"], 1)
                elif step == "logits":
                    pe.wait_ge(S["h3"], 1)
                    for j in range(NT):
                        ins = mmul(PS[1][:, j * E:(j + 1) * E], h3[:, j * P:(j + 1) * P], C["gateT"], start=True,
                                   stop=True)
                    ins.then_inc(S["lg_ps"], 1)

            def run(it, a, b):
                for part, n in steps(a, b):
                    if part == "a":
                        stage_a(n, b)
                    elif part == "in":
                        project(n)
                    elif part == "seg":
                        segment(n)
                    elif part == "xtok":
                        turn_xb(n)
                    elif part == "grow":
                        grow(n)
                    elif part == "y":
                        outcome(n)
                    elif part == "mlp up":
                        mlp_up(n)
                    elif part == "score":
                        score(n)
                    elif part == "values":
                        values(n)
                    elif part == "turn out":
                        turn_out(n)
                    elif part == "tables":
                        tables()
                    elif part == "b":
                        stage_b(n)
                    elif part == "gate":
                        gate(n)
                    elif part == "up":
                        up(n)
                    elif part == "down":
                        down(n)
                    elif part == "ffn up":
                        ffn_up(n)
                    elif part == "ffn down":
                        ffn_down(n)
                    elif part == "max":
                        max_score(n)
                    elif part == "turn max":
                        turn_max(n)
                pass_ends(pe, "pe")

            passes(pe, run)

        @block.scalar
        def _(act):
            A = nc.scalar.activation
            act.wait_ge(s_a, 16)
            A(negA[:, :], C["alog"], ACT.Exp).then_inc(s_set["exps"], 1)

            def tables():
                act.wait_ge(s_load, 48)
                A(mtmp[:, 0:1], C["mcol"], ACT.Exp, scale=-1.0).then_inc(s_set["exps"], 1)
                act.wait_ge(s_set["sig"], 2)
                A(mtmp[:, 3:4], mtmp[:, 2:3], ACT.Exp, scale=-float(np.log(T))).then_inc(s_set["scal"], 1)

            def gate(u):
                act.wait_ge(S["ea_ps"], u + 1)
                if u >= 2:
                    act.wait_ge(S["hid"], u - 1)
                A(sa[:, u % 2, :], PS[5][:, :], ACT.Silu).then_inc(S["sa"], 1)

            def ffn_up(u):
                act.wait_ge(S["fu_ps"], u + 1)
                if u >= 6:
                    act.wait_ge(S["fd_ps"], (u - 6) // 4 + 1)
                A(fh[:, u % 6, :], PS[5 + u % 2][:, :], ACT.Relu, bias=bias1[:, u:u + 1]).then_inc(S["fh"], 1)

            def stage_b(step):
                if step == "silu":
                    act.wait_ge(S["eacc"], 32)
                    A(g0[:, :, :], hb[:, :, :], ACT.Silu).then_inc(S["g0"], 1)
                elif step == "turn norms":
                    act.wait_ge(S["tr_xn1"], 1)
                    A(xn1T[:, :], PS[5][:, :], ACT.Copy).then_inc(S["xn1T"], 1)
                elif step == "lengths":
                    act.wait_ge(S["tpf1"], 1)
                    A(tw[:, 1, :], tw[:, 0, :], ACT.Exp, scale=-1.0).then_inc(S["tpe1"], 1)
                    act.wait_ge(S["nrm"], 2)
                    A(inv[:, 1, :], inv[:, 0, :], ACT.Sqrt).then_inc(S["rt"], 1)
                elif step == "v.k":
                    act.wait_ge(S["qT_ps"], 1)
                    A(qT[:, :], PS[7][:, :], ACT.Copy).then_inc(S["qT"], 1)
                    act.wait_ge(S["tr_ohs"], 1)
                    A(ohT[:, :], PS[5][0:E, :], ACT.Copy).then_inc(S["ohT"], 1)
                    act.wait_ge(S["mm_ps"], 1)
                    A(mm[:, :], PS[6][:, P:2 * P], ACT.Copy).then_inc(S["mm"], 1)
                elif step == "output":
                    act.wait_ge(S["facc"], 33)
                    A(g0[:, :, :], fa[:, :, :], ACT.Silu).then_inc(S["g1"], 1)

            def first_part(g):
                act.wait_ge(S["tr_mx"], g + 1)
                if g:
                    act.wait_ge(S["m_store"], 16 * g)
                A(mpart[:, 0, :], PS[4][0:GH * NT, 0:P], ACT.Copy, scale=-1.0).then_inc(S["m1"], 1)

            def exps(n):
                u, i = divmod(n, GH)
                act.wait_ge(S["sc_ps"], n + 1)
                if u >= 2 and i == 0:
                    act.wait_ge(S["pv"], u - 1)
                A(pr[:, GH * (u % 2) + i, :], PS[n % RING][:, :], ACT.Exp,
                  scale=float(DH) ** -0.5).then_inc(S["ex"], 1)

            def outputs(g):
                act.wait_ge(S["pv"], 4 * (g + 1))
                if g:
                    act.wait_ge(S["tr_o"], g)
                A(oc[:, :], PS[3][:, :], ACT.Copy).then_inc(S["oc"], 1)

            def project(c):
                act.wait_ge(S["xbc_ps"], c + 1)
                A(xbc[:, c, TAPS - 1:], PS[(0, 1, 4)[c]][:, :], ACT.Copy).then_inc(S["xbc"], 1)

            def segment(c):
                if c == 0:
                    act.wait_ge(S["q_store"], 32)
                    act.wait_ge(S["k_store"], 32)
                act.wait_ge(S["seg_ps"], c + 1)
                A(lex[:, c, :, :], hm(PS[SEG_BANK[c % 2]][:, :]), ACT.Exp).then_inc(S["lex"], 1)

            def turn_xb(c):
                act.wait_ge(S["xtr"], c + 1)
                A(xtok[:, c, :], PS[XT_BANK[c % 2]][:, 0:DI + NS], ACT.Copy).then_inc(S["xtok"], 1)

            def mlp_up(c):
                act.wait_ge(S["up_ps"], c + 1)
                A(gel[:, c, :], PS[UP_BANK[c]][:, :], ACT.Gelu, bias=C["mb1"][:, c:c + 1]).then_inc(S["gel"], 1)

            def conv(c):
                act.wait_ge(S["conv"], c + 1)
                if c == 2:
                    A(xc[0:NS, 3, :], xc[NS:2 * NS, 2, :], ACT.Silu).then_inc(S["xc"], 1)
                    A(xc[0:NS, 2, :], xc[0:NS, 2, :], ACT.Silu).then_inc(S["xc"], 1)
                else:
                    A(xc[:, c, :], xc[:, c, :], ACT.Silu).then_inc(S["xc"], 1)

            def stage_a(step, b):
                if step == "norm":
                    act.wait_ge(S["hA"], 1)
                    A(hB[:, :], PS[0][:, :], ACT.Copy, scale=C["r1w"]).then_inc(S["hB"], 1)
                elif step == "dt, q, k, v":
                    act.wait_ge(S["dtabs"], 1)
                    A(dts[:, 2, :], dts[:, 1, :], ACT.Exp, scale=-1.0).then_inc(S["dtu"], 1)
                    for k in range(2):
                        act.wait_ge(S["qk_ps"], k + 1)
                        A(part[:, k, 0, :], PS[1 + k][:, :], ACT.Copy).then_inc(S["q1"], 1)
                    for k in range(2):
                        act.wait_ge(S["r1"], k + 1)
                        A(part[:, k, 1, :], rem[:, k, :], ACT.Copy).then_inc(S["q2"], 1)
                    act.wait_ge(S["v_ps"], 1)
                    A(vext[:, :, :, 0:DH], PS[3][:, :].rearrange("p (j h d) -> p j h d", j=NT, h=HA),
                      ACT.Copy).then_inc(S["vext"], 1)
                elif step == "z":
                    for k, bank in enumerate((3, 0)):
                        act.wait_ge(S["z_ps"], k + 1)
                        A(zs[:, 2 * k:2 * k + 2, :], PS[bank][:, :].rearrange("p (j n) -> p j n", j=2),
                          ACT.Silu).then_inc(S["zs"], 1)
                elif step == "decays":
                    act.wait_ge(S["cum_ps"], 1)
                    A(ec[:, :, :], PS[4][:, 0:NT * 8].rearrange("p (c n) -> p c n", c=NT), ACT.Exp).then_inc(S["ec"], 1)
                elif step == "turn y":
                    act.wait_ge(S["ytr"], 1)
                    for k in range(2):
                        A(yT[:, k, :], PS[1 + k][:, :], ACT.Copy, scale=C["nw"][:, k:k + 1]).then_inc(S["yT"], 1)
                elif step == "turn att":
                    act.wait_ge(S["tr_att"], 1)
                    A(attT[:, :], PS[3][:, :], ACT.Copy).then_inc(S["attT"], 1)
                elif step == "norm 3":
                    act.wait_ge(S["tr_un3"], 1)
                    A(h3[:, :], PS[0][:, :], ACT.Copy, scale=C["r2w"]).then_inc(S["h3"], 1)
                elif step == "top two":
                    act.wait_ge(S["topf"], 1)
                    A(tw[:, 1, :], tw[:, 0, :], ACT.Exp).then_inc(S["tope"], 1)

            def run(it, a, b):
                for part, n in steps(a, b):
                    if part == "a":
                        stage_a(n, b)
                    elif part == "in":
                        project(n)
                    elif part == "conv":
                        conv(n)
                    elif part == "seg":
                        segment(n)
                    elif part == "xtok":
                        turn_xb(n)
                    elif part == "mlp up":
                        mlp_up(n)
                    elif part == "score":
                        exps(n)
                    elif part == "outputs":
                        outputs(n)
                    elif part == "tables":
                        tables()
                    elif part == "b":
                        stage_b(n)
                    elif part == "gate":
                        gate(n)
                    elif part == "ffn up":
                        ffn_up(n)
                    elif part == "turn max":
                        first_part(n)
                pass_ends(act, "act")

            passes(act, run)

        @block.vector
        def _(dve):
            V = nc.vector
            V.memset(ones[:, :], 1.0).then_inc(s_set["prep"], 1)
            V.memset(xbc[:, :, 0:TAPS - 1], 0.0)
            V.memset(vext[:, :, :, DH:DH + 1], 1.0)
            V.memset(PS[3][:, :], 0.0)
            V.memset(state[:, 0, :], 0.0).then_inc(s_set["prep"], 1)
            V.memset(kx[32:64, :, :], 1.0).then_inc(s_set["prep"], 1)
            V.memset(kx[96:128, :, :], 1.0).then_inc(s_set["prep"], 1)
            dve.wait_ge(s_a, 16)
            dve.wait_ge(s_set["exps"], 1)
            V.tensor_scalar(negA[:, :], negA[:, :], -1.0, None, ALU.mult).then_inc(s_set["prep"], 1)
            dve.wait_ge(s_set["prep"], 5)

            def tables():
                dve.wait_ge(s_load, 48)
                dve.wait_ge(s_set["exps"], 2)
                V.tensor_scalar(mtmp[:, 1:2], mtmp[:, 0:1], 1.0, None, ALU.add).then_inc(s_set["sig"], 1)
                dve.wait_ge(s_set["sig"], 1)
                V.reciprocal(mtmp[:, 2:3], mtmp[:, 1:2]).then_inc(s_set["sig"], 1)
                dve.wait_ge(s_set["scal"], 1)
                V.tensor_scalar(msc[:, :], C["blk"], mtmp[:, 3:4], None, ALU.mult)
                dve.wait_ge(s_set["bias_ps"], 1)
                V.tensor_tensor(bias1[:, :], PS[5][:, 0:E * 4], C["fb1"], ALU.add)
                for e in range(E):
                    w = C["fw1T"][:, e * I1:(e + 1) * I1]
                    V.tensor_scalar(w, w, C["lng"][:, e:e + 1], None, ALU.mult)

            links = [0]

            def link(ins):
                ins.then_inc(S["dve_chain"], 1)
                links[0] += 1
                dve.wait_ge(S["dve_chain"], links[0])

            def stats(src, n):
                for j in range(NT):
                    V.bn_stats(bst[:, j, :], src(j)).then_inc(S["bn"], 1)
                for j in range(NT):
                    dve.wait_ge(S["bn"], n * NT + j + 1)
                    V.bn_aggr(mv[:, j, :], bst[:, j, :]).then_inc(S["mv"], 1)

            bc = lambda t, n=NT: t.rearrange("p (a h) -> p a h", a=1).broadcast_to([P, n, t.shape[1]])
            t4 = lambda k: dts[:, k, :].rearrange("p (j h) -> p j h", j=NT)
            wide = lambda t: t.rearrange("p (j a) -> p j a", a=1).broadcast_to([P, NT, E])
            io = bc(C["iota"], NT)

            def best(n):
                for j in range(NT):
                    V.max(top[:, j, :], lg[:, j, :]).then_inc(S["top"], 1)
                for j in range(NT):
                    dve.wait_ge(S["top"], n * NT + j + 1)
                    V.max_index(topi[:, j, :], top[:, j, :], lg[:, j, :]).then_inc(S["topi"], 1)
                dve.wait_ge(S["topi"], (n + 1) * NT)
                link(V.tensor_copy(topf[:, :, :], topi[:, :, :]))

            def up(u):
                dve.wait_ge(S["sa"], u + 1)
                dve.wait_ge(S["eb_ps"], u + 1)
                if u >= 4:
                    dve.wait_ge(S["ed_ps"], u // 2 - 1)
                V.tensor_tensor(hid[:, u % 4, :], sa[:, u % 2, :], PS[6][:, :], ALU.mult).then_inc(S["hid"], 1)

            def expert_sum(n):
                if n % 2 == 0:
                    return
                e = n // 2
                dve.wait_ge(S["ed_ps"], e + 1)
                for j in range(NT):
                    if e:
                        dve.wait_ge(S["eacc"], 4 * (e - 1) + j + 1)
                    V.scalar_tensor_tensor(hb[:, j, :], PS[7][:, j * D:(j + 1) * D], we[:, j, e:e + 1], hb[:, j, :],
                                           ALU.mult, ALU.add).then_inc(S["eacc"], 1)

            def ffn_sum(n):
                e, j = divmod(n, NT)
                if j < NT - 1:
                    return
                dve.wait_ge(S["fd_ps"], e + 1)
                for j in range(NT):
                    dve.wait_ge(S["facc"], 1 if e == 0 else 4 * (e - 1) + j + 2)
                    V.scalar_tensor_tensor(fa[:, j, :], PS[7][:, j * D:(j + 1) * D], wf[:, j, e:e + 1], fa[:, j, :],
                                           ALU.mult, ALU.add).then_inc(S["facc"], 1)

            def stage_b(step):
                if step == "residual":
                    dve.wait_ge(S["g0"], 1)
                    link(V.tensor_tensor(x2[:, :, :], s0[:, :, :], g0[:, :, :], ALU.mult))
                    dve.wait_ge(S["xr_in"], 16)
                    V.tensor_tensor(x2[:, :, :], x2[:, :, :], xres[:, :, :], ALU.add).then_inc(S["x2"], 1)
                    dve.wait_ge(S["x2"], 1)
                    for j in range(NT):
                        V.bn_stats(bstB[:, j, :], x2[:, j, :]).then_inc(S["bnB"], 1)
                    for j in range(NT):
                        dve.wait_ge(S["bnB"], j + 1)
                        V.bn_aggr(mvB[:, j, :], bstB[:, j, :]).then_inc(S["mvB"], 1)
                elif step == "norms":
                    dve.wait_ge(S["rr4"], 1)
                    dve.wait_ge(y_out, 16)
                    for j in range(NT):
                        V.tensor_scalar(xn1[:, j, :], x2[:, j, :], mvB[:, j, 0:1], smB[:, 1, j:j + 1], ALU.subtract,
                                        ALU.mult).then_inc(S["xn1"], 1)
                    for j in range(NT):
                        V.tensor_scalar(un4[:, j, :], x2[:, j, :], mvB[:, j, 0:1], smB[:, 3, j:j + 1], ALU.subtract,
                                        ALU.mult).then_inc(S["un4"], 1)
                elif step == "turn norms":
                    dve.wait_ge(S["tr_un4"], 1)
                    V.tensor_copy(un4T[:, :], PS[6][:, :]).then_inc(S["un4T"], 1)
                elif step == "q, k, v":
                    for j in range(NT):
                        dve.wait_ge(S["qkv_ps"], j + 1)
                        V.tensor_tensor(qkv[:, j, :], PS[(7, 5, 6, 7)[j]][:, 0:3 * D], C["bqkv"], ALU.add
                                        ).then_inc(S["qkv"], 1)
                    dve.wait_ge(S["af_ps"], 1)
                    V.tensor_copy(lg[:, :, :], tk(PS[5][:, 0:NT * E])).then_inc(S["af"], 1)
                    dve.wait_ge(S["af"], 1)
                    best(0)
                    V.tensor_copy(tw[:, 0, :], top[:, :, 0]).then_inc(S["tpf1"], 1)
                    link(V.tensor_tensor(oh[:, 0, :, :], io, wide(topf[:, :, 0]), ALU.is_equal))
                elif step == "lengths":
                    dve.wait_ge(S["sq"], 1)
                    V.tensor_reduce(inv[:, 0, :].rearrange("p (j h) -> p j h", j=NT),
                                    sq[:, :, :].rearrange("p j (h d) -> p j h d", d=DH), AX.X, ALU.add
                                    ).then_inc(S["nrm"], 1)
                    dve.wait_ge(S["nrm"], 1)
                    V.tensor_scalar(inv[:, 0, :], inv[:, 0, :], 1e-24, None, ALU.max).then_inc(S["nrm"], 1)
                    dve.wait_ge(S["tpe1"], 1)
                    link(V.tensor_scalar(tw[:, 2, :], tw[:, 1, :], 1.0, None, ALU.add))
                    link(V.reciprocal(tw[:, 3, :], tw[:, 2, :]))
                    V.tensor_tensor(wf[:, :, :], oh[:, 0, :, :], wide(tw[:, 3, :]), ALU.mult).then_inc(S["ohs"], 1)
                elif step == "inverse lengths":
                    dve.wait_ge(S["rt"], 1)
                    link(V.reciprocal(inv[:, 2, :], inv[:, 1, :]))
                    link(V.tensor_tensor(inv[:, 3, :], inv[:, 0, :], inv[:, 2, :], ALU.mult))
                    link(V.tensor_tensor(inv[:, 3, :], inv[:, 3, :], inv[:, 2, :], ALU.mult))
                    link(V.tensor_scalar(inv[:, 3, :], inv[:, 3, :], -0.5, 1.5, ALU.mult, ALU.add))
                    V.tensor_tensor(inv[:, 2, :], inv[:, 3, :], inv[:, 2, :], ALU.mult).then_inc(S["inv"], 1)
                elif step == "v.k":
                    dve.wait_ge(S["vk_ps"], 1)
                    V.tensor_tensor(vkm[:, :], PS[6][:, 0:P], msc[:, :], ALU.mult).then_inc(S["vkm"], 1)
                elif step == "attention out":
                    dve.wait_ge(S["o1_ps"], 1)
                    V.tensor_tensor(s1[:, :, :], tk(PS[7][:, :]), bc(C["bo1"], NT), ALU.add).then_inc(S["s1"], 1)
                    dve.wait_ge(S["b2_ps"], 1)
                    V.tensor_tensor(fa[:, :, :], tk(PS[5][:, :]), xn1[:, :, :], ALU.add).then_inc(S["facc"], 1)
                elif step == "output":
                    dve.wait_ge(S["g1"], 1)
                    link(V.tensor_tensor(s1[:, :, :], s1[:, :, :], g0[:, :, :], ALU.mult))
                    V.tensor_tensor(ob[:, :, :], s1[:, :, :], x2[:, :, :], ALU.add).then_inc(S["out"], 1)

            def maximum(n):
                h, j = divmod(n, NT)
                dve.wait_ge(S["mx_ps"], n + 1)
                V.tensor_reduce(mx[:, h, j:j + 1], PS[4][:, :], AX.X, ALU.max).then_inc(S["mx"], 1)

            def remainder(g):
                dve.wait_ge(S["m1"], g + 1)
                if g:
                    dve.wait_ge(S["m3"], g)
                V.scalar_tensor_tensor(mrem[:, :], PS[4][0:GH * NT, 0:P], -1.0, mpart[:, 0, :], ALU.mult,
                                       ALU.subtract).then_inc(S["mr"], 1)

            def normalise(g):
                dve.wait_ge(S["tr_o"], g + 1)
                o = PS[4][:, :].rearrange("p (j h d) -> p j h d", j=NT, h=GH)
                link(V.reciprocal(orec[:, :, :], o[:, :, :, DH]))
                w = orec[:, :, :].rearrange("p j (h a) -> p j h a", a=1).broadcast_to([P, NT, GH, DH])
                V.tensor_tensor(att[:, :, GH * DH * g:GH * DH * (g + 1)].rearrange("p j (h d) -> p j h d", h=GH),
                                o[:, :, :, 0:DH], w, ALU.mult).then_inc(S["att"], 1)

            def decayed(c):
                dve.wait_ge(S["lex"], c + 1)
                V.tensor_tensor(av[:, c, :, :], lex[:, c, :, :], bc(gm[:, c, :], HM), ALU.mult
                                ).then_inc(S["wmat"], 1)

            def grow(c):
                dve.wait_ge(S["state"], c + 1)
                tot = ec[0:NS, c, HM:2 * HM].rearrange("p (h a) -> p h a", a=1).broadcast_to([NS, HM, PM])
                link(V.tensor_tensor(hm(stmp[:, :]), hm(state[:, c, :]), tot, ALU.mult))
                dve.wait_ge(S["st_ps"], c + 1)
                V.tensor_tensor(state[:, c + 1, :], stmp[:, :], PS[ST_BANK[c]][0:NS, 0:DI], ALU.add
                                ).then_inc(S["state"], 1)

            def outcome(c):
                bank = PS[Y_BANK[c]]
                dve.wait_ge(S["y_ps"], c + 1)
                cum = ec[:, c, 0:HM].rearrange("p (h a) -> p h a", a=1).broadcast_to([P, HM, PM])
                link(V.tensor_tensor(hm(yg[:, c, :]), hm(bank[:, DI:2 * DI]), cum, ALU.mult))
                V.tensor_tensor(yg[:, c, :], yg[:, c, :], bank[:, 0:DI], ALU.add).then_inc(S["yj"], 1)

            def conv(c):
                w = C["cw"][:, c * TAPS:(c + 1) * TAPS]
                y = xc[:, c, :]
                dve.wait_ge(S["xbc"], c + 1)
                link(V.tensor_scalar(y, xbc[:, c, 0:T], w[:, 0:1], C["cb"][:, c:c + 1], ALU.mult, ALU.add))
                for k in range(1, TAPS - 1):
                    link(V.scalar_tensor_tensor(y, xbc[:, c, k:k + T], w[:, k:k + 1], y, ALU.mult, ALU.add))
                V.scalar_tensor_tensor(y, xbc[:, c, TAPS - 1:], w[:, TAPS - 1:TAPS], y, ALU.mult, ALU.add
                                       ).then_inc(S["conv"], 1)

            def stage_a(step, b):
                if step == "stats":
                    dve.wait_ge(S["x_in"], 16)
                    stats(lambda j: xin[:, j, :], 0)
                elif step == "norm":
                    dve.wait_ge(S["rr"], 1)
                    for j in range(NT):
                        V.tensor_scalar(un[:, j, :], xin[:, j, :], mv[:, j, 0:1], sm[:, 3, j:j + 1], ALU.subtract,
                                        ALU.mult).then_inc(S["un"], 1)
                    for j in range(NT):
                        V.tensor_scalar(xn[:, j, :], xin[:, j, :], mv[:, j, 0:1], sm[:, 1, j:j + 1], ALU.subtract,
                                        ALU.mult).then_inc(S["xn"], 1)
                    dve.wait_ge(S["tr_un"], 1)
                    V.tensor_scalar(hA[:, :], PS[0][:, :], C["ln1w"], C["ln1b"], ALU.mult, ALU.add
                                    ).then_inc(S["hA"], 1)
                elif step == "dt, q, k, v":
                    dve.wait_ge(S["dt_ps"], 1)
                    V.tensor_tensor(t4(0), PS[4][:, 0:NT * HM].rearrange("p (j h) -> p j h", j=NT), bc(C["dtb"]),
                                    ALU.add).then_inc(S["dtraw"], 1)
                    dve.wait_ge(S["dtraw"], 1)
                    V.scalar_tensor_tensor(dts[:, 1, :], dts[:, 0, :], -1.0, dts[:, 0, :], ALU.mult, ALU.max
                                           ).then_inc(S["dtabs"], 1)
                    for k in range(2):
                        dve.wait_ge(S["q1"], k + 1)
                        V.tensor_tensor(rem[:, k, :], PS[1 + k][:, :], part[:, k, 0, :], ALU.subtract
                                        ).then_inc(S["r1"], 1)
                elif step == "softplus":
                    dve.wait_ge(S["dtu"], 1)
                    link(V.tensor_scalar(dts[:, 3, :], dts[:, 2, :], 2.0, None, ALU.add))
                    link(V.reciprocal(dts[:, 4, :], dts[:, 3, :]))
                    link(V.tensor_tensor(dts[:, 3, :], dts[:, 2, :], dts[:, 4, :], ALU.mult))
                    link(V.tensor_tensor(dts[:, 4, :], dts[:, 3, :], dts[:, 3, :], ALU.mult))
                    link(V.tensor_scalar(dts[:, 5, :], dts[:, 4, :], 1.0 / 15, None, ALU.mult))
                    for k in (13, 11, 9, 7, 5, 3):
                        link(V.scalar_tensor_tensor(dts[:, 5, :], dts[:, 5, :], 1.0 / k, dts[:, 4, :], ALU.add,
                                                    ALU.mult))
                    link(V.tensor_scalar(dts[:, 5, :], dts[:, 5, :], 1.0, 2.0, ALU.add, ALU.mult))
                    link(V.tensor_tensor(dts[:, 5, :], dts[:, 5, :], dts[:, 3, :], ALU.mult))
                    V.scalar_tensor_tensor(dts[:, 7, :], dts[:, 0, :], 0.0, dts[:, 5, :], ALU.max, ALU.add
                                           ).then_inc(S["dt"], 1)
                    dve.wait_ge(S["dt"], 1)
                    V.tensor_tensor(t4(6), t4(7), bc(negA[:, :]), ALU.mult).then_inc(S["adec"], 1)
                    dve.wait_ge(S["adec"], 1)
                    for c in range(NT):
                        w = dts[:, 6, c * HM:(c + 1) * HM].rearrange("p (h a) -> p h a", a=1).broadcast_to([P, HM, P])
                        V.tensor_tensor(av[:, c, :, :], bc(C["le"], HM), w, ALU.mult).then_inc(S["av"], 1)
                elif step == "B.C":
                    dve.wait_ge(S["g_ps"], 1)
                    V.tensor_tensor(gm[:, :, :], tk(PS[3][:, :]), bc(C["le"], NT), ALU.mult).then_inc(S["gm"], 1)
                    dve.wait_ge(S["gm"], 1)
                elif step == "first state":
                    V.memset(state[:, 0, :], 0.0).then_inc(S["state"], 1)
                    dve.wait_ge(S["ec"], 1)
                elif step == "scan":
                    dve.wait_ge(S["q3"], 2)
                elif step == "turn y":
                    dve.wait_ge(S["yg"], 4)
                    stats(lambda j: yg[:, j, :], 1)
                elif step == "mamba out":
                    dve.wait_ge(S["op_ps"], 1)
                    dve.wait_ge(S["yr"], 1)
                    for j in range(NT):
                        V.scalar_tensor_tensor(x1[:, j, :], PS[3][:, j * D:(j + 1) * D], sm[:, 1, j:j + 1],
                                               xn[:, j, :], ALU.mult, ALU.add).then_inc(S["x1"], 1)
                    dve.wait_ge(S["x1"], 4)
                    stats(lambda j: x1[:, j, :], 2)
                elif step == "norm 2":
                    dve.wait_ge(S["rr2"], 1)
                    for j in range(NT):
                        V.tensor_scalar(un[:, j, :], x1[:, j, :], mv[:, j, 0:1], sm[:, 1, j:j + 1], ALU.subtract,
                                        ALU.mult).then_inc(S["un2"], 1)
                    dve.wait_ge(S["tr_un2"], 1)
                    V.tensor_scalar(h2[:, :], PS[1][:, :], C["ln2w"], C["ln2b"], ALU.mult, ALU.add
                                    ).then_inc(S["h2"], 1)
                elif step == "mlp down":
                    dve.wait_ge(S["down_ps"], 1)
                    dve.wait_ge(S["res2"], 1)
                    V.tensor_tensor(x1[:, :, :], tk(PS[0][:, :]), x1[:, :, :], ALU.add).then_inc(S["s0"], 1)
                elif step == "attention out":
                    dve.wait_ge(S["wo_ps"], 1)
                    V.tensor_tensor(hb[:, :, :], tk(PS[4][:, :]), xn[:, :, :], ALU.add).then_inc(S["hb"], 1)
                    dve.wait_ge(S["hb"], 1)
                    stats(lambda j: hb[:, j, :], 3)
                elif step == "norm 3":
                    dve.wait_ge(S["rr3"], 1)
                    for j in range(NT):
                        V.tensor_scalar(un[:, j, :], hb[:, j, :], sm[:, 1, j:j + 1], None, ALU.mult
                                        ).then_inc(S["un3"], 1)
                elif step == "top two":
                    dve.wait_ge(S["lg_ps"], 1)
                    V.tensor_copy(lg[:, :, :], tk(PS[1][:, 0:NT * E])).then_inc(S["lg"], 1)
                    dve.wait_ge(S["lg"], 1)
                    best(1 if b else 0)
                    V.tensor_tensor(tw[:, 0, :], top[:, :, 1], top[:, :, 0], ALU.subtract).then_inc(S["topf"], 1)
                    link(V.tensor_tensor(oh[:, 0, :, :], io, wide(topf[:, :, 0]), ALU.is_equal))
                    link(V.tensor_tensor(oh[:, 1, :, :], io, wide(topf[:, :, 1]), ALU.is_equal))
                    dve.wait_ge(S["tope"], 1)
                    link(V.tensor_scalar(tw[:, 2, :], tw[:, 1, :], 1.0, None, ALU.add))
                    link(V.reciprocal(tw[:, 3, :], tw[:, 2, :]))
                    link(V.tensor_tensor(tw[:, 4, :], tw[:, 3, :], tw[:, 1, :], ALU.mult))
                    link(V.tensor_tensor(oh[:, 0, :, :], oh[:, 0, :, :], wide(tw[:, 3, :]), ALU.mult))
                    link(V.tensor_tensor(oh[:, 1, :, :], oh[:, 1, :, :], wide(tw[:, 4, :]), ALU.mult))
                    V.tensor_tensor(we[:, :, :], oh[:, 0, :, :], oh[:, 1, :, :], ALU.add).then_inc(S["we"], 1)

            def run(it, a, b):
                links[0] = 0
                for part, n in steps(a, b):
                    if part == "a":
                        stage_a(n, b)
                    elif part == "conv":
                        conv(n)
                    elif part == "xtok":
                        decayed(n)
                    elif part == "grow":
                        grow(n)
                    elif part == "y":
                        outcome(n)
                    elif part == "turn out":
                        normalise(n)
                    elif part == "tables":
                        tables()
                    elif part == "b":
                        stage_b(n)
                    elif part == "up":
                        up(n)
                    elif part == "down":
                        expert_sum(n)
                    elif part == "ffn down":
                        ffn_sum(n)
                    elif part == "max":
                        maximum(n)
                    elif part == "turn max":
                        remainder(n)
                pass_ends(dve, "dve")

            passes(dve, run)

        @block.gpsimd
        def _(pool):
            G = nc.gpsimd
            pool.wait_ge(s_a, 16)
            links = [0]

            def link(ins):
                ins.then_inc(S["pool_chain"], 1)
                links[0] += 1
                pool.wait_ge(S["pool_chain"], links[0])

            def rsqrt(small, k, src, signal=None):
                link(G.tensor_scalar(small[:, k, :], src, EPS, None, ALU.add))
                ins = G.tensor_tensor(small[:, k, :], small[:, k, :], C["mhalf"], ALU.pow)
                ins.then_inc(signal, 1) if signal else link(ins)

            def twice_normed(small, mvs, signal):
                rsqrt(small, 1, mvs[:, :, 1])
                link(G.tensor_tensor(small[:, 2, :], small[:, 1, :], mvs[:, :, 1], ALU.mult))
                link(G.tensor_tensor(small[:, 2, :], small[:, 2, :], small[:, 1, :], ALU.mult))
                rsqrt(small, 2, small[:, 2, :])
                G.tensor_tensor(small[:, 3, :], small[:, 1, :], small[:, 2, :], ALU.mult).then_inc(signal, 1)

            def mean_square():
                link(G.tensor_tensor(sm[:, 0, :], mv[:, :, 0], mv[:, :, 0], ALU.mult))
                link(G.tensor_tensor(sm[:, 0, :], sm[:, 0, :], mv[:, :, 1], ALU.add))

            bc = lambda t, n=PM: t.rearrange("p (h a) -> p h a", a=1).broadcast_to([P, HM, n])

            def max_parts(g):
                pool.wait_ge(S["mr"], g + 1)
                if g:
                    pool.wait_ge(S["m_store"], 16 * g)
                link(G.tensor_copy(mpart[:, 1, :], mrem[:, :]))
                G.tensor_tensor(mpart[:, 2, :], mrem[:, :], mpart[:, 1, :], ALU.subtract).then_inc(S["m3"], 1)

            def stage_b(step):
                if step == "residual":
                    pool.wait_ge(S["mvB"], 4)
                    twice_normed(smB, mvB, S["rr4"])
                elif step == "q, k, v":
                    pool.wait_ge(S["qkv"], 4)
                    G.tensor_tensor(sq[:, :, :], qkv[:, :, 0:2 * D], qkv[:, :, 0:2 * D], ALU.mult).then_inc(S["sq"], 1)
                elif step == "inverse lengths":
                    pool.wait_ge(S["inv"], 1)
                    for k in range(2):
                        t = qkv[:, :, k * D:(k + 1) * D].rearrange("p j (h d) -> p j h d", d=DH)
                        w = inv[:, 2, :].rearrange("p (j h a) -> p j h a", j=NT, a=1)[:, :, k * HA:(k + 1) * HA, :]
                        G.tensor_tensor(t, t, w.broadcast_to([P, NT, HA, DH]), ALU.mult).then_inc(S["qkn"], 1)

            def weigh(c):
                xt = hm(xtok[:, c, 0:DI])
                pool.wait_ge(S["xtok"], c + 1)
                G.tensor_tensor(hm(xdt[:, c, :]), xt, bc(dts[:, 7, c * HM:(c + 1) * HM]), ALU.mult
                                ).then_inc(S["xdt"], 1)
                pool.wait_ge(S["xdt"], c + 1)
                pool.wait_ge(S["lex"], c + 1)
                G.tensor_tensor(hm(xw[:, c, :]), hm(xdt[:, c, :]), bc(lex[:, c, :, P - 1]), ALU.mult
                                ).then_inc(S["xw"], 1)
                link(G.tensor_tensor(xt, xt, bc(C["dskip"]), ALU.mult))

            def outcome(c):
                if c == 0:
                    pool.wait_ge(S["zs"], 2)
                pool.wait_ge(S["yj"], c + 1)
                link(G.tensor_tensor(yg[:, c, :], yg[:, c, :], xtok[:, c, 0:DI], ALU.add))
                G.tensor_tensor(yg[:, c, :], yg[:, c, :], zs[:, c, :], ALU.mult).then_inc(S["yg"], 1)

            def stage_a(step, b):
                if step == "stats":
                    for k, row in enumerate((32, 96)):
                        G.memset(qx[row:row + 32, :, :].bitcast(U32), 0).then_inc(S["qz"], 1)
                        pool.wait_ge(S["qz"], k + 1)
                    pool.wait_ge(S["mv"], 4)
                    twice_normed(sm, mv, S["rr"])
                elif step == "dt, q, k, v":
                    for k in range(2):
                        pool.wait_ge(S["q2"], k + 1)
                        G.tensor_tensor(part[:, k, 2, :], rem[:, k, :], part[:, k, 1, :], ALU.subtract
                                        ).then_inc(S["q3"], 1)
                elif step == "turn y":
                    pool.wait_ge(S["mv"], 8)
                    mean_square()
                    rsqrt(sm, 1, sm[:, 0, :], S["yr"])
                elif step == "mamba out":
                    pool.wait_ge(S["mv"], 12)
                    pool.wait_ge(S["x1"], 4)
                    rsqrt(sm, 1, mv[:, :, 1], S["rr2"])
                elif step == "bias 2":
                    pool.wait_ge(S["un2"], 4)
                    G.tensor_tensor(x1[:, :, :], x1[:, :, :],
                                    C["mb2"].rearrange("p (a n) -> p a n", a=1).broadcast_to([P, NT, D]), ALU.add
                                    ).then_inc(S["res2"], 1)
                elif step == "attention out":
                    pool.wait_ge(S["mv"], 16)
                    mean_square()
                    rsqrt(sm, 1, sm[:, 0, :], S["rr3"])
                elif step == "top two":
                    if b:
                        pool.wait_ge(S["x2"], 1)
                    pool.wait_ge(S["s0"], 1)
                    G.tensor_copy(s0[:, :, :], x1[:, :, :])

            def run(it, a, b):
                links[0] = 0
                for part, n in steps(a, b):
                    if part == "a":
                        stage_a(n, b)
                    elif part == "xtok":
                        weigh(n)
                    elif part == "y":
                        outcome(n)
                    elif part == "b":
                        stage_b(n)
                    elif part == "turn max":
                        max_parts(n)
                pass_ends(pool, "pool")

            passes(pool, run)



def _tables(i):
    T_ = np.transpose
    row = lambda a: np.broadcast_to(a.reshape(1, -1), (P, a.size))
    col = lambda a: a.reshape(-1, P).T
    r = np.arange(P)
    f = np.float32
    head = r // DH
    heads = lambda w: T_(w.reshape(HA // 2, 2, DH, D), (3, 1, 2, 0)).reshape(D, P)
    up = lambda w: T_(w, (2, 0, 1)).reshape(P, -1)
    down = lambda w: T_(w.reshape(E, D, -1, P), (3, 0, 2, 1)).reshape(P, -1)
    a = dict(
        ident=np.eye(P, dtype=f), le=(r[:, None] <= r[None, :]).astype(f), gt=(r[:, None] > r[None, :]).astype(f),
        blk=(head[:, None] == head[None, :]).astype(f), iota=row(np.arange(E, dtype=f)),
        mhalf=np.full((P, NT), -0.5, f), ln1w=col(i["L0_attn_ln1_w"]), ln1b=col(i["L0_attn_ln1_b"]),
        winT=i["L0_attn_in_proj_w"].T, cw=T_(i["L0_attn_conv_w"].reshape(3, P, TAPS), (1, 0, 2)).reshape(P, 3 * TAPS),
        cb=col(i["L0_attn_conv_b"]),
        dtb=row(i["L0_attn_dt_bias"]), alog=row(i["L0_attn_A_log"]), dskip=row(i["L0_attn_D"]),
        nw=col(i["L0_attn_norm_w"]), woutT=T_(i["L0_attn_out_proj_w"].reshape(D, 2, P), (2, 1, 0)).reshape(P, -1),
        ln2w=col(i["L0_attn_ln2_w"]), ln2b=col(i["L0_attn_ln2_b"]), mw1T=i["L0_attn_mlp_w1"].T,
        mb1=col(i["L0_attn_mlp_b1"]), mw2T=T_(i["L0_attn_mlp_w2"].reshape(D, 4, P), (2, 1, 0)).reshape(P, -1),
        mb2=row(i["L0_attn_mlp_b2"]), r1w=col(i["L0_ffn_ln1_w"]), r2w=col(i["L0_ffn_ln2_w"]),
        wqT=heads(i["L0_ffn_wq"]), wkT=heads(i["L0_ffn_wk"]), wvT=i["L0_ffn_wv"].T, woT=i["L0_ffn_wo"].T,
        gateT=i["L0_ffn_gate_w"].T)
    b = dict(ew1T=up(i["L0_ffn_w1"]), ew3T=up(i["L0_ffn_w3"]), ew2T=down(i["L0_ffn_w2"]))
    c = dict(
        wqkv=np.concatenate([i["L1_attn_Wq"], i["L1_attn_Wk"], i["L1_attn_Wv"]], axis=1),
        bqkv=row(np.concatenate([i["L1_attn_bq"], i["L1_attn_bk"], i["L1_attn_bv"]])), wo1=i["L1_attn_Wo"],
        bo1=row(i["L1_attn_bo"]), mcol=np.repeat(i["L1_attn_m"], DH).reshape(P, 1), centT=i["L1_ffn_centroids"].T,
        lng=i["L1_ffn_ln_g"].T, lnb=i["L1_ffn_ln_b"].T, fb1=T_(i["L1_ffn_b1"].reshape(E * 4, P), (1, 0)),
        fw1T=up(i["L1_ffn_w1"]), fw2T=down(i["L1_ffn_w2"]))
    return [np.ascontiguousarray(np.concatenate([t[k] for k in pack], axis=1))
            for t, pack in ((a, PACK_A), (b, PACK_B), (c, PACK_C))]


def kernel(**inputs):
    import concourse.bacc as bacc
    from concourse.bass_utils import run_bass_kernel_spmd

    i = {k: np.asarray(v) for k, v in inputs.items()}
    pack_a, pack_b, pack_c = _tables(i)
    arrays = {"x": np.ascontiguousarray(i["L0_attn_x"]), "pack_a": pack_a, "pack_b": pack_b, "pack_c": pack_c,
              "b2": np.ascontiguousarray(i["L1_ffn_b2"])}
    nc = bacc.Bacc("TRN2", target_bir_lowering=False, num_devices=1)
    aps = [nc.dram_tensor(k, a.shape, F32, kind="ExternalInput").ap() for k, a in arrays.items()]
    y = nc.dram_tensor("y", (B, T, D), F32, kind="ExternalOutput").ap()
    build(nc, *aps, y)
    r = run_bass_kernel_spmd(nc, [arrays], core_ids=[0])
    return r.results[0]["y"]
```
